# Optimizing a Trainium2 kernel written in Bass

```python
import numpy as np
import jax
import jax.numpy as jnp

def _softmax(x, axis=-1):
    return jax.nn.softmax(x, axis=axis)

def _gelu(x):
    return jax.nn.gelu(x, approximate=True)

def _silu(x):
    return jax.nn.silu(x)

def _sigmoid(x):
    return jax.nn.sigmoid(x)

def _layernorm(x, axis=-1, eps=1e-05):
    m = jnp.mean(x, axis=axis, keepdims=True)
    v = jnp.var(x, axis=axis, keepdims=True)
    return (x - m) / jnp.sqrt(v + eps)

def _scatter_add(tgt, idx, src, axis=0):
    return tgt.at[idx].add(src)

def _segment_sum(src, seg, n):
    return jax.ops.segment_sum(src, seg, n)
kernel_name = 'mk_adaln_d2_jaxref_r8_ca1ffb'

def setup_inputs(seed: int=0):
    np.random.seed(seed)
    _w = jnp.asarray

    def _L0_attn_setup():
        import jax, jax.numpy as jnp
        import numpy as np
        B, S, E = (2, 256, 128)
        H, D = (16, 64)

        def _attention(q, k, v):
            dtype = q.dtype
            logits = jnp.einsum('bqhd,bkhd->bhqk', q.astype(jnp.float32), k.astype(jnp.float32))
            logits = logits / jnp.sqrt(jnp.float32(q.shape[-1]))
            mask = jnp.tril(jnp.ones((q.shape[1], q.shape[1]), dtype=jnp.bool_))
            neg = jnp.asarray(-0.7 * jnp.finfo(logits.dtype).max, dtype=logits.dtype)
            logits = jnp.where(mask, logits, neg)
            probs = jax.nn.softmax(logits, axis=-1).astype(dtype)
            return jnp.einsum('bhqk,bkhd->bqhd', probs, v)
        key = jax.random.key(seed)
        k1, k2, k3 = jax.random.split(key, 3)
        x = jax.random.normal(k1, (B, S, E), dtype=jnp.float32)
        w_qkv = jax.random.normal(k2, (E, H, 3 * D), dtype=jnp.float32) * 0.01
        w_out = jax.random.normal(k3, (H, D, E), dtype=jnp.float32) * 0.01
        return {'x': x, 'w_qkv': w_qkv, 'w_out': w_out}
    _L0_attn_in = _L0_attn_setup()

    def _L0_ffn_setup():
        import jax, jax.numpy as jnp
        import numpy as np
        B, S, D, H, F = (4, 512, 128, 16, 512)
        CAP = 0.125
        ROPE_BASE = 10000.0

        def rmsnorm(x, g):
            return x * jax.lax.rsqrt(jnp.mean(x * x, -1, keepdims=True) + 1e-06) * g

        def rope(t, pos):
            hd = t.shape[-1]
            inv = 1.0 / ROPE_BASE ** (jnp.arange(0, hd, 2, dtype=jnp.float32) / hd)
            f = pos[:, None, :, None].astype(jnp.float32) * inv
            emb = jnp.concatenate([f, f], axis=-1)
            cos, sin = (jnp.cos(emb), jnp.sin(emb))
            rot = jnp.concatenate([-t[..., hd // 2:], t[..., :hd // 2]], axis=-1)
            return t * cos + rot * sin
        key = jax.random.key(seed)
        ks = jax.random.split(key, 9)
        scale = 0.02
        x = jax.random.normal(ks[0], (B, S, D), jnp.float32)
        causal = jnp.where(jnp.tril(jnp.ones((S, S), bool)), 0.0, -1000000000.0).astype(jnp.float32)
        attention_mask = jnp.broadcast_to(causal[None, None], (B, 1, S, S))
        position_ids = jnp.broadcast_to(jnp.arange(S, dtype=jnp.int32), (B, S))
        return {'x': x, 'attention_mask': attention_mask, 'position_ids': position_ids, 'router_w': jax.random.normal(ks[1], (D, 1), jnp.float32) * scale, 'router_b': jnp.zeros((1,), jnp.float32), 'wq': jax.random.normal(ks[2], (D, D), jnp.float32) * scale, 'wk': jax.random.normal(ks[3], (D, D), jnp.float32) * scale, 'wv': jax.random.normal(ks[4], (D, D), jnp.float32) * scale, 'wo': jax.random.normal(ks[5], (D, D), jnp.float32) * scale, 'w1': jax.random.normal(ks[6], (D, F), jnp.float32) * scale, 'w2': jax.random.normal(ks[7], (F, D), jnp.float32) * scale, 'ln1': jnp.ones((D,), jnp.float32), 'ln2': jnp.ones((D,), jnp.float32)}
    _L0_ffn_in = _L0_ffn_setup()
    _L0_c = _w((lambda *s: np.random.randn(*s).astype(np.float32) * 0.05)(4, 128))
    _L0_wmod = _w((lambda *s: np.random.randn(*s).astype(np.float32) * 0.05)(128, 6 * 128) * 128 ** (-0.5))

    def _L1_attn_setup():
        import jax, jax.numpy as jnp
        import numpy as np
        H = 16
        GRID = 16
        TOK_PER_FRAME = GRID * GRID

        def _rope(x, pos, dim):
            half = dim // 2
            omega = jnp.arange(half, dtype=x.dtype) / (dim / 2.0)
            inv = 1.0 / 10000.0 ** omega
            freq = pos.astype(x.dtype)[:, None] * inv
            sin = jnp.concatenate([jnp.sin(freq), jnp.sin(freq)], axis=-1)
            cos = jnp.concatenate([jnp.cos(freq), jnp.cos(freq)], axis=-1)
            y = x.reshape(*x.shape[:-1], half, 2)
            y1, y2 = (y[..., 0], y[..., 1])
            rot = jnp.stack((-y2, y1), axis=-1).reshape(x.shape)
            return x * cos + rot * sin

        def _apply_3d_rope(qk, f_ids, h_ids, w_ids, d_dim):
            s = 0
            parts = []
            for pos in (f_ids, h_ids, w_ids):
                parts.append(_rope(qk[..., s:s + d_dim], pos, d_dim))
                s += d_dim
            if s < qk.shape[-1]:
                parts.append(qk[..., s:])
            return jnp.concatenate(parts, axis=-1)
        key = jax.random.key(seed)
        ks = jax.random.split(key, 5)
        D = 128
        B, N = (4, 256)
        sc = 0.02
        return {'hidden_states': jax.random.normal(ks[0], (B, N, D), jnp.float32), 'Wq': jax.random.normal(ks[1], (D, D), jnp.float32) * sc, 'bq': jnp.zeros((D,), jnp.float32), 'Wk': jax.random.normal(ks[2], (D, D), jnp.float32) * sc, 'bk': jnp.zeros((D,), jnp.float32), 'Wv': jax.random.normal(ks[3], (D, D), jnp.float32) * sc, 'bv': jnp.zeros((D,), jnp.float32), 'Wo': jax.random.normal(ks[4], (D, D), jnp.float32) * sc, 'bo': jnp.zeros((D,), jnp.float32)}
    _L1_attn_in = _L1_attn_setup()

    def _L1_ffn_setup():
        import jax, jax.numpy as jnp
        import numpy as np
        K_TOP = 2
        key = jax.random.key(seed)
        k1, k2, k3 = jax.random.split(key, 3)
        B, S, H, E = (4, 256, 128, 8)
        hidden_states = jax.random.normal(k1, (B, S, H), dtype=jnp.float32)
        router_w = jax.random.normal(k2, (E, H), dtype=jnp.float32) * 0.02
        expert_weights = jax.random.normal(k3, (E, H, H), dtype=jnp.float32) * 0.02
        return {'hidden_states': hidden_states, 'router_w': router_w, 'expert_weights': expert_weights}
    _L1_ffn_in = _L1_ffn_setup()
    _L1_c = _w((lambda *s: np.random.randn(*s).astype(np.float32) * 0.05)(4, 128))
    _L1_wmod = _w((lambda *s: np.random.randn(*s).astype(np.float32) * 0.05)(128, 6 * 128) * 128 ** (-0.5))
    _d = {'L0_attn_x': _L0_attn_in['x'], 'L0_attn_w_qkv': _L0_attn_in['w_qkv'], 'L0_attn_w_out': _L0_attn_in['w_out'], 'L0_ffn_attention_mask': _L0_ffn_in['attention_mask'], 'L0_ffn_position_ids': _L0_ffn_in['position_ids'], 'L0_ffn_router_w': _L0_ffn_in['router_w'], 'L0_ffn_router_b': _L0_ffn_in['router_b'], 'L0_ffn_wq': _L0_ffn_in['wq'], 'L0_ffn_wk': _L0_ffn_in['wk'], 'L0_ffn_wv': _L0_ffn_in['wv'], 'L0_ffn_wo': _L0_ffn_in['wo'], 'L0_ffn_w1': _L0_ffn_in['w1'], 'L0_ffn_w2': _L0_ffn_in['w2'], 'L0_ffn_ln1': _L0_ffn_in['ln1'], 'L0_ffn_ln2': _L0_ffn_in['ln2'], 'L0_c': _L0_c, 'L0_wmod': _L0_wmod, 'L1_attn_Wq': _L1_attn_in['Wq'], 'L1_attn_bq': _L1_attn_in['bq'], 'L1_attn_Wk': _L1_attn_in['Wk'], 'L1_attn_bk': _L1_attn_in['bk'], 'L1_attn_Wv': _L1_attn_in['Wv'], 'L1_attn_bv': _L1_attn_in['bv'], 'L1_attn_Wo': _L1_attn_in['Wo'], 'L1_attn_bo': _L1_attn_in['bo'], 'L1_ffn_router_w': _L1_ffn_in['router_w'], 'L1_ffn_expert_weights': _L1_ffn_in['expert_weights'], 'L1_c': _L1_c, 'L1_wmod': _L1_wmod}
    _x0 = _d['L0_attn_x']
    _d['L0_attn_x'] = jax.random.normal(jax.random.fold_in(jax.random.key(seed), 1), (4, 1024, 128), dtype=_x0.dtype)
    del _x0
    return _d

def reference(L0_attn_x, L0_attn_w_qkv, L0_attn_w_out, L0_ffn_attention_mask, L0_ffn_position_ids, L0_ffn_router_w, L0_ffn_router_b, L0_ffn_wq, L0_ffn_wk, L0_ffn_wv, L0_ffn_wo, L0_ffn_w1, L0_ffn_w2, L0_ffn_ln1, L0_ffn_ln2, L0_c, L0_wmod, L1_attn_Wq, L1_attn_bq, L1_attn_Wk, L1_attn_bk, L1_attn_Wv, L1_attn_bv, L1_attn_Wo, L1_attn_bo, L1_ffn_router_w, L1_ffn_expert_weights, L1_c, L1_wmod):

    def _L0_attn_ref(x, w_qkv, w_out):
        import jax, jax.numpy as jnp
        import numpy as np
        B, S, E = (2, 256, 128)
        H, D = (16, 64)

        def _attention(q, k, v):
            dtype = q.dtype
            logits = jnp.einsum('bqhd,bkhd->bhqk', q.astype(jnp.float32), k.astype(jnp.float32))
            logits = logits / jnp.sqrt(jnp.float32(q.shape[-1]))
            mask = jnp.tril(jnp.ones((q.shape[1], q.shape[1]), dtype=jnp.bool_))
            neg = jnp.asarray(-0.7 * jnp.finfo(logits.dtype).max, dtype=logits.dtype)
            logits = jnp.where(mask, logits, neg)
            probs = jax.nn.softmax(logits, axis=-1).astype(dtype)
            return jnp.einsum('bhqk,bkhd->bqhd', probs, v)
        qkv = jnp.einsum('bse,ehd->bshd', x, w_qkv)
        q, k, v = jnp.split(qkv, 3, axis=-1)
        out = _attention(q, k, v)
        return jnp.einsum('bshd,hde->bse', out, w_out)

    def _L0_ffn_ref(x, attention_mask, position_ids, router_w, router_b, wq, wk, wv, wo, w1, w2, ln1, ln2):
        import jax, jax.numpy as jnp
        import numpy as np
        B, S, D, H, F = (4, 512, 128, 16, 512)
        CAP = 0.125
        ROPE_BASE = 10000.0

        def rmsnorm(x, g):
            return x * jax.lax.rsqrt(jnp.mean(x * x, -1, keepdims=True) + 1e-06) * g

        def rope(t, pos):
            hd = t.shape[-1]
            inv = 1.0 / ROPE_BASE ** (jnp.arange(0, hd, 2, dtype=jnp.float32) / hd)
            f = pos[:, None, :, None].astype(jnp.float32) * inv
            emb = jnp.concatenate([f, f], axis=-1)
            cos, sin = (jnp.cos(emb), jnp.sin(emb))
            rot = jnp.concatenate([-t[..., hd // 2:], t[..., :hd // 2]], axis=-1)
            return t * cos + rot * sin
        b, s, d = x.shape
        hd = d // H
        weights = (x @ router_w)[..., 0] + router_b[0]
        k = int(CAP * s)
        topv, topi = jax.lax.top_k(weights, k)
        thr = topv[:, -1]
        sel_mask = (weights > thr[:, None]).astype(x.dtype)
        kc = k - 1
        sel_idx = jnp.sort(topi[:, :kc], axis=1)
        bidx = jnp.arange(b)[:, None]
        x_sel = x[bidx, sel_idx]
        pos_sel = position_ids[bidx, sel_idx]
        w_sel = weights[bidx, sel_idx]
        m = attention_mask[:, 0]
        m_sel = m[bidx[:, :, None], sel_idx[:, :, None], sel_idx[:, None, :]]
        hn = rmsnorm(x_sel, ln1)

        def heads(t):
            return t.reshape(b, kc, H, hd).transpose(0, 2, 1, 3)
        q = rope(heads(hn @ wq), pos_sel)
        kk = rope(heads(hn @ wk), pos_sel)
        v = heads(hn @ wv)
        sc = jnp.einsum('bhqd,bhkd->bhqk', q, kk) / np.sqrt(hd).astype(np.float32)
        sc = sc + m_sel[:, None]
        a = jax.nn.softmax(sc, axis=-1)
        o = jnp.einsum('bhqk,bhkd->bhqd', a, v).transpose(0, 2, 1, 3).reshape(b, kc, d) @ wo
        x1 = x_sel + o
        x2 = x1 + jax.nn.gelu(rmsnorm(x1, ln2) @ w1) @ w2
        proc = x2 * w_sel[..., None]
        out = jnp.zeros_like(x).at[bidx, sel_idx].set(proc)
        return out + x * (1.0 - sel_mask)[..., None]

    def _L1_attn_ref(hidden_states, Wq, bq, Wk, bk, Wv, bv, Wo, bo):
        import jax, jax.numpy as jnp
        import numpy as np
        H = 16
        GRID = 16
        TOK_PER_FRAME = GRID * GRID

        def _rope(x, pos, dim):
            half = dim // 2
            omega = jnp.arange(half, dtype=x.dtype) / (dim / 2.0)
            inv = 1.0 / 10000.0 ** omega
            freq = pos.astype(x.dtype)[:, None] * inv
            sin = jnp.concatenate([jnp.sin(freq), jnp.sin(freq)], axis=-1)
            cos = jnp.concatenate([jnp.cos(freq), jnp.cos(freq)], axis=-1)
            y = x.reshape(*x.shape[:-1], half, 2)
            y1, y2 = (y[..., 0], y[..., 1])
            rot = jnp.stack((-y2, y1), axis=-1).reshape(x.shape)
            return x * cos + rot * sin

        def _apply_3d_rope(qk, f_ids, h_ids, w_ids, d_dim):
            s = 0
            parts = []
            for pos in (f_ids, h_ids, w_ids):
                parts.append(_rope(qk[..., s:s + d_dim], pos, d_dim))
                s += d_dim
            if s < qk.shape[-1]:
                parts.append(qk[..., s:])
            return jnp.concatenate(parts, axis=-1)
        B, N, D = hidden_states.shape
        hd = D // H
        d_dim = 2 * (hd // 3 // 2)

        def heads(x):
            return x.reshape(B, N, H, hd).transpose(0, 2, 1, 3)
        q = heads(hidden_states @ Wq + bq)
        k = heads(hidden_states @ Wk + bk)
        v = heads(hidden_states @ Wv + bv)
        ids = jnp.arange(N)
        f_ids = ids // TOK_PER_FRAME
        rem = ids - TOK_PER_FRAME * f_ids
        h_ids = rem // GRID
        w_ids = rem - GRID * h_ids
        q = _apply_3d_rope(q, f_ids, h_ids, w_ids, d_dim)
        k = _apply_3d_rope(k, f_ids, h_ids, w_ids, d_dim)
        scale = hd ** (-0.5)
        attn = jnp.einsum('bhqd,bhkd->bhqk', q, k) * scale
        attn = jax.nn.softmax(attn.astype(jnp.float32), axis=-1).astype(q.dtype)
        ctx = jnp.einsum('bhqk,bhkd->bhqd', attn, v)
        ctx = ctx.transpose(0, 2, 1, 3).reshape(B, N, D)
        return ctx @ Wo + bo

    def _L1_ffn_ref(hidden_states, router_w, expert_weights):
        import jax, jax.numpy as jnp
        import numpy as np
        K_TOP = 2
        B, S, H = hidden_states.shape
        x = hidden_states.reshape(-1, H)
        logits = x @ router_w.T
        probs = jax.nn.softmax(logits, axis=-1)
        topk_vals, topk_idx = jax.lax.top_k(probs, K_TOP)
        topk_w = topk_vals / (topk_vals.sum(-1, keepdims=True) + 1e-06)
        expert_out = jnp.einsum('nh,eho->eno', x, expert_weights)
        combined = jnp.take_along_axis(expert_out.transpose(1, 0, 2), topk_idx[:, :, None], axis=1)
        combined = combined.transpose(1, 0, 2)
        remap_bias = jnp.take_along_axis(probs, topk_idx, axis=1).T[:, :, None]
        weights = topk_w.T[:, :, None]
        out = ((combined + remap_bias) * weights).sum(axis=0)
        return out.reshape(B, S, H)
    x = L0_attn_x
    mod = (_silu(L0_c) @ L0_wmod).reshape(L0_c.shape[0], 6, 1, -1)
    sa, ca, ga, sb, cb, gb = (mod[:, 0], mod[:, 1], mod[:, 2], mod[:, 3], mod[:, 4], mod[:, 5])
    ga = (2 * (ga >= 0) - 1) * jnp.maximum(jnp.abs(ga), 0.25)
    gb = (2 * (gb >= 0) - 1) * jnp.maximum(jnp.abs(gb), 0.25)
    h = _layernorm(x, axis=-1) * (1 + ca) + sa
    x = x + ga * _L0_attn_ref(h, L0_attn_w_qkv, L0_attn_w_out)
    h = _layernorm(x, axis=-1) * (1 + cb) + sb
    x = x + gb * _L0_ffn_ref(h, L0_ffn_attention_mask, L0_ffn_position_ids, L0_ffn_router_w, L0_ffn_router_b, L0_ffn_wq, L0_ffn_wk, L0_ffn_wv, L0_ffn_wo, L0_ffn_w1, L0_ffn_w2, L0_ffn_ln1, L0_ffn_ln2)
    mod = (_silu(L1_c) @ L1_wmod).reshape(L1_c.shape[0], 6, 1, -1)
    sa, ca, ga, sb, cb, gb = (mod[:, 0], mod[:, 1], mod[:, 2], mod[:, 3], mod[:, 4], mod[:, 5])
    ga = (2 * (ga >= 0) - 1) * jnp.maximum(jnp.abs(ga), 0.25)
    gb = (2 * (gb >= 0) - 1) * jnp.maximum(jnp.abs(gb), 0.25)
    h = _layernorm(x, axis=-1) * (1 + ca) + sa
    x = x + ga * _L1_attn_ref(h, L1_attn_Wq, L1_attn_bq, L1_attn_Wk, L1_attn_bk, L1_attn_Wv, L1_attn_bv, L1_attn_Wo, L1_attn_bo)
    h = _layernorm(x, axis=-1) * (1 + cb) + sb
    x = x + gb * _L1_ffn_ref(h, L1_ffn_router_w, L1_ffn_expert_weights)
    return x

_drawn_inputs = setup_inputs


def setup_inputs(seed=0):
    import zlib

    import numpy as np

    out = dict(_drawn_inputs(seed))
    spreads = {'L0_ffn_ln1': (1.0, 0.6),
     'L0_ffn_ln2': (1.0, 0.6),
     'L1_attn_bq': (0.0, 0.8),
     'L1_attn_bk': (0.0, 0.8),
     'L1_attn_bv': (0.0, 0.8),
     'L1_attn_bo': (0.0, 0.336)}
    factors = {'L0_attn_w_qkv': 8.0,
     'L0_attn_w_out': 8.0,
     'L0_ffn_wq': 8.0,
     'L0_ffn_wk': 8.0,
     'L0_ffn_wv': 8.0,
     'L0_ffn_wo': 8.0,
     'L0_ffn_w1': 8.0,
     'L0_ffn_w2': 8.0,
     'L1_attn_Wq': 8.0,
     'L1_attn_Wk': 8.0,
     'L1_attn_Wv': 8.0,
     'L1_attn_Wo': 8.0}
    for name, (base, spread) in spreads.items():
        noise = np.random.default_rng([zlib.crc32(name.encode()), seed]).standard_normal(out[name].shape)
        drawn = base * np.exp(spread * noise) if base else spread * noise
        out[name] = jnp.asarray(drawn.astype(out[name].dtype))
    for name, factor in factors.items():
        out[name] = (out[name] * factor).astype(out[name].dtype)
    return out
```

```python
from contextlib import ExitStack

import numpy as np

import concourse.bass as bass
from concourse import mybir
from concourse.alu_op_type import AluOpType as ALU

ACT = mybir.ActivationFunctionType
AX = mybir.AxisListType.X
F32 = mybir.dt.float32
BF16 = mybir.dt.bfloat16
I32 = mybir.dt.int32

P = 128
D = 128
B = 4
S = 1024
T = S // P
HALF = S // 2
C = 2
H = 16
HD0 = 64
HD = D // H
MS = 512
MC = MS // P
SLOTS = P
TOPK = S // 8
F = 512
FC = F // P
E = 8
GH = 4
NG = H // GH
SCALE0 = HD0 ** -0.5
SCALE = HD ** -0.5
BIG = -1e30
LN_EPS = 1e-5
RMS_EPS = 1e-6
RSQRT_MAGIC = float(0x5F3759DF)
HM = 64
M_ROW = 32
TERMS = [(0, "h", "h"), (8, "h", "m"), (16, "m", "h"), (24, "h", "l"), (40, "m", "m"), (48, "l", "h")]

MAX_ITEMS = [(t, c, min(HALF, (t + 1) * P - c * HALF)) for t in range(T) for c in range(t // 4 + 1)]
EXP_ITEMS = [(c, j, max(0, j * P - c * HALF)) for c in range(C) for j in range(4 * c + 4)]
NI = len(EXP_ITEMS)
assert len(MAX_ITEMS) == NI == 12
MAX_AT = {3: (0, 1), 4: (2, 3), 5: (4, 5), 6: (6,), 7: (7, 8), 8: (9, 10), 9: (11,)}


def shape_constants():
    p = np.arange(P)
    eye = np.eye(P, dtype=np.float32)
    later = (p[None, :] > p[:, None]).astype(np.float32)
    rot0 = np.zeros((P, P), np.float32)
    rot1 = np.zeros((P, P), np.float32)
    for m in range(P):
        d = m % HD
        if d < HD // 2:
            rot0[m + HD // 2, m] = -1.0
        else:
            rot0[m - HD // 2, m] = 1.0
        if d < 6:
            rot1[m + 1 if d % 2 == 0 else m - 1, m] = -1.0 if d % 2 == 0 else 1.0
    tok = np.arange(S)
    frame, rest = tok // 256, tok % 256
    ids = np.stack([frame, rest // 16, rest % 16]).astype(np.float32)
    cos, sin = np.ones((P, S), np.float32), np.zeros((P, S), np.float32)
    for m in range(P):
        if m % HD < 6:
            cos[m], sin[m] = np.cos(ids[m % HD // 2]), np.sin(ids[m % HD // 2])
    parts = {
        "eye": eye,
        "mask_q": later * BIG,
        "mask_k": later.T * BIG,
        "before": later,
        "lower": later.T.copy(),
        "rot0": rot0,
        "rot1": rot1,
        "slot": np.broadcast_to(p.astype(np.float32), (P, P)),
        "row": (p[:, None] + P * np.arange(T)[None, :]).astype(np.float32),
        "head": (p[:, None] // HD == np.arange(H)[None, :]).astype(np.float32),
        "invf": np.broadcast_to((1.0 / np.float32(10000.0) ** (np.arange(0, HD, 2, dtype=np.float32) / HD)).astype(np.float32), (P, HD // 2)),
        "expert": np.broadcast_to(np.arange(E, dtype=np.float32) - E, (P, E)),
        "cos1": cos,
        "sin1": sin,
    }
    at, n = {}, 0
    for name, a in parts.items():
        at[name] = (n, n + a.shape[1])
        n += a.shape[1]
    return at, np.concatenate(list(parts.values()), axis=1).astype(np.float32)


def adaln_kernel(nc, i, out):
    CONST_AT, const_values = shape_constants()
    const_dram = nc.inline_tensor(const_values, "shape_constants")

    with ExitStack() as ctx:
        def sb(name, shape, dt=F32):
            return ctx.enter_context(nc.sbuf_tensor(name, shape, dt))

        consts = sb("consts", [P, const_values.shape[1]])

        def const(name):
            a, z = CONST_AT[name]
            return consts[:, a:z]

        eye = const("eye")
        eye_bf = sb("eye_bf", [P, P], BF16)
        mask_q = sb("mask_q_bf", [P, P], BF16)
        mask_k = sb("mask_k_bf", [P, P], BF16)
        ones = sb("ones", [P, P])
        silu_c = sb("silu_c", [P, 2, B])
        c_raw = sb("c_raw", [P, 2, B])
        c_den = sb("c_den", [P, 2, B])
        wmod = sb("wmod", [P, 2, 6 * D])
        w_out0 = sb("w_out0", [P, H // 2, D])
        router0 = sb("router0", [P, 1])
        router0_b = sb("router0_b", [P, 1])
        ln_rows = sb("ln_rows", [P, 2, D])
        ffn_w = sb("ffn_w", [P, 4, D])
        w1 = sb("w1", [P, F])
        w2 = sb("w2", [P, FC, D])
        attn_w = sb("attn_w", [P, 4, D])
        qk_bias = sb("qk_bias", [P, 2])
        vo_bias = sb("vo_bias", [P, 2, D])
        router1 = sb("router1", [P, E])
        experts = sb("experts", [P, E, D])
        pos_int = sb("pos_int", [P, B * MC], I32)
        pos_f = sb("pos_f", [P, B * MC])
        angle = sb("angle", [P, 2, B * MC, HD // 2])
        turns = sb("turns", [P, 2, B * MC, HD // 2])
        trig = sb("trig", [P, 2, B, MC, HD // 2])

        x = sb("x", [P, T, D])
        h = sb("h", [P, T, D])
        hT = sb("hT", [P, S])
        cond = sb("cond", [P, 2, P])
        mod = sb("mod", [P, 2, 6, D])
        stats = sb("stats", [P, T, 6])
        mv = sb("mv", [P, T, 2])
        nvar = sb("nvar", [P, T])
        nbits = sb("nbits", [P, T], I32)
        ntmp = sb("ntmp", [P, T])
        rstd = sb("rstd", [P, T])
        tmp = sb("tmp", [P, HALF])
        gate_abs = tmp[:, :].rearrange("p (l a d) -> p l a d", l=2, a=2)

        w_qkv = [sb(f"w_qkv{s}", [P, 3 * HD0]) for s in range(2)]
        qT = [sb(f"qT{s}", [P, S]) for s in range(2)]
        kT = [sb(f"kT{s}", [P, S]) for s in range(2)]
        q_bf = sb("q_bf", [P, S], BF16)
        k_bf = sb("k_bf", [P, S], BF16)
        v0 = [sb(f"v0{s}", [P, T, HD0]) for s in range(2)]
        part_max = sb("part_max", [P, T, C])
        neg_max = sb("neg_max", [P, T])
        probs_room = sb("probs", [P, 4, HALF])
        probs = [probs_room[:, n, :] for n in range(4)]
        o_raw = [sb(f"o_raw{c}", [P, HALF]) for c in range(C)]
        inv_den = sb("inv_den", [P, C, 4])
        room = sb("room", [P, 8 * S])
        oT = room[:, :].rearrange("p (g s) -> p g s", s=S)

        w_col = sb("w_col", [P, T])
        w_row = sb("w_row", [P, S])
        cmp = sb("cmp", [P, S], BF16)
        cnt = sb("cnt", [P, T, 3])
        rank = sb("rank", [P, T])
        sel = sb("sel", [P, T])
        thr_part = sb("thr_part", [P, 1])
        thr = sb("thr", [P, 1])
        unpicked = sb("unpicked", [P, T])
        slot_of = sb("slot_of", [P, T])
        pick = sb("pick", [P, T, SLOTS])
        pickT = sb("pickT", [P, S])
        extra = sb("extra", [P, T, 2])
        xs = sb("xs", [P, D])
        ws_idx = sb("ws_idx", [P, 2])
        idx_row = sb("idx_row", [P, SLOTS])
        mask_pick = sb("mask_pick", [P, MC, SLOTS])
        mask_in = sb("mask_in", [P, MC, MS])
        mask_rows = sb("mask_rows", [P, MC, SLOTS])
        mask_sel = sb("mask_sel", [P, SLOTS])
        trig_rep = sb("trig_rep", [P, 2, MC, H, HD // 2 * 2])
        trig_sel = sb("trig_sel", [P, 2, SLOTS])
        hn = sb("hn", [P, D])
        hnT = sb("hnT", [P, SLOTS])
        qk_s = sb("qk_s", [P, 2, SLOTS])
        rot_s = sb("rot_s", [P, 2, SLOTS])
        v_s = sb("v_s", [P, D])
        k_diag = room[:, 4 * S:6 * S].rearrange("p (h s) -> p h s", h=H)
        sc = room[:, 6 * S:8 * S].rearrange("p (h s) -> p h s", h=H)
        sc_max = sb("sc_max", [P, H])
        sc_sum = sb("sc_sum", [P, H])
        pT = probs_room[:, :, :].rearrange("p n (a s) -> p (n a) s", a=4)
        o_s = sb("o_s", [P, D])
        o_sT = sb("o_sT", [P, SLOTS])
        x1 = sb("x1", [P, D])
        gelu = sb("gelu", [P, FC, SLOTS])
        proc = sb("proc", [P, D])

        qk_f = room[:, 4 * S:6 * S].rearrange("p (a s) -> p a s", a=2)
        rot_f = w_row
        sc_room = room[:, 6 * S:8 * S].bitcast(BF16).rearrange("p (n s) -> p n s", s=S)
        pT_room = probs_room[:, :, :].rearrange("p n s -> p (n s)").bitcast(BF16).rearrange("p (n s) -> p n s", s=S)
        split = {"q": {n: sc_room[:, m, :] for m, n in enumerate("hml")}, "k": {n: pT_room[:, m, :] for m, n in enumerate("hml")}}
        q_stack = sb("q_stack", [P, H, S], BF16)
        k_stack = room[:, 0:4 * S].bitcast(BF16).rearrange("p (g s) -> p g s", s=S)
        v1 = room[:, 4 * S:8 * S].rearrange("p (t h c) -> p t h c", t=T, h=H)
        pmax1 = sb("pmax1", [P, GH, T, C])
        nmax1 = sb("nmax1", [P, GH, T])
        nmax_hl = sb("nmax_hl", [P, GH, T, 2], BF16)
        den1 = sb("den1", [P, 4, GH])
        ctx1 = pick
        ctxT = pickT

        lg = sb("lg", [P, T, E])
        m1 = sb("m1", [P, T])
        m2 = sb("m2", [P, T])
        e1 = sb("e1", [P, T])
        oh1 = sb("oh1", [P, T, E])
        oh2 = sb("oh2", [P, T, E])
        lg2 = sb("lg2", [P, T, E])
        coef = sb("coef", [P, T, E])
        bias_tok = sb("bias_tok", [P, T])
        moe = w_row[:, :].rearrange("p (t d) -> p t d", t=T)

        bank = [ctx.enter_context(nc.psum_tensor(f"bank{n}", [P, HALF], F32)) for n in range(8)]

        scratch = {a: {n: nc.dram_tensor(f"scratch_{a}{n}", [P, S], BF16).ap() for n in "hml"} for a in "qk"}

        ONCE = ("setup_loads setup_masks setup_pool setup_dve setup_c_exp setup_trig setup_chain "
                "batch_arrived batch_cleared batch_left").split()
        PER_BATCH = """
                 attn0_mm attn1_mm cast_go cond ctx1 ctxT ctx_raw ctx_tr den_col dve_chain ex_mm expd expd1 gather_mm gelu hn1
                 hn1T hn1_tr hn2 hn2T hn2_tr idx_row idx_tr inv_den inv_rows k_clear k_diag k_evac kb_cast lg_exp lg_mm lg_sub
                 mask_in mask_pick mask_rows mask_rows_mm mask_sel mask_sel0 mask_sel_mm mod_evac mod_mm moe mrow1 mrow1_mm
                 mrow_evac mrow_mm neg_max nmax_hl o1_raw o_norm o_raw o_s o_sT o_s_mm o_s_tr pT p_tr pick pickT pickT_tr proc
                 pv pv1 q_evac qb_cast qk1 qk1_mm qk_proj qk_s qkv_s_mm res_a res_b res_c rot0_mm rot1_done rot1_mm rot_s
                 row_max row_max1 s1_mm s_mm sc_exp sc_mm sc_sub scatter_mm scratch_k scratch_q sel slot_mm slot_of split1
                 st1_mm st_mm stack_clear stacks stored thr_mm thr_part trig_mm trig_rep trig_sel v1 v1_mm v_clear v_evac
                 v_proj v_s w1_mm w2_mm w_col w_head0 w_head1 w_mm w_row wo_mm wrow_tr ws_idx x_final x_in
        """.split() + [f"ln_{a}_{b_}" for a in "abcd" for b_ in ("stats", "mv", "n", "s", "h", "tr", "hT")]
        sems = {name: ctx.enter_context(nc.semaphore(name)) for name in ONCE + PER_BATCH}

        def sem(name):
            return sems[name]

        arrived, cleared, left = sem("batch_arrived"), sem("batch_cleared"), sem("batch_left")

        SETUP_LOADS = []

        def end_of_batch(eng):
            eng.drain().then_inc(arrived, 1)
            eng.wait_ge(cleared, 1)
            eng.sem_inc(left, 1)

        block = ctx.enter_context(nc.Block())

        @block.sync
        def _(sp):
            def load(dst, src, s="setup_loads"):
                sp.dma_start(dst, src, allow_slow_non_contiguous=True).then_inc(sem(s), 16)
                SETUP_LOADS.append(1)

            load(consts[:, :], const_dram[:])
            for l in range(2):
                load(wmod[:, l, :], i[f"L{l}_wmod"])
                load(c_raw[:, l, :], i[f"L{l}_c"].rearrange("b d -> d b"))
            load(pos_int[:, :], i["L0_ffn_position_ids"].rearrange("b (c p) -> p (b c)", p=P))
            load(w_out0[:, :, :], i["L0_attn_w_out"].rearrange("(g a) d e -> (a d) g e", a=2))
            load(router0[:, :], i["L0_ffn_router_w"])
            load(router0_b[:, :], i["L0_ffn_router_b"].rearrange("(a n) -> a n", a=1).broadcast_to([P, 1]))
            for n, name in enumerate(["L0_ffn_ln1", "L0_ffn_ln2"]):
                load(ln_rows[:, n, :], i[name].rearrange("(a n) -> a n", a=1).broadcast_to([P, D]))
            for n, name in enumerate(["L0_ffn_wq", "L0_ffn_wk", "L0_ffn_wv", "L0_ffn_wo"]):
                load(ffn_w[:, n, :], i[name])
            load(w1[:, :], i["L0_ffn_w1"])
            load(w2[:, :, :], i["L0_ffn_w2"].rearrange("(c p) n -> p c n", p=P))
            for n, name in enumerate(["L1_attn_Wq", "L1_attn_Wk", "L1_attn_Wv", "L1_attn_Wo"]):
                load(attn_w[:, n, :], i[name])
            for n, name in enumerate(["L1_attn_bq", "L1_attn_bk"]):
                load(qk_bias[:, n:n + 1], i[name].rearrange("(p a) -> p a", a=1))
            for n, name in enumerate(["L1_attn_bv", "L1_attn_bo"]):
                load(vo_bias[:, n, :], i[name].rearrange("(a n) -> a n", a=1).broadcast_to([P, D]))
            load(router1[:, :], i["L1_ffn_router_w"].rearrange("e d -> d e"))
            load(experts[:, :, :], i["L1_ffn_expert_weights"].rearrange("e h o -> h e o"))

            def load_head_weights(hh, s, first):
                if not first:
                    sp.wait_ge(sem("v_proj"), hh - 1)
                    sp.wait_ge(sem("qk_proj"), 2 * hh - 2)
                src = i["L0_attn_w_qkv"].rearrange("e h n -> h e n")
                sp.dma_start(w_qkv[s][:, :], src[hh, :, :]).then_inc(sem(f"w_head{s}"), 16)

            with sp.Fori(0, B) as b:
                sp.dma_start(x[:, :, :], i["L0_attn_x"][b, :, :].rearrange("(t p) d -> p t d", p=P)).then_inc(sem("x_in"), 16)
                load_head_weights(0, 0, True)
                load_head_weights(1, 1, True)
                sp.dma_start(mask_in[:, :, :], i["L0_ffn_attention_mask"][b, 0, :, :].rearrange("(c p) n -> p c n", p=P)).then_inc(sem("mask_in"), 16)
                with sp.Fori(0, H // 2 - 1) as g:
                    for s in range(2):
                        load_head_weights(2 * g + 2 + s, s, False)
                for n, a in enumerate("qk"):
                    for m, part in enumerate("hml"):
                        sp.wait_ge(sem("split1"), 3 * n + m + 1)
                        sp.dma_start(scratch[a][part], split[a][part]).then_inc(sem(f"scratch_{a}"), 16)
                sp.wait_ge(sem("stack_clear"), 4)
                sp.wait_ge(sem("k_clear"), 3)
                for a, stack in (("q", q_stack), ("k", k_stack)):
                    sp.wait_ge(sem(f"scratch_{a}"), 48)
                    for row, qn, kn in TERMS:
                        src = scratch[a][qn if a == "q" else kn].rearrange("(g a d) t -> a d g t", a=2, d=HD)
                        for par in range(2):
                            rows = slice(par * HM + row, par * HM + row + HD)
                            dst = q_stack[rows, par::2, :] if a == "q" else k_stack[rows, :, :]
                            sp.dma_start(dst, src[par]).then_inc(sem("stacks"), 16)
                for t in range(T):
                    sp.wait_ge(sem("x_final"), t + 1)
                    sp.dma_start(out[b, t * P:(t + 1) * P, :], x[:, t, :]).then_inc(sem("stored"), 16)
                sp.wait_ge(sem("stored"), 16 * T)
                end_of_batch(sp)

        N_SETUP_LOADS = 16 * len(SETUP_LOADS)

        @block.gpsimd
        def _(pool):
            def set_once(count, ap, value):
                if count:
                    pool.wait_ge(sem("setup_pool"), count)
                pool.memset(ap, value).then_inc(sem("setup_pool"), 1)

            fills = [(ones[:, :], 1.0)]
            for s in range(2):
                fills += [(qT[s][HD0:P, :], 0.0), (kT[s][HD0:P, :], 0.0), (kT[s][HD0:HD0 + 1, :], 1.0)]
            fills += [(q_bf[HD0:P, :], 0.0), (k_bf[HD0:P, :], 0.0), (part_max[:, 0:4, 1:2], -3e38),
                      (q_stack[:, :, :].rearrange("p h s -> p (h s)").bitcast(F32), 0.0)]
            for count, (ap, value) in enumerate(fills):
                set_once(count, ap, value)
            pool.wait_ge(sem("setup_pool"), len(fills))

            def cast_head(hh, s, first):
                for c in range(C):
                    cols = slice(c * HALF, (c + 1) * HALF)
                    if not first:
                        pool.wait_ge(sem("s_mm"), NI * hh)
                    pool.wait_ge(sem("q_evac"), 2 * hh + c + 1)
                    pool.sem_inc(sem("cast_go"), 1)
                    pool.tensor_copy(q_bf[0:HD0, cols], qT[s][0:HD0, cols]).then_inc(sem("qb_cast"), 1)
                    pool.wait_ge(sem("k_evac"), 2 * hh + c + 1)
                    pool.sem_inc(sem("cast_go"), 1)
                    pool.tensor_copy(k_bf[0:HD0, cols], kT[s][0:HD0, cols]).then_inc(sem("kb_cast"), 1)

            with pool.Fori(0, B) as b:
                for par in range(2):
                    for hf in range(2):
                        rows = slice(par * HM + M_ROW, par * HM + M_ROW + 2)
                        heads = slice(par + 8 * hf, par + 8 * hf + 7, 2)
                        if par + hf:
                            pool.wait_ge(sem("stack_clear"), 2 * par + hf)
                        pool.memset(q_stack[rows, heads, :], 0.0).then_inc(sem("stack_clear"), 1)
                pool.wait_ge(sem("stack_clear"), 4)
                cast_head(0, 0, True)
                with pool.Fori(0, H // 2 - 1) as g:
                    cast_head(2 * g + 1, 1, False)
                    cast_head(2 * g + 2, 0, False)
                cast_head(H - 1, 1, False)
                pool.wait_ge(sem("kb_cast"), 2 * H)
                pool.wait_ge(sem("attn0_mm"), 2)
                pool.memset(room[:, 0:4 * S], 0.0).then_inc(sem("k_clear"), 1)
                for par in range(2):
                    pool.wait_ge(sem("k_clear"), par + 1)
                    pool.memset(k_stack[par * HM + M_ROW:par * HM + M_ROW + 2, :, :], 1.0).then_inc(sem("k_clear"), 1)
                pool.wait_ge(sem("k_clear"), 3)
                pool.wait_ge(sem("scratch_q"), 48)
                pool.wait_ge(sem("scratch_k"), 48)
                pool.memset(room[:, 4 * S:8 * S], 0.0).then_inc(sem("v_clear"), 1)
                pool.wait_ge(sem("v_clear"), 1)
                pool.memset(v1[:, :, :, HD:HD + 1], 1.0).then_inc(sem("v_clear"), 1)
                pool.wait_ge(sem("v_clear"), 2)
                pool.drain().then_inc(arrived, 1)
                pool.wait_ge(arrived, 5)
                for name in PER_BATCH:
                    pool.sem_clear(sem(name))
                pool.sem_clear(arrived)
                pool.drain()
                pool.sem_inc(cleared, 1)
                pool.wait_ge(left, 4)
                pool.sem_clear(left)
                pool.sem_clear(cleared)

        @block.scalar
        def _(act):
            act.wait_ge(sem("setup_loads"), N_SETUP_LOADS)
            act.activation(c_den[:, :, :], c_raw[:, :, :], ACT.Exp, scale=-1.0).then_inc(sem("setup_c_exp"), 1)
            act.wait_ge(sem("setup_dve"), 1)
            act.activation(trig[:, :, :, :, :].rearrange("p a b c f -> p (a b c f)"), angle[:, :, :, :].rearrange("p a n f -> p (a n f)"), ACT.Sin).then_inc(sem("setup_trig"), 1)

            def copy(dst, src):
                return act.activation(dst, src, ACT.Copy)

            def evac_hT(name):
                for c in range(C):
                    act.wait_ge(sem(name + "_tr"), c + 1)
                    copy(hT[:, c * HALF:(c + 1) * HALF], bank[6 + c][:, :]).then_inc(sem(name + "_hT"), 1)

            def prep_early(hh, s, first):
                for c in range(C):
                    act.wait_ge(sem("qk_proj"), 2 * hh + c + 1)
                    if not first:
                        act.wait_ge(sem("st_mm"), NI * (hh - 1))
                    copy(qT[s][0:HD0, c * HALF:(c + 1) * HALF], bank[6 + c][0:HD0, :]).then_inc(sem("q_evac"), 1)

            def prep_v(hh, s, first):
                act.wait_ge(sem("v_proj"), hh + 1)
                if not first:
                    act.wait_ge(sem("pv"), NI * (hh - 1))
                copy(v0[s][:, :, :], bank[6][:, :].rearrange("p (t d) -> p t d", t=T)).then_inc(sem("v_evac"), 1)

            def prep_max(hh, s):
                for c in range(C):
                    act.wait_ge(sem("mrow_mm"), 2 * hh + c + 1)
                    copy(qT[s][HD0:HD0 + 1, c * HALF:(c + 1) * HALF], bank[6 + c][HD0:HD0 + 1, :]).then_inc(sem("mrow_evac"), 1)

            def exps(hh, s, nxt, first=False):
                for n, (c, j, lo) in enumerate(EXP_ITEMS):
                    act.wait_ge(sem("st_mm"), NI * hh + n + 1)
                    if not (first and n < 4):
                        act.wait_ge(sem("pv"), NI * hh + n - 3)
                    act.activation(probs[n % 4][:, 0:HALF - lo], bank[2 + n % 2][:, lo:HALF], ACT.Exp, scale=SCALE0).then_inc(sem("expd"), 1)
                    if nxt:
                        if n == 0:
                            prep_early(hh + 1, 1 - s, first)
                        if n == 2:
                            prep_v(hh + 1, 1 - s, first)
                if nxt:
                    prep_max(hh + 1, 1 - s)

            with act.Fori(0, B) as b:
                for l in range(2):
                    for a in range(2):
                        act.wait_ge(sem("mod_mm"), 2 * l + a + 1)
                        copy(mod[:, l, 3 * a:3 * a + 3, :].rearrange("p a d -> p (a d)"), bank[2 * l + a][:, 0:3 * D]).then_inc(sem("mod_evac"), 1)
                evac_hT("ln_a")
                prep_early(0, 0, True)
                prep_v(0, 0, True)
                prep_max(0, 0)
                exps(0, 0, True, first=True)
                exps(1, 1, True)
                with act.Fori(1, H // 2 - 1) as g:
                    exps(2 * g, 0, True)
                    exps(2 * g + 1, 1, True)
                exps(H - 2, 0, True)
                exps(H - 1, 1, False)
                evac_hT("ln_b")
                for c in range(C):
                    act.wait_ge(sem("wrow_tr"), c + 1)
                    copy(w_row[:, c * HALF:(c + 1) * HALF], bank[1 + c][:, :]).then_inc(sem("w_row"), 1)
                for c in range(C):
                    act.wait_ge(sem("pickT_tr"), c + 1)
                    copy(pickT[:, c * HALF:(c + 1) * HALF], bank[1 + c][:, :]).then_inc(sem("pickT"), 1)
                act.wait_ge(sem("mask_rows_mm"), 1)
                copy(mask_rows[:, :, :], bank[0][:, :].rearrange("p (c s) -> p c s", c=MC)).then_inc(sem("mask_rows"), 1)
                act.wait_ge(sem("trig_mm"), 1)
                copy(trig_sel[:, :, :], bank[2][:, 0:2 * SLOTS].rearrange("p (a s) -> p a s", a=2)).then_inc(sem("trig_sel"), 1)
                act.wait_ge(sem("hn1_tr"), 1)
                copy(hnT[:, :], bank[4][:, 0:SLOTS]).then_inc(sem("hn1T"), 1)
                act.wait_ge(sem("qkv_s_mm"), 1)
                copy(qk_s[:, :, :], bank[5][:, 0:2 * SLOTS].rearrange("p (a s) -> p a s", a=2)).then_inc(sem("qk_s"), 1)
                act.wait_ge(sem("qkv_s_mm"), 2)
                copy(v_s[:, :], bank[6][:, 0:D]).then_inc(sem("v_s"), 1)
                act.wait_ge(sem("sc_sub"), 1)
                act.activation(sc[:, :, :], sc[:, :, :], ACT.Exp).then_inc(sem("sc_exp"), 1)
                for n in range(4):
                    act.wait_ge(sem("p_tr"), n + 1)
                    copy(pT[:, 4 * n:4 * n + 4, :], bank[4 + n][:, :].rearrange("p (a s) -> p a s", a=4)).then_inc(sem("pT"), 1)
                act.wait_ge(sem("o_s_tr"), 1)
                copy(o_sT[:, :], bank[1][:, 0:SLOTS]).then_inc(sem("o_sT"), 1)
                act.wait_ge(sem("hn2_tr"), 1)
                copy(hnT[:, :], bank[3][:, 0:SLOTS]).then_inc(sem("hn2T"), 1)
                act.wait_ge(sem("w1_mm"), 1)
                act.activation(gelu[:, :, :], bank[4][:, :].rearrange("p (c s) -> p c s", c=FC), ACT.Gelu_apprx_tanh).then_inc(sem("gelu"), 1)
                evac_hT("ln_c")
                for n in range(2):
                    for c in range(C):
                        act.wait_ge(sem("qk1_mm"), 2 * n + c + 1)
                        act.activation(qk_f[:, n, c * HALF:(c + 1) * HALF], bank[2 * n + c][:, :], ACT.Identity, bias=qk_bias[:, n:n + 1]).then_inc(sem("qk1"), 1)

                def max_rows(g):
                    for a in range(GH):
                        for c in range(C):
                            n = 8 * g + 2 * a + c
                            hh = GH * g + a
                            r = (a % 2) * HM + M_ROW
                            act.wait_ge(sem("mrow1_mm"), n + 1)
                            copy(q_stack[r:r + 2, hh, c * HALF:(c + 1) * HALF], bank[6 + c][r:r + 2, :]).then_inc(sem("mrow1"), 1)

                max_rows(0)
                for g in range(NG):
                    for n in range(64):
                        m = 64 * g + n
                        act.wait_ge(sem("st1_mm"), m + 1)
                        if m >= 4:
                            act.wait_ge(sem("pv1"), m - 3)
                        act.activation(probs[n % 4][:, :], bank[2 + n % 2][:, :], ACT.Exp, scale=SCALE).then_inc(sem("expd1"), 1)
                    if g < NG - 1:
                        max_rows(g + 1)
                for c in range(C):
                    act.wait_ge(sem("ctx_tr"), c + 1)
                    copy(ctxT[:, c * HALF:(c + 1) * HALF], bank[c][:, :]).then_inc(sem("ctxT"), 1)
                evac_hT("ln_d")
                act.wait_ge(sem("lg_sub"), 1)
                act.activation(lg[:, :, :], lg[:, :, :], ACT.Exp).then_inc(sem("lg_exp"), 1)
                end_of_batch(act)

        @block.tensor
        def _(pe):
            def mm(dst, lhsT, rhs, start=True, stop=True):
                return pe.matmul(dst, lhsT, rhs, start=start, stop=stop)

            pe.wait_ge(sem("setup_pool"), 11)
            pe.wait_ge(sem("setup_dve"), 1)
            pe.wait_ge(sem("setup_masks"), 3)

            def transpose_h(name):
                for c in range(C):
                    for t in range(4 * c, 4 * c + 4):
                        pe.wait_ge(sem(name + "_h"), t + 1)
                        last = pe.transpose(bank[6 + c][:, (t % 4) * P:(t % 4 + 1) * P], h[:, t, :], eye)
                    last.then_inc(sem(name + "_tr"), 1)

            def project(hh, s, first):
                pe.wait_ge(sem(f"w_head{s}"), 16 * (hh // 2 + 1) if isinstance(hh, int) else 16 * w_round(hh, s))
                for c in range(C):
                    if not first:
                        pe.wait_ge(sem("mrow_evac"), 2 * hh - 1 + c)
                    mm(bank[6 + c][:, :], w_qkv[s][:, 0:2 * HD0], hT[:, c * HALF:(c + 1) * HALF]).then_inc(sem("qk_proj"), 1)

            def w_round(hh, s):
                return (hh - s) // 2 + 1

            def project_v(hh, s):
                pe.wait_ge(sem("q_evac"), 2 * hh + 1)
                pe.wait_ge(sem("k_evac"), 2 * hh + 1)
                for t in range(T):
                    last = mm(bank[6][:, t * HD0:(t + 1) * HD0], hT[:, t * P:(t + 1) * P], w_qkv[s][:, 2 * HD0:])
                last.then_inc(sem("v_proj"), 1)

            def max_item(hh, n, first):
                t, c, w = MAX_ITEMS[n]
                dst = bank[n % 2]
                pe.wait_ge(sem("qb_cast"), 2 * hh + t // 4 + 1)
                pe.wait_ge(sem("kb_cast"), 2 * hh + c + 1)
                if not (first and n < 2):
                    pe.wait_ge(sem("row_max"), NI * hh + n - 1)
                diag = c == t // 4
                last = mm(dst[:, 0:w], q_bf[:, t * P:(t + 1) * P], k_bf[:, c * HALF:c * HALF + w], stop=not diag)
                if diag:
                    last = mm(dst[:, w - P:w], eye_bf[:, :], mask_q[:, :], start=False)
                last.then_inc(sem("s_mm"), 1)

            def max_to_row(hh):
                pe.wait_ge(sem("neg_max"), hh + 1)
                pe.wait_ge(sem("v_evac"), hh + 1)
                pe.wait_ge(sem("q_evac"), 2 * hh + 2)
                pe.wait_ge(sem("k_evac"), 2 * hh + 2)
                for c in range(C):
                    for t in range(4):
                        last = mm(bank[6 + c][HD0:HD0 + 1, t * P:(t + 1) * P], neg_max[:, 4 * c + t:4 * c + t + 1], eye)
                    last.then_inc(sem("mrow_mm"), 1)

            def st_item(hh, s, n, first):
                c, j, lo = EXP_ITEMS[n]
                dst = bank[2 + n % 2]
                if n == 0:
                    pe.wait_ge(sem("mrow_evac"), 2 * hh + 2)
                if not (first and n < 2):
                    pe.wait_ge(sem("expd"), NI * hh + n - 1)
                diag = j * P >= c * HALF
                last = mm(dst[:, lo:], kT[s][:, j * P:(j + 1) * P], qT[s][:, c * HALF + lo:(c + 1) * HALF], stop=not diag)
                if diag:
                    last = mm(dst[:, lo:lo + P], eye_bf[:, :], mask_k[:, :], start=False)
                last.then_inc(sem("st_mm"), 1)

            def pv_item(hh, s, n, first):
                c, j, lo = EXP_ITEMS[n]
                pe.wait_ge(sem("expd"), NI * hh + n + 1)
                if j == 0 and not first:
                    pe.wait_ge(sem("o_norm"), 2 * hh - 1 + c)
                p = probs[n % 4][:, 0:HALF - lo]
                end = j == 4 * c + 3
                mm(bank[4 + c][0:HD0, lo:], v0[s][:, j, :], p, start=j == 0, stop=end)
                mm(bank[4 + c][HD0:HD0 + 1, lo:], ones[:, 0:1], p, start=j == 0, stop=end).then_inc(sem("pv"), 1)

            def den_to_column(hh, c):
                pe.wait_ge(sem("o_raw"), 2 * hh + c + 1)
                for t in range(4):
                    last = mm(bank[4 + c][:, t:t + 1], o_raw[c][HD0:HD0 + 1, t * P:(t + 1) * P], ones[HD0:HD0 + 1, 0:1])
                last.then_inc(sem("den_col"), 1)

            def inv_to_rows(hh, c):
                pe.wait_ge(sem("inv_den"), 2 * hh + c + 1)
                for t in range(4):
                    last = pe.transpose(bank[4 + c][:, t * P:(t + 1) * P], inv_den[:, c, t:t + 1].to_broadcast([P, P]), eye)
                last.then_inc(sem("inv_rows"), 1)

            def head(hh, s, nxt, first=False):
                st_item(hh, s, 0, first)
                for n in range(NI):
                    if n + 1 < NI:
                        st_item(hh, s, n + 1, first)
                    if nxt and n == 0:
                        project(hh + 1, 1 - s, False)
                    if nxt and n == 1:
                        project_v(hh + 1, 1 - s)
                    if nxt:
                        for m in MAX_AT.get(n, ()):
                            max_item(hh + 1, m, False)
                    pv_item(hh, s, n, first)
                    if n == 5:
                        den_to_column(hh, 0)
                    if n == 7:
                        inv_to_rows(hh, 0)
                if nxt:
                    max_to_row(hh + 1)
                den_to_column(hh, 1)
                inv_to_rows(hh, 1)

            with pe.Fori(0, B) as b:
                for l in range(2):
                    pe.wait_ge(sem("cond"), l + 1)
                    for a in range(2):
                        mm(bank[2 * l + a][:, 0:3 * D], cond[:, l, :], wmod[:, l, 3 * a * D:3 * (a + 1) * D]).then_inc(sem("mod_mm"), 1)
                transpose_h("ln_a")
                pe.wait_ge(sem("ln_a_hT"), 2)
                pe.wait_ge(sem("mod_evac"), 4)
                project(0, 0, True)
                project_v(0, 0)
                for n in range(NI):
                    max_item(0, n, True)
                max_to_row(0)
                head(0, 0, True, first=True)
                head(1, 1, True)
                with pe.Fori(1, H // 2 - 1) as g:
                    head(2 * g, 0, True)
                    head(2 * g + 1, 1, True)
                head(H - 2, 0, True)
                head(H - 1, 1, False)
                for c in range(C):
                    pe.wait_ge(sem("o_norm"), 2 * H - 1 + c)
                    for t in range(4 * c, 4 * c + 4):
                        for g in range(H // 2):
                            last = mm(bank[c][:, (t % 4) * P:(t % 4 + 1) * P], oT[:, g, t * P:(t + 1) * P], w_out0[:, g, :], start=g == 0, stop=g == H // 2 - 1)
                    last.then_inc(sem("attn0_mm"), 1)
                transpose_h("ln_b")
                pe.wait_ge(sem("ln_b_hT"), 2)
                pe.wait_ge(sem("res_a"), 2)
                for t in range(T):
                    last = mm(bank[0][:, t:t + 1], hT[:, t * P:(t + 1) * P], router0[:, :])
                last.then_inc(sem("w_mm"), 1)
                pe.wait_ge(sem("w_col"), 1)
                for c in range(C):
                    for t in range(4 * c, 4 * c + 4):
                        last = pe.transpose(bank[1 + c][:, (t % 4) * P:(t % 4 + 1) * P], w_col[:, t:t + 1].to_broadcast([P, P]), eye)
                    last.then_inc(sem("wrow_tr"), 1)
                pe.wait_ge(sem("thr_part"), 1)
                mm(bank[3][:, 0:1], ones[:, :], thr_part[:, :]).then_inc(sem("thr_mm"), 1)
                pe.wait_ge(sem("sel"), 1)
                last = mm(bank[4][:, 0:T], const("before"), sel[:, :], stop=False)
                for t in range(T - 1):
                    last = mm(bank[4][:, t + 1:T], ones[:, :], sel[:, t:t + 1].to_broadcast([P, T - 1 - t]), start=False, stop=t == T - 2)
                last.then_inc(sem("slot_mm"), 1)
                pe.wait_ge(sem("pick"), T)
                for t in range(T):
                    last = mm(bank[6][:, 0:2], pick[:, t, :], extra[:, t, :], start=t == 0, stop=t == T - 1)
                last.then_inc(sem("gather_mm"), 1)
                for t in range(T):
                    last = mm(bank[5][:, 0:D], pick[:, t, :], h[:, t, :], start=t == 0, stop=t == T - 1)
                last.then_inc(sem("gather_mm"), 1)
                pe.wait_ge(sem("ws_idx"), 1)
                pe.transpose(bank[7][:, 0:SLOTS], ws_idx[:, 1:2].to_broadcast([P, P]), eye).then_inc(sem("idx_tr"), 1)
                for c in range(C):
                    for t in range(4 * c, 4 * c + 4):
                        last = pe.transpose(bank[1 + c][:, (t % 4) * P:(t % 4 + 1) * P], pick[:, t, :], eye)
                    last.then_inc(sem("pickT_tr"), 1)
                pe.wait_ge(sem("mask_pick"), MC)
                pe.wait_ge(sem("mask_in"), 16)
                for c in range(MC):
                    for r in range(MC):
                        last = mm(bank[0][:, c * P:(c + 1) * P], mask_in[:, r, c * P:(c + 1) * P], mask_pick[:, r, :], start=r == 0, stop=r == MC - 1)
                last.then_inc(sem("mask_rows_mm"), 1)
                pe.wait_ge(sem("trig_rep"), 2)
                pe.wait_ge(sem("pickT"), 2)
                for a in range(2):
                    for c in range(MC):
                        last = mm(bank[2][:, a * SLOTS:(a + 1) * SLOTS], trig_rep[:, a, c, :, :].rearrange("p h d -> p (h d)"), mask_pick[:, c, :], start=c == 0, stop=c == MC - 1)
                last.then_inc(sem("trig_mm"), 1)
                pe.wait_ge(sem("mask_rows"), 1)
                for c in range(MC):
                    last = mm(bank[1][:, 0:SLOTS], mask_rows[:, c, :], mask_pick[:, c, :], start=c == 0, stop=c == MC - 1)
                last.then_inc(sem("mask_sel_mm"), 1)
                pe.wait_ge(sem("hn1"), 1)
                pe.wait_ge(sem("slot_of"), 1)
                pe.transpose(bank[4][:, 0:SLOTS], hn[:, :], eye).then_inc(sem("hn1_tr"), 1)
                pe.wait_ge(sem("hn1T"), 1)
                for n in range(2):
                    last = mm(bank[5][:, n * SLOTS:(n + 1) * SLOTS], ffn_w[:, n, :], hnT[:, :])
                last.then_inc(sem("qkv_s_mm"), 1)
                mm(bank[6][:, 0:D], hnT[:, :], ffn_w[:, 2, :]).then_inc(sem("qkv_s_mm"), 1)
                pe.wait_ge(sem("qk_s"), 1)
                pe.wait_ge(sem("idx_row"), 1)
                mm(bank[7][:, 0:2 * SLOTS], const("rot0"), qk_s[:, :, :].rearrange("p a s -> p (a s)")).then_inc(sem("rot0_mm"), 1)
                pe.wait_ge(sem("k_diag"), 1)
                pe.wait_ge(sem("mask_sel"), 1)
                pe.wait_ge(sem("trig_sel"), 1)
                for n in range(4):
                    mm(bank[n][:, :], qk_s[:, 0, :], k_diag[:, 4 * n:4 * n + 4, :].rearrange("p a s -> p (a s)")).then_inc(sem("sc_mm"), 1)
                pe.wait_ge(sem("sc_exp"), 1)
                pe.wait_ge(sem("v_s"), 1)
                pe.wait_ge(sem("rot_s"), 1)
                for n in range(4):
                    for a in range(4):
                        last = pe.transpose(bank[4 + n][:, a * P:(a + 1) * P], sc[:, 4 * n + a, :], eye)
                    last.then_inc(sem("p_tr"), 1)
                for n in range(4):
                    pe.wait_ge(sem("pT"), n + 1)
                    for a in range(4):
                        hh = 4 * n + a
                        last = mm(bank[0][:, hh * HD:(hh + 1) * HD], pT[:, hh, :], v_s[:, hh * HD:(hh + 1) * HD])
                last.then_inc(sem("o_s_mm"), 1)
                pe.wait_ge(sem("o_s"), 1)
                pe.transpose(bank[1][:, 0:SLOTS], o_s[:, :], eye).then_inc(sem("o_s_tr"), 1)
                pe.wait_ge(sem("o_sT"), 1)
                mm(bank[2][:, 0:D], o_sT[:, :], ffn_w[:, 3, :]).then_inc(sem("wo_mm"), 1)
                pe.wait_ge(sem("hn2"), 1)
                pe.transpose(bank[3][:, 0:SLOTS], hn[:, :], eye).then_inc(sem("hn2_tr"), 1)
                pe.wait_ge(sem("hn2T"), 1)
                for c in range(FC):
                    last = mm(bank[4][:, c * SLOTS:(c + 1) * SLOTS], w1[:, c * P:(c + 1) * P], hnT[:, :])
                last.then_inc(sem("w1_mm"), 1)
                pe.wait_ge(sem("gelu"), 1)
                for c in range(FC):
                    last = mm(bank[5][:, 0:D], gelu[:, c, :], w2[:, c, :], start=c == 0, stop=c == FC - 1)
                last.then_inc(sem("w2_mm"), 1)
                pe.wait_ge(sem("proc"), 1)
                for c in range(C):
                    for t in range(4 * c, 4 * c + 4):
                        last = mm(bank[c][:, (t % 4) * P:(t % 4 + 1) * P], pickT[:, t * P:(t + 1) * P], proc[:, :])
                    last.then_inc(sem("scatter_mm"), 1)
                transpose_h("ln_c")
                pe.wait_ge(sem("ln_c_hT"), 2)
                pe.wait_ge(sem("res_b"), 2)
                for n in range(2):
                    for c in range(C):
                        mm(bank[2 * n + c][:, :], attn_w[:, n, :], hT[:, c * HALF:(c + 1) * HALF]).then_inc(sem("qk1_mm"), 1)
                for n in range(2):
                    for c in range(C):
                        pe.wait_ge(sem("qk1"), 2 * n + c + 1)
                        mm(bank[4 + 2 * n + c][:, :], const("rot1"), qk_f[:, n, c * HALF:(c + 1) * HALF]).then_inc(sem("rot1_mm"), 1)
                for c in range(C):
                    for t in range(4 * c, 4 * c + 4):
                        last = mm(bank[c][:, (t % 4) * P:(t % 4 + 1) * P], hT[:, t * P:(t + 1) * P], attn_w[:, 2, :])
                    last.then_inc(sem("v1_mm"), 1)
                pe.wait_ge(sem("stacks"), 16 * 4 * len(TERMS))
                pe.wait_ge(sem("v1"), 2)
                pe.wait_ge(sem("rot1_done"), 4)

                def max1_item(g, n):
                    t, a, c = n // 8, n // 2 % 4, n % 2
                    m = 64 * g + n
                    hh = GH * g + a
                    if m >= 2:
                        pe.wait_ge(sem("row_max1"), m - 1)
                    mm(bank[n % 2][:, :], q_stack[:, hh, t * P:(t + 1) * P], k_stack[:, hh // 2, c * HALF:(c + 1) * HALF]).then_inc(sem("s1_mm"), 1)

                def max1_to_rows(g):
                    pe.wait_ge(sem("nmax_hl"), g + 1)
                    if g:
                        pe.wait_ge(sem("ctx1"), 2 * g)
                    for a in range(GH):
                        r = (a % 2) * HM + M_ROW
                        for c in range(C):
                            n = 8 * g + 2 * a + c
                            if n % 8 >= 2:
                                pe.wait_ge(sem("mrow1"), n - 1)
                            for t in range(4):
                                last = pe.matmul(bank[6 + c][r:r + 2, t * P:(t + 1) * P], nmax_hl[:, a, 4 * c + t, :], eye_bf[:, :], start=True, stop=True)
                            last.then_inc(sem("mrow1_mm"), 1)

                def st1_item(g, n):
                    c, j, a = n // 32, n // 4 % 8, n % 4
                    m = 64 * g + n
                    hh = GH * g + a
                    if n == 0:
                        pe.wait_ge(sem("mrow1"), 8 * g + 8)
                    if m >= 2:
                        pe.wait_ge(sem("expd1"), m - 1)
                    mm(bank[2 + n % 2][:, :], k_stack[:, hh // 2, j * P:(j + 1) * P], q_stack[:, hh, c * HALF:(c + 1) * HALF]).then_inc(sem("st1_mm"), 1)

                def pv1_item(g, n):
                    c, j, a = n // 32, n // 4 % 8, n % 4
                    m = 64 * g + n
                    pe.wait_ge(sem("expd1"), m + 1)
                    if j == 0 and g:
                        pe.wait_ge(sem("o1_raw"), 2 * g - 1 + c)
                    mm(bank[4 + c][32 * a:32 * a + 32, :], v1[:, j, GH * g + a, :], probs[n % 4][:, :], start=j == 0, stop=j == T - 1).then_inc(sem("pv1"), 1)

                def ctx_transposes(g, c):
                    pe.wait_ge(sem("o1_raw"), 2 * g + c + 1)
                    for t in range(4):
                        last = pe.transpose(bank[6 + c][:, t * P:(t + 1) * P], o_raw[c][:, t * P:(t + 1) * P], eye)
                    last.then_inc(sem("ctx_raw"), 1)

                for n in range(64):
                    max1_item(0, n)
                max1_to_rows(0)
                for g in range(NG):
                    st1_item(g, 0)
                    for n in range(64):
                        if n + 1 < 64:
                            st1_item(g, n + 1)
                        if g + 1 < NG:
                            max1_item(g + 1, n)
                        pv1_item(g, n)
                        if n == 36:
                            ctx_transposes(g, 0)
                    ctx_transposes(g, 1)
                    if g + 1 < NG:
                        max1_to_rows(g + 1)
                for c in range(C):
                    pe.wait_ge(sem("ctx1"), 2 * NG - 1 + c)
                    for t in range(4 * c, 4 * c + 4):
                        last = pe.transpose(bank[c][:, (t % 4) * P:(t % 4 + 1) * P], ctx1[:, t, :], eye)
                    last.then_inc(sem("ctx_tr"), 1)
                for c in range(C):
                    pe.wait_ge(sem("ctxT"), c + 1)
                    for t in range(4 * c, 4 * c + 4):
                        last = mm(bank[2 + c][:, (t % 4) * P:(t % 4 + 1) * P], ctxT[:, t * P:(t + 1) * P], attn_w[:, 3, :])
                    last.then_inc(sem("attn1_mm"), 1)
                transpose_h("ln_d")
                pe.wait_ge(sem("ln_d_hT"), 2)
                for t in range(T):
                    last = mm(bank[0][:, t * E:(t + 1) * E], hT[:, t * P:(t + 1) * P], router1[:, :])
                last.then_inc(sem("lg_mm"), 1)
                pe.wait_ge(sem("res_c"), 2)
                for t in range(T):
                    for a in range(2):
                        n = 2 * t + a
                        if n >= 4:
                            pe.wait_ge(sem("moe"), n - 3)
                        mm(bank[2 + n % 4][:, :], hT[:, t * P:(t + 1) * P], experts[:, 4 * a:4 * a + 4, :].rearrange("p e d -> p (e d)")).then_inc(sem("ex_mm"), 1)
                end_of_batch(pe)

        @block.vector
        def _(dve):
            links = {}

            def link(ins, s="dve_chain", base=0):
                links[s] = links.get(s, 0) + 1
                ins.then_inc(sem(s), 1)
                dve.wait_ge(sem(s), links[s])

            def tt(dst, a, b_, op):
                return dve.tensor_tensor(dst, a, b_, op)

            dve.wait_ge(sem("setup_loads"), N_SETUP_LOADS)
            dve.tensor_copy(eye_bf[:, :], eye).then_inc(sem("setup_masks"), 1)
            dve.tensor_copy(mask_q[:, :], const("mask_q")).then_inc(sem("setup_masks"), 1)
            dve.tensor_copy(mask_k[:, :], const("mask_k")).then_inc(sem("setup_masks"), 1)
            dve.wait_ge(sem("setup_c_exp"), 1)
            SC = "setup_chain"
            link(dve.tensor_scalar(c_den[:, :, :], c_den[:, :, :], 1.0, None, ALU.add), SC)
            link(dve.reciprocal(c_den[:, :, :], c_den[:, :, :]), SC)
            link(tt(silu_c[:, :, :], c_raw[:, :, :], c_den[:, :, :], ALU.mult), SC)
            link(dve.tensor_copy(pos_f[:, :], pos_int[:, :]), SC)
            link(tt(angle[:, 1, :, :], pos_f[:, :].unsqueeze(2).to_broadcast([P, B * MC, HD // 2]),
                    const("invf").unsqueeze(1).to_broadcast([P, B * MC, HD // 2]), ALU.mult), SC)
            link(dve.tensor_copy(angle[:, 0, :, :], angle[:, 1, :, :]), SC)
            round_to = 12582912.0
            for a in range(2):
                link(dve.tensor_scalar(turns[:, a, :, :], angle[:, a, :, :], 1.0 / (2.0 * np.pi), 0.25 * (1 - a), ALU.mult, ALU.add), SC)
            link(dve.tensor_scalar(turns[:, :, :, :], turns[:, :, :, :], round_to, None, ALU.add), SC)
            link(dve.tensor_scalar(turns[:, :, :, :], turns[:, :, :, :], -round_to, None, ALU.add), SC)
            two_pi = 2.0 * np.pi
            part1 = 6.28125
            part2 = float(np.float32(round((two_pi - part1) * 2 ** 21) / 2 ** 21))
            part3 = two_pi - part1 - part2
            tn, an = turns[:, :, :, :].rearrange("p a n f -> p (a n f)"), angle[:, :, :, :].rearrange("p a n f -> p (a n f)")
            for part in (part1, part2, part3):
                link(dve.scalar_tensor_tensor(an, tn, -part, an, ALU.mult, ALU.add), SC)
            link(dve.tensor_scalar(angle[:, 0, :, :], angle[:, 0, :, :], float(np.pi / 2), None, ALU.add), SC)
            link(dve.tensor_scalar(an, an, 3.1415925, -3.1415925, ALU.min, ALU.max), SC)
            dve.memset(extra[:, :, 0:1], 0.0).then_inc(sem("setup_dve"), 1)

            def rsqrt(dst, src, bits, t_):
                link(dve.tensor_scalar(bits, src.bitcast(I32), 1, None, ALU.logical_shift_right))
                link(dve.tensor_scalar(bits, bits, -1.0, RSQRT_MAGIC, ALU.mult, ALU.add))
                cur = bits.bitcast(F32)
                for _ in range(4):
                    link(dve.scalar_tensor_tensor(t_, cur, -0.5, cur, ALU.mult, ALU.mult))
                    link(tt(t_, t_, src, ALU.mult))
                    link(dve.scalar_tensor_tensor(dst, t_, 1.5, cur, ALU.add, ALU.mult))
                    cur = dst

            def layernorm(name, l, shift, scale1):
                for t in range(T):
                    dve.bn_stats(stats[:, t, :], x[:, t, :]).then_inc(sem(name + "_stats"), 1)
                for t in range(T):
                    dve.wait_ge(sem(name + "_stats"), t + 1)
                    dve.bn_aggr(mv[:, t, :], stats[:, t, :]).then_inc(sem(name + "_mv"), 1)
                dve.wait_ge(sem(name + "_mv"), T)
                link(dve.tensor_scalar(nvar[:, :], mv[:, :, 1], LN_EPS, None, ALU.add))
                rsqrt(rstd[:, :], nvar[:, :], nbits[:, :], ntmp[:, :])
                for t in range(T):
                    dve.tensor_scalar(h[:, t, :], x[:, t, :], mv[:, t, 0:1], rstd[:, t:t + 1], ALU.subtract, ALU.mult).then_inc(sem(name + "_n"), 1)
                for t in range(T):
                    dve.wait_ge(sem(name + "_n"), t + 1)
                    tt(h[:, t, :], h[:, t, :], mod[:, l, scale1, :], ALU.mult).then_inc(sem(name + "_s"), 1)
                for t in range(T):
                    dve.wait_ge(sem(name + "_s"), t + 1)
                    tt(h[:, t, :], h[:, t, :], mod[:, l, shift, :], ALU.add).then_inc(sem(name + "_h"), 1)

            def residual(c, src, l, gate, done, bias=None):
                if c:
                    dve.wait_ge(sem(done), c)
                tv = tmp[:, :].rearrange("p (t d) -> p t d", t=4)
                sv = src[:, :].rearrange("p (t d) -> p t d", t=4)
                g_ = mod[:, l, gate, :].unsqueeze(1).to_broadcast([P, 4, D])
                if bias is not None:
                    link(tt(tv, sv, bias.unsqueeze(1).to_broadcast([P, 4, D]), ALU.add))
                    link(tt(tv, tv, g_, ALU.mult))
                else:
                    link(tt(tv, sv, g_, ALU.mult))
                xv = x[:, 4 * c:4 * c + 4, :]
                ins = tt(xv, xv, tv, ALU.add)
                ins.then_inc(sem(done), 1)

            def prep_k(hh, s, first):
                for c in range(C):
                    dve.wait_ge(sem("qk_proj"), 2 * hh + c + 1)
                    if not first:
                        dve.wait_ge(sem("st_mm"), NI * (hh - 1))
                    dve.tensor_copy(kT[s][0:HD0, c * HALF:(c + 1) * HALF], bank[6 + c][HD0:P, :]).then_inc(sem("k_evac"), 1)

            def row_max(hh, n):
                t, c, w = MAX_ITEMS[n]
                dve.wait_ge(sem("s_mm"), NI * hh + n + 1)
                dve.reduce_max(part_max[:, t, c:c + 1], bank[n % 2][:, 0:w], AX).then_inc(sem("row_max"), 1)

            def final_max(hh, first):
                dve.wait_ge(sem("row_max"), NI * hh + NI)
                if not first:
                    dve.wait_ge(sem("mrow_mm"), 2 * hh)
                dve.tensor_reduce(neg_max[:, :], part_max[:, :, :], AX, ALU.max, negate=True).then_inc(sem("neg_max"), 1)

            def o_out(hh, c, first):
                dve.wait_ge(sem("pv"), NI * hh + (4 if c == 0 else NI))
                if not first:
                    dve.wait_ge(sem("o_norm"), 2 * hh - 1 + c)
                dve.tensor_copy(o_raw[c][0:HD0 + 1, :], bank[4 + c][0:HD0 + 1, :]).then_inc(sem("o_raw"), 1)

            def o_inv(hh, c):
                dve.wait_ge(sem("den_col"), 2 * hh + c + 1)
                dve.reciprocal(inv_den[:, c, :], bank[4 + c][:, 0:4]).then_inc(sem("inv_den"), 1)

            def o_norm(hh, s, c):
                dve.wait_ge(sem("inv_rows"), 2 * hh + c + 1)
                g_ = (hh - s) // 2
                tt(oT[s * HD0:(s + 1) * HD0, g_, c * HALF:(c + 1) * HALF], o_raw[c][0:HD0, :], bank[4 + c][0:HD0, :], ALU.mult).then_inc(sem("o_norm"), 1)

            def head(hh, s, nxt, first=False):
                for n in range(NI):
                    if nxt and n == 0:
                        prep_k(hh + 1, 1 - s, first)
                    if nxt:
                        for m in MAX_AT.get(n, ()):
                            row_max(hh + 1, m)
                    if n == 4:
                        o_out(hh, 0, first)
                    if n == 6:
                        o_inv(hh, 0)
                    if n == 8:
                        o_norm(hh, s, 0)
                if nxt:
                    final_max(hh + 1, False)
                o_out(hh, 1, first)
                o_inv(hh, 1)
                o_norm(hh, s, 1)

            dve.wait_ge(sem("setup_trig"), 1)
            with dve.Fori(0, B) as b:
                links["dve_chain"] = 0
                for l in range(2):
                    dve.tensor_copy(cond[:, l, :], silu_c[:, l, bass.ds(b, 1)].to_broadcast([P, P])).then_inc(sem("cond"), 1)
                for a in range(2):
                    for hf in range(2):
                        ins = dve.tensor_copy(trig_rep[:, a, :, :, hf * (HD // 2):(hf + 1) * (HD // 2)],
                                              trig[:, a, bass.ds(b, 1), :, :].rearrange("p o c f -> p (o c) f").unsqueeze(2).to_broadcast([P, MC, H, HD // 2]))
                    ins.then_inc(sem("trig_rep"), 1)
                dve.wait_ge(sem("mod_evac"), 4)
                gates = mod[:, :, 2::3, :]
                link(dve.scalar_tensor_tensor(gate_abs.rearrange("p l a d -> p (l a) d"), gates_view(gates), -1.0, gates_view(gates), ALU.mult, ALU.max))
                link(dve.tensor_scalar(gate_abs, gate_abs, 0.25, None, ALU.max))
                link(dve.tensor_scalar(gates, gates, 0.0, 2.0, ALU.is_ge, ALU.mult))
                link(dve.tensor_scalar(gates, gates, -1.0, None, ALU.add))
                link(tt(gates, gates, gate_abs, ALU.mult))
                scales = mod[:, :, 1::3, :]
                link(dve.tensor_scalar(scales, scales, 1.0, None, ALU.add))
                dve.wait_ge(sem("x_in"), 16)
                layernorm("ln_a", 0, 0, 1)
                prep_k(0, 0, True)
                for n in range(NI):
                    row_max(0, n)
                final_max(0, True)
                head(0, 0, True, first=True)
                head(1, 1, True)
                with dve.Fori(1, H // 2 - 1) as g:
                    head(2 * g, 0, True)
                    head(2 * g + 1, 1, True)
                head(H - 2, 0, True)
                head(H - 1, 1, False)
                for c in range(C):
                    dve.wait_ge(sem("attn0_mm"), c + 1)
                    residual(c, bank[c], 0, 2, "res_a")
                dve.wait_ge(sem("res_a"), 2)
                dve.wait_ge(sem("ln_a_tr"), 2)
                layernorm("ln_b", 0, 3, 4)
                dve.wait_ge(sem("w_mm"), 1)
                dve.tensor_scalar(w_col[:, :], bank[0][:, 0:T], router0_b[:, 0:1], None, ALU.add).then_inc(sem("w_col"), 1)
                dve.wait_ge(sem("w_col"), 1)
                link(dve.tensor_copy(extra[:, :, 0], w_col[:, :]))
                link(dve.tensor_copy(extra[:, :, 1], const("row")))
                dve.wait_ge(sem("w_row"), 2)
                link(dve.memset(cnt[:, :, :], 0.0))
                for t in range(T):
                    wt = w_col[:, t:t + 1]
                    if t:
                        link(dve.tensor_scalar(cmp[:, 0:t * P], w_row[:, 0:t * P], wt, None, ALU.is_ge, ALU.add, accum_out=cnt[:, t, 0:1]))
                    link(dve.tensor_scalar(cmp[:, t * P:], w_row[:, t * P:], wt, None, ALU.is_gt, ALU.add, accum_out=cnt[:, t, 1:2]))
                    link(dve.scalar_tensor_tensor(tmp[:, 0:P], w_row[:, t * P:(t + 1) * P], wt, const("lower"), ALU.is_equal, ALU.mult, accum_out=cnt[:, t, 2:3]))
                link(dve.tensor_reduce(rank[:, :], cnt[:, :, :], AX, ALU.add))
                dve.tensor_scalar(sel[:, :], rank[:, :], float(TOPK - 1), None, ALU.is_lt).then_inc(sem("sel"), 1)
                dve.scalar_tensor_tensor(tmp[:, 0:T], rank[:, :], float(TOPK - 1), w_col[:, :], ALU.is_equal, ALU.mult, accum_out=thr_part[:, :]).then_inc(sem("thr_part"), 1)
                dve.wait_ge(sem("thr_mm"), 1)
                link(dve.tensor_copy(thr[:, :], bank[3][:, 0:1]))
                link(dve.tensor_scalar(unpicked[:, :], w_col[:, :], thr[:, 0:1], None, ALU.is_le))
                dve.wait_ge(sem("slot_mm"), 1)
                dve.tensor_copy(slot_of[:, :], bank[4][:, 0:T]).then_inc(sem("slot_of"), 1)
                dve.wait_ge(sem("slot_of"), 1)
                dve.wait_ge(sem("sel"), 1)
                for t in range(T):
                    dve.tensor_scalar(pick[:, t, :], const("slot"), slot_of[:, t:t + 1], sel[:, t:t + 1], ALU.is_equal, ALU.mult).then_inc(sem("pick"), 1)
                dve.wait_ge(sem("gather_mm"), 1)
                dve.tensor_copy(ws_idx[:, :], bank[6][:, 0:2]).then_inc(sem("ws_idx"), 1)
                dve.wait_ge(sem("gather_mm"), 2)
                link(dve.tensor_copy(xs[:, :], bank[5][:, 0:D]))
                dve.wait_ge(sem("idx_tr"), 1)
                dve.tensor_scalar(idx_row[:, :], bank[7][:, 0:SLOTS], float(MS - 1), None, ALU.min).then_inc(sem("idx_row"), 1)
                dve.wait_ge(sem("idx_row"), 1)
                for c in range(MC):
                    dve.tensor_scalar(mask_pick[:, c, :], idx_row[:, :], const("row")[:, c:c + 1], None, ALU.is_equal).then_inc(sem("mask_pick"), 1)

                def rmsnorm(src, n, done):
                    link(dve.scalar_tensor_tensor(hn[:, :], src, 1.0 / D, src, ALU.mult, ALU.mult, accum_out=nvar[:, 0:1]))
                    link(dve.tensor_scalar(nvar[:, 0:1], nvar[:, 0:1], RMS_EPS, None, ALU.add))
                    rsqrt(rstd[:, 0:1], nvar[:, 0:1], nbits[:, 0:1], ntmp[:, 0:1])
                    dve.scalar_tensor_tensor(hn[:, :], src, rstd[:, 0:1], ln_rows[:, n, :], ALU.mult, ALU.mult).then_inc(sem(done), 1)

                rmsnorm(xs[:, :], 0, "hn1")
                dve.wait_ge(sem("mask_sel_mm"), 1)
                dve.tensor_copy(mask_sel[:, :], bank[1][:, 0:SLOTS]).then_inc(sem("mask_sel0"), 1)
                dve.wait_ge(sem("mask_sel0"), 1)
                dve.memset(mask_sel[:, SLOTS - 1:SLOTS], BIG).then_inc(sem("mask_sel"), 1)
                dve.wait_ge(sem("trig_sel"), 1)
                dve.wait_ge(sem("rot0_mm"), 1)
                dve.wait_ge(sem("qk_s"), 1)
                two = [P, 2, SLOTS]
                link(tt(rot_s[:, :, :], bank[7][:, 0:2 * SLOTS].rearrange("p (a s) -> p a s", a=2), trig_sel[:, 1, :].unsqueeze(1).to_broadcast(two), ALU.mult))
                link(tt(qk_s[:, :, :], qk_s[:, :, :], trig_sel[:, 0, :].unsqueeze(1).to_broadcast(two), ALU.mult))
                tt(qk_s[:, :, :], qk_s[:, :, :], rot_s[:, :, :], ALU.add).then_inc(sem("rot_s"), 1)
                dve.wait_ge(sem("rot_s"), 1)
                all_h = [P, H, SLOTS]
                tt(k_diag[:, :, :], qk_s[:, 1, :].unsqueeze(1).to_broadcast(all_h), const("head").unsqueeze(2).to_broadcast(all_h), ALU.mult).then_inc(sem("k_diag"), 1)
                dve.wait_ge(sem("mask_sel"), 1)
                for n in range(4):
                    dve.wait_ge(sem("sc_mm"), n + 1)
                    link(dve.scalar_tensor_tensor(sc[:, 4 * n:4 * n + 4, :], bank[n][:, :].rearrange("p (a s) -> p a s", a=4), SCALE, mask_sel[:, :].unsqueeze(1).to_broadcast([P, 4, SLOTS]), ALU.mult, ALU.add))
                link(dve.reduce_max(sc_max[:, :], sc[:, :, :], AX))
                tt(sc[:, :, :], sc[:, :, :], sc_max[:, :].unsqueeze(2).to_broadcast(all_h), ALU.subtract).then_inc(sem("sc_sub"), 1)
                dve.wait_ge(sem("sc_exp"), 1)
                link(dve.reduce_sum(sc_sum[:, :], sc[:, :, :], AX))
                link(dve.reciprocal(sc_sum[:, :], sc_sum[:, :]))
                dve.wait_ge(sem("o_s_mm"), 1)
                tt(o_s[:, :].rearrange("p (h d) -> p h d", h=H), bank[0][:, 0:D].rearrange("p (h d) -> p h d", h=H), sc_sum[:, :].unsqueeze(2).to_broadcast([P, H, HD]), ALU.mult).then_inc(sem("o_s"), 1)
                dve.wait_ge(sem("wo_mm"), 1)
                link(tt(x1[:, :], xs[:, :], bank[2][:, 0:D], ALU.add))
                dve.wait_ge(sem("hn1_tr"), 1)
                rmsnorm(x1[:, :], 1, "hn2")
                dve.wait_ge(sem("w2_mm"), 1)
                link(tt(x1[:, :], x1[:, :], bank[5][:, 0:D], ALU.add))
                dve.tensor_scalar(proc[:, :], x1[:, :], ws_idx[:, 0:1], None, ALU.mult).then_inc(sem("proc"), 1)
                for c in range(C):
                    hv = h[:, 4 * c:4 * c + 4, :]
                    xv = x[:, 4 * c:4 * c + 4, :]
                    link(tt(hv, hv, unpicked[:, 4 * c:4 * c + 4].unsqueeze(2).to_broadcast([P, 4, D]), ALU.mult))
                    dve.wait_ge(sem("scatter_mm"), c + 1)
                    link(tt(hv, hv, bank[c][:, :].rearrange("p (t d) -> p t d", t=4), ALU.add))
                    link(tt(hv, hv, mod[:, 0, 5, :].unsqueeze(1).to_broadcast([P, 4, D]), ALU.mult))
                    tt(xv, xv, hv, ALU.add).then_inc(sem("res_b"), 1)
                dve.wait_ge(sem("res_b"), 2)
                layernorm("ln_c", 1, 0, 1)
                for n, a in enumerate("qk"):
                    for c in range(C):
                        cols = slice(c * HALF, (c + 1) * HALF)
                        dve.wait_ge(sem("qk1"), 2 * n + c + 1)
                        dve.wait_ge(sem("rot1_mm"), 2 * n + c + 1)
                        tt(rot_f[:, cols], bank[4 + 2 * n + c][:, :], const("sin1")[:, cols], ALU.mult).then_inc(sem("rot1_done"), 1)
                        link(tt(qk_f[:, n, cols], qk_f[:, n, cols], const("cos1")[:, cols], ALU.mult))
                        dve.wait_ge(sem("rot1_done"), 2 * n + c + 1)
                        link(tt(qk_f[:, n, cols], qk_f[:, n, cols], rot_f[:, cols], ALU.add))
                    dve.tensor_copy(split[a]["h"], qk_f[:, n, :]).then_inc(sem("split1"), 1)
                    dve.wait_ge(sem("split1"), 3 * n + 1)
                    link(tt(qk_f[:, n, :], qk_f[:, n, :], split[a]["h"], ALU.subtract))
                    dve.tensor_copy(split[a]["m"], qk_f[:, n, :]).then_inc(sem("split1"), 1)
                    dve.wait_ge(sem("split1"), 3 * n + 2)
                    tt(split[a]["l"], qk_f[:, n, :], split[a]["m"], ALU.subtract).then_inc(sem("split1"), 1)
                dve.wait_ge(sem("v_clear"), 2)
                for c in range(C):
                    dve.wait_ge(sem("v1_mm"), c + 1)
                    tt(v1[:, 4 * c:4 * c + 4, :, 0:HD], bank[c][:, :].rearrange("p (t h d) -> p t h d", t=4, h=H),
                       vo_bias[:, 0, :].rearrange("p (h d) -> p h d", h=H).unsqueeze(1).to_broadcast([P, 4, H, HD]), ALU.add).then_inc(sem("v1"), 1)

                def row_max1(g, n):
                    t, a, c = n // 8, n // 2 % 4, n % 2
                    dve.wait_ge(sem("s1_mm"), 64 * g + n + 1)
                    dve.reduce_max(pmax1[:, a, t, c:c + 1], bank[n % 2][:, :], AX).then_inc(sem("row_max1"), 1)

                def final_max1(g):
                    dve.wait_ge(sem("row_max1"), 64 * g + 64)
                    link(dve.tensor_reduce(nmax1[:, :, :], pmax1[:, :, :, :], AX, ALU.max, negate=True))
                    if g:
                        dve.wait_ge(sem("mrow1_mm"), 8 * g)
                    link(dve.tensor_copy(nmax_hl[:, :, :, 0], nmax1[:, :, :]))
                    tt(nmax_hl[:, :, :, 1], nmax1[:, :, :], nmax_hl[:, :, :, 0], ALU.subtract).then_inc(sem("nmax_hl"), 1)

                def o1_raw(g, c):
                    dve.wait_ge(sem("pv1"), 64 * g + 32 * c + 32)
                    if g:
                        dve.wait_ge(sem("ctx_raw"), 2 * g - 1 + c)
                    dve.tensor_copy(o_raw[c][:, :], bank[4 + c][:, :]).then_inc(sem("o1_raw"), 1)

                def ctx_out(g, c):
                    dve.wait_ge(sem("ctx_raw"), 2 * g + c + 1)
                    bv = bank[6 + c][:, :].rearrange("p (t a e) -> p t a e", t=4, a=GH)
                    link(dve.reciprocal(den1[:, :, :], bv[:, :, :, HD]))
                    tt(ctx1[:, 4 * c:4 * c + 4, GH * HD * g:GH * HD * (g + 1)].rearrange("p t (a d) -> p t a d", a=GH), bv[:, :, :, 0:HD],
                       den1[:, :, :].unsqueeze(3).to_broadcast([P, 4, GH, HD]), ALU.mult).then_inc(sem("ctx1"), 1)

                for n in range(64):
                    row_max1(0, n)
                final_max1(0)
                for g in range(NG):
                    for n in range(64):
                        if g + 1 < NG:
                            row_max1(g + 1, n)
                        if n == 34:
                            o1_raw(g, 0)
                        if n == 38:
                            ctx_out(g, 0)
                    if g + 1 < NG:
                        final_max1(g + 1)
                    o1_raw(g, 1)
                    ctx_out(g, 1)
                for c in range(C):
                    dve.wait_ge(sem("attn1_mm"), c + 1)
                    residual(c, bank[2 + c], 1, 2, "res_c", bias=vo_bias[:, 1, :])
                dve.wait_ge(sem("res_c"), 2)
                layernorm("ln_d", 1, 3, 4)
                te = [P, T, E]

                def over_e(a):
                    return a.unsqueeze(2).to_broadcast(te)

                expert = const("expert").unsqueeze(1).to_broadcast(te)
                dve.wait_ge(sem("lg_mm"), 1)
                link(dve.tensor_copy(lg[:, :, :], bank[0][:, 0:T * E].rearrange("p (t e) -> p t e", t=T)))
                link(dve.reduce_max(m1[:, :], lg[:, :, :], AX))
                tt(lg[:, :, :], lg[:, :, :], over_e(m1[:, :]), ALU.subtract).then_inc(sem("lg_sub"), 1)
                dve.wait_ge(sem("lg_exp"), 1)
                link(dve.reduce_sum(m2[:, :], lg[:, :, :], AX))
                link(dve.reciprocal(m2[:, :], m2[:, :]))
                link(tt(lg[:, :, :], lg[:, :, :], over_e(m2[:, :]), ALU.mult))

                def best(p_, top, oh):
                    link(dve.reduce_max(top, p_, AX))
                    link(tt(oh, p_, over_e(top), ALU.is_equal))
                    link(tt(oh, oh, expert, ALU.mult))
                    link(dve.tensor_reduce(e1[:, :], oh, AX, ALU.min))
                    link(tt(oh, expert, over_e(e1[:, :]), ALU.is_equal))

                best(lg[:, :, :], m1[:, :], oh1[:, :, :])
                link(dve.scalar_tensor_tensor(lg2[:, :, :], oh1[:, :, :], -4.0, lg[:, :, :], ALU.mult, ALU.add))
                best(lg2[:, :, :], m2[:, :], oh2[:, :, :])
                link(tt(e1[:, :], m1[:, :], m2[:, :], ALU.add))
                link(dve.tensor_scalar(e1[:, :], e1[:, :], 1e-6, None, ALU.add))
                link(dve.reciprocal(e1[:, :], e1[:, :]))
                link(tt(nvar[:, :], m1[:, :], m1[:, :], ALU.mult))
                link(tt(ntmp[:, :], m2[:, :], m2[:, :], ALU.mult))
                link(tt(nvar[:, :], nvar[:, :], ntmp[:, :], ALU.add))
                link(tt(bias_tok[:, :], nvar[:, :], e1[:, :], ALU.mult))
                link(tt(m1[:, :], m1[:, :], e1[:, :], ALU.mult))
                link(tt(m2[:, :], m2[:, :], e1[:, :], ALU.mult))
                link(tt(oh1[:, :, :], oh1[:, :, :], over_e(m1[:, :]), ALU.mult))
                link(tt(oh2[:, :, :], oh2[:, :, :], over_e(m2[:, :]), ALU.mult))
                link(tt(coef[:, :, :], oh1[:, :, :], oh2[:, :, :], ALU.add))
                for t in range(T):
                    mt = moe[:, t, :]
                    for e in range(E):
                        dve.wait_ge(sem("ex_mm"), 2 * t + e // 4 + 1)
                        src = bank[2 + (2 * t + e // 4) % 4][:, (e % 4) * D:(e % 4 + 1) * D]
                        if e == 0:
                            ins = dve.tensor_scalar(mt, src, coef[:, t, 0:1], bias_tok[:, t:t + 1], ALU.mult, ALU.add)
                        else:
                            ins = dve.scalar_tensor_tensor(mt, src, coef[:, t, e:e + 1], mt, ALU.mult, ALU.add)
                        if e % 4 == 3:
                            ins.then_inc(sem("moe"), 1)
                            dve.wait_ge(sem("moe"), 2 * t + e // 4 + 1)
                        else:
                            link(ins)
                    link(tt(mt, mt, mod[:, 1, 5, :], ALU.mult))
                    tt(x[:, t, :], x[:, t, :], mt, ALU.add).then_inc(sem("x_final"), 1)
                end_of_batch(dve)


def gates_view(a):
    return a.rearrange("p l a d -> p (l a) d")


_INS = ["L0_attn_x", "L0_attn_w_qkv", "L0_attn_w_out", "L0_ffn_attention_mask", "L0_ffn_position_ids", "L0_ffn_router_w", "L0_ffn_router_b",
        "L0_ffn_wq", "L0_ffn_wk", "L0_ffn_wv", "L0_ffn_wo", "L0_ffn_w1", "L0_ffn_w2", "L0_ffn_ln1", "L0_ffn_ln2", "L0_c", "L0_wmod",
        "L1_attn_Wq", "L1_attn_bq", "L1_attn_Wk", "L1_attn_bk", "L1_attn_Wv", "L1_attn_bv", "L1_attn_Wo", "L1_attn_bo",
        "L1_ffn_router_w", "L1_ffn_expert_weights", "L1_c", "L1_wmod"]


def kernel(**inputs):
    import numpy as _np
    import concourse.bacc as _bacc
    from concourse import mybir as _mybir
    from concourse.bass_utils import run_bass_kernel_spmd as _run

    nc = _bacc.Bacc("TRN2", target_bir_lowering=False, num_devices=1)
    arrays, aps = {}, {}
    for name in _INS:
        a = _np.ascontiguousarray(inputs[name])
        arrays[f"in_{name}"] = a
        aps[name] = nc.dram_tensor(f"in_{name}", a.shape, _mybir.dt.from_np(a.dtype), kind="ExternalInput").ap()
    out = nc.dram_tensor("out_0", (B, S, D), F32, kind="ExternalOutput").ap()
    adaln_kernel(nc, aps, out)
    r = _run(nc, [arrays], core_ids=[0])
    return r.results[0]["out_0"]
```

```python
from contextlib import ExitStack

import numpy as np

import concourse.bass as bass
from concourse import mybir
from concourse.alu_op_type import AluOpType as ALU

ACT = mybir.ActivationFunctionType
AX = mybir.AxisListType.X
F32 = mybir.dt.float32
BF16 = mybir.dt.bfloat16
I32 = mybir.dt.int32

P = 128
D = 128
B = 4
S = 1024
T = S // P
HALF = S // 2
C = 2
H = 16
HD0 = 64
HD = D // H
MS = 512
MC = MS // P
SLOTS = P
TOPK = S // 8
F = 512
FC = F // P
E = 8
GH = 4
NG = H // GH
SCALE0 = HD0 ** -0.5
SCALE = HD ** -0.5
BIG = -1e30
LN_EPS = 1e-5
RMS_EPS = 1e-6
RSQRT_MAGIC = float(0x5F3759DF)
DEN_ROW = HD0
HM = 64
M_ROW = 32
TERMS = [(0, "h", "h"), (8, "h", "m"), (16, "m", "h"), (24, "h", "l"), (40, "m", "m"), (48, "l", "h")]

MAX_ITEMS = [(t, c, min(HALF, (t + 1) * P - c * HALF)) for t in range(T) for c in range(t // 4 + 1)]
EXP_ITEMS = [(c, j, max(0, j * P - c * HALF)) for c in range(C) for j in range(4 * c + 4)]
NI = len(EXP_ITEMS)
assert len(MAX_ITEMS) == NI == 12
MAX_AT = {3: (0, 1), 4: (2, 3), 5: (4, 5), 6: (6,), 7: (7, 8), 8: (9, 10), 9: (11,)}

UNITS = NG * C
UI = 32
NI1 = UNITS * UI
LEAD = 40
ROWS_AT = {UI * (u + 1) - LEAD + 2: u for u in range(UNITS)}
CTX_AT = {UI * (u + 1) + 4: u for u in range(UNITS - 1)}
assert UI + 2 < LEAD < 2 * UI


def max_item1(m):
    u, r = divmod(m, UI)
    return u, 4 * (u % C) + r // 8, GH * (u // C) + r // 2 % GH, r % 2


MAX1_BANK = (0, 1, 5)
ST1_BANK = (2, 3, 7)
ROW_AT = (32, 96, 0, 64)

def exp_item1(m):
    u, r = divmod(m, UI)
    return u, r // GH, GH * (u // C) + r % GH


def shape_constants():
    p = np.arange(P)
    eye = np.eye(P, dtype=np.float32)
    later = (p[None, :] > p[:, None]).astype(np.float32)
    rot0 = np.zeros((P, P), np.float32)
    rot1 = np.zeros((P, P), np.float32)
    for m in range(P):
        d = m % HD
        if d < HD // 2:
            rot0[m + HD // 2, m] = -1.0
        else:
            rot0[m - HD // 2, m] = 1.0
        if d < 6:
            rot1[m + 1 if d % 2 == 0 else m - 1, m] = -1.0 if d % 2 == 0 else 1.0
    tok = np.arange(S)
    frame, rest = tok // 256, tok % 256
    ids = np.stack([frame, rest // 16, rest % 16]).astype(np.float32)
    cos, sin = np.ones((P, S), np.float32), np.zeros((P, S), np.float32)
    for m in range(P):
        if m % HD < 6:
            cos[m], sin[m] = np.cos(ids[m % HD // 2]), np.sin(ids[m % HD // 2])
    parts = {
        "eye": eye,
        "mask_q": later * BIG,
        "mask_k": later.T * BIG,
        "before": later,
        "lower": later.T.copy(),
        "rot0": rot0,
        "rot1": rot1,
        "slot": np.broadcast_to(p.astype(np.float32), (P, P)),
        "tile": np.broadcast_to(P * np.arange(T, dtype=np.float32), (P, T)),
        "row": (p[:, None] + P * np.arange(T)[None, :]).astype(np.float32),
        "head": (p[:, None] // HD == np.arange(H)[None, :]).astype(np.float32),
        "den_sel": np.broadcast_to((np.arange(2 * H - 1) == H - 1).astype(np.float32), (P, 2 * H - 1)),
        "invf": np.broadcast_to((1.0 / np.float32(10000.0) ** (np.arange(0, HD, 2, dtype=np.float32) / HD)).astype(np.float32), (P, HD // 2)),
        "expert": np.broadcast_to(np.arange(E, dtype=np.float32) - E, (P, E)),
        "cos1": cos,
        "sin1": sin,
    }
    pair_rows = np.zeros((P, H // 2, P), np.float32)
    for hh in range(H):
        pair_rows[DEN_ROW + H - 1 - hh, hh // 2, hh % 2 * HD0:(hh % 2 + 1) * HD0] = 1.0
    at, n = {}, 0
    for name, a in parts.items():
        at[name] = (n, n + a.shape[1])
        n += a.shape[1]
    return at, np.concatenate(list(parts.values()), axis=1).astype(np.float32), pair_rows


def adaln_kernel(nc, i, out):
    CONST_AT, const_values, pair_values = shape_constants()
    const_dram = nc.inline_tensor(const_values, "shape_constants")
    pair_dram = nc.inline_tensor(pair_values, "pair_rows")

    with ExitStack() as ctx:
        def sb(name, shape, dt=F32):
            return ctx.enter_context(nc.sbuf_tensor(name, shape, dt))

        consts = sb("consts", [P, const_values.shape[1]])

        def const(name):
            a, z = CONST_AT[name]
            return consts[:, a:z]

        eye = const("eye")
        eye_bf = sb("eye_bf", [P, P], BF16)
        mask_q = sb("mask_q_bf", [P, P], BF16)
        mask_k = sb("mask_k_bf", [P, P], BF16)
        ones = sb("ones", [P, P])
        silu_c = sb("silu_c", [P, 2, B])
        c_raw = sb("c_raw", [P, 2, B])
        c_den = sb("c_den", [P, 2, B])
        wmod = sb("wmod", [P, 2, 6 * D])
        w_out0 = sb("w_out0", [P, H // 2, D])
        router0 = sb("router0", [P, 1])
        router0_rep = sb("router0_rep", [P, P])
        router0_b = sb("router0_b", [P, 1])
        ln_rows = sb("ln_rows", [P, 2, D])
        ffn_w = sb("ffn_w", [P, 4, D])
        w1 = sb("w1", [P, F])
        w2 = sb("w2", [P, FC, D])
        attn_w = sb("attn_w", [P, 4, D])
        qk_bias = sb("qk_bias", [P, 2])
        vo_bias = sb("vo_bias", [P, 2, D])
        router1 = sb("router1", [P, E])
        experts = sb("experts", [P, E, D])
        pos_int = sb("pos_int", [P, B * MC], I32)
        pos_f = sb("pos_f", [P, B * MC])
        angle = sb("angle", [P, 2, B * MC, HD // 2])
        turns = sb("turns", [P, 2, B * MC, HD // 2])
        trig = sb("trig", [P, 2, B, MC, HD // 2])

        x = sb("x", [P, T, D])
        h_room = sb("h", [P, T, D + 2])
        h, extra = h_room[:, :, 0:D], h_room[:, :, D:D + 2]
        hT = sb("hT", [P, S])
        mod = sb("mod", [P, 2, 6, D])
        mod_col = sb("mod_col", [P, 2, 6, B])
        stats = sb("stats", [P, T, 6])
        mv = sb("mv", [P, T, 2])
        nvar = sb("nvar", [P, T])
        nbits = sb("nbits", [P, T], I32)
        ntmp = sb("ntmp", [P, T])
        rstd = sb("rstd", [P, T])
        tmp = sb("tmp", [P, HALF])
        gate_abs = tmp[:, :].rearrange("p (l a d) -> p l a d", l=2, a=2)

        w_qk = [sb(f"w_qk{s}", [P, 2 * HD0]) for s in range(2)]
        w_v = [sb(f"w_v{q}", [P, 2 * HD0]) for q in range(2)]
        qT = [sb(f"qT{s}", [P, S]) for s in range(2)]
        kT = [sb(f"kT{s}", [P, S]) for s in range(2)]
        q_bf = sb("q_bf", [P, S], BF16)
        k_bf = sb("k_bf", [P, S], BF16)
        v0 = [sb(f"v0{q}", [P, T, 2 * HD0]) for q in range(2)]
        part_max = sb("part_max", [P, T, C])
        neg_max = sb("neg_max", [P, T])
        probs_room = sb("probs", [P, 4, HALF])
        probs = [probs_room[:, n, :] for n in range(4)]
        o_raw = [sb(f"o_raw{c}", [P, HALF]) for c in range(C)]
        den_sel = [sb(f"den_sel{s}", [P, H]) for s in range(2)]
        inv_den = o_raw
        room = sb("room", [P, 8 * S])
        oT = room[:, :].rearrange("p (g s) -> p g s", s=S)
        cond = room[:, 0:2 * P].rearrange("p (l s) -> p l s", l=2)

        w_col = sb("w_col", [P, T])
        w_row = sb("w_row", [P, S])
        larger = [room[:, 4 * S:8 * S].bitcast(BF16)[:, t * S:t * S + (T - t) * P] for t in range(T)]
        cnt = sb("cnt", [P, T, 2])
        ones_bf = sb("ones_bf", [P, P], BF16)
        before_bf = sb("before_bf", [P, P], BF16)
        sel_bf = sb("sel_bf", [P, T], BF16)
        rank = sb("rank", [P, T])
        sel = sb("sel", [P, T])
        thr_part = sb("thr_part", [P, 1])
        thr = sb("thr", [P, 1])
        unpicked = sb("unpicked", [P, T])
        slot_of = sb("slot_of", [P, T])
        pick = sb("pick", [P, T, SLOTS])
        pickT = sb("pickT", [P, S])
        ties = pick
        pair_rows = pick
        xs = sb("xs", [P, D])
        ws_idx = sb("ws_idx", [P, 2])
        idx_row = sb("idx_row", [P, SLOTS])
        mask_pick = sb("mask_pick", [P, MC, SLOTS])
        mask_in = sb("mask_in", [P, MC, MS])
        mask_rows = sb("mask_rows", [P, MC, SLOTS])
        mask_sel = sb("mask_sel", [P, SLOTS])
        trig_rep = sb("trig_rep", [P, 2, MC, H, HD // 2 * 2])
        trig_sel = sb("trig_sel", [P, 2, SLOTS])
        hn = sb("hn", [P, D])
        hnT = sb("hnT", [P, SLOTS])
        qk_s = sb("qk_s", [P, 2, SLOTS])
        rot_s = sb("rot_s", [P, 2, SLOTS])
        v_s = sb("v_s", [P, D])
        k_diag = room[:, 4 * S:6 * S].rearrange("p (h s) -> p h s", h=H)
        sc = room[:, 6 * S:8 * S].rearrange("p (h s) -> p h s", h=H)
        sc_max = sb("sc_max", [P, H])
        sc_sum = sb("sc_sum", [P, H])
        pT = probs_room[:, :, :].rearrange("p n (a s) -> p (n a) s", a=4)
        o_s = sb("o_s", [P, D])
        o_sT = sb("o_sT", [P, SLOTS])
        x1 = sb("x1", [P, D])
        gelu = sb("gelu", [P, FC, SLOTS])
        proc = sb("proc", [P, D])

        qk_f = room[:, 4 * S:6 * S].rearrange("p (a s) -> p a s", a=2)
        rot_f = w_row
        sc_room = room[:, 6 * S:8 * S].bitcast(BF16).rearrange("p (n s) -> p n s", s=S)
        pT_room = probs_room[:, :, :].rearrange("p n s -> p (n s)").bitcast(BF16).rearrange("p (n s) -> p n s", s=S)
        split = {"q": {n: sc_room[:, m, :] for m, n in enumerate("hml")}, "k": {n: pT_room[:, m, :] for m, n in enumerate("hml")}}
        ring1 = probs + [mask_in[:, n, :] for n in range(4)]
        q_stack = sb("q_stack", [P, H, S], BF16)
        k_stack = room[:, 0:4 * S].bitcast(BF16).rearrange("p (g s) -> p g s", s=S)
        v1 = room[:, 4 * S:8 * S].rearrange("p (t h c) -> p t h c", t=T, h=H)
        pmax1 = sb("pmax1", [P, GH, T, C])
        nmax1 = sb("nmax1", [P, GH, T])
        nmax_hl = sb("nmax_hl", [P, GH, T, 2], BF16)
        den1 = sb("den1", [P, 4, GH])
        ctx1 = pick
        ctxT = pickT

        lg = sb("lg", [P, T, E])
        m1 = sb("m1", [P, T])
        m2 = sb("m2", [P, T])
        e1 = sb("e1", [P, T])
        oh1 = sb("oh1", [P, T, E])
        oh2 = sb("oh2", [P, T, E])
        lg2 = sb("lg2", [P, T, E])
        coef = sb("coef", [P, T, E])
        bias_tok = sb("bias_tok", [P, T])
        prod = room[:, 0:4 * S].rearrange("p (n e d) -> p n e d", n=4, e=E)
        moe = w_row[:, :].rearrange("p (t d) -> p t d", t=T)

        bank = [ctx.enter_context(nc.psum_tensor(f"bank{n}", [P, HALF], F32)) for n in range(8)]

        scratch = {a: {n: nc.dram_tensor(f"scratch_{a}{n}", [P, S], BF16).ap() for n in "hml"} for a in "qk"}

        ONCE = ("setup_loads setup_masks setup_pool setup_dve setup_c_exp setup_trig setup_chain setup_mod_mm "
                "batch_arrived batch_shares batch_cleared batch_left").split()
        PER_BATCH = """
                 attn0_mm attn1_mm cast_go cond ctx1 ctxT ctx_raw ctx_tr den_sel den_zero dve_chain ex_mm expd expd1 gather_mm gelu hn
                 hnT hn_tr idx_row idx_tr inv_den inv_rows k_clear k_diag larger not_before k_evac kb_cast lg_exp lg_mm lg_sub
                 mask_in mask_pick mask_rows mask_sel mod_evac mod_mm moe mrow1 mrow1_mm
                 mrow_evac mrow_mm neg_max nmax_hl o1_raw o_norm o_out o_s o_sT o_s_mm o_s_tr pT p_tr pair_rows pick pickT pickT_tr proc
                 pv pv1 q_evac qb_cast qk1 qk1_mm qk_proj qk_s qkv_s_mm res_a res_b res_c rot0_mm rot1_done rot1_mm rope1 rest1 rot_s
                 row_max row_max1 s1_mm s_mm sc_exp sc_mm sc_sub scatter_mm sel slot_mm slot_of split_h split_m split_l
                 st1_mm st_mm stack_clear stacks stored thr_part select_mm trig_rep trig_sel v1 v1_mm v_clear v_evac
                 v_proj v_s w1_mm w2_mm w_col w_head0 w_head1 w_pair0 w_pair1 w_mm w_row wo_mm coef prod ws_idx x_final x_in
        """.split() + [f"scratch_{a}{part}" for a in "qk" for part in "hml"] + [f"ln_{a}_{b_}" for a in "abcd" for b_ in ("stats", "h", "tr", "hT")]
        sems = {name: ctx.enter_context(nc.semaphore(name)) for name in ONCE + PER_BATCH}

        def sem(name):
            return sems[name]

        arrived, cleared, left = sem("batch_arrived"), sem("batch_cleared"), sem("batch_left")

        SETUP_LOADS = []

        ENGINES = 5

        def clear_share(eng, k):
            eng.drain().then_inc(arrived, 1)
            eng.wait_ge(arrived, ENGINES)
            for name in PER_BATCH[k::ENGINES]:
                eng.sem_clear(sem(name))
            eng.sem_inc(sem("batch_shares"), 1)

        def end_of_batch(eng, k):
            clear_share(eng, k)
            eng.wait_ge(cleared, 1)
            eng.sem_inc(left, 1)

        def to_stack(eng, n):
            a = "qk"[n]

            def write(part):
                eng.wait_ge(sem("split_" + part), C * (n + 1))
                eng.dma_start(scratch[a][part], split[a][part]).then_inc(sem(f"scratch_{a}{part}"), 16)

            def spread(part):
                eng.wait_ge(sem(f"scratch_{a}{part}"), 16)
                for row, *parts in TERMS:
                    if parts[n] == part:
                        src = scratch[a][part].rearrange("(g a d) t -> a d g t", a=2, d=HD)
                        for par in range(2):
                            rows = slice(par * HM + row, par * HM + row + HD)
                            dst = q_stack[rows, par::2, :] if a == "q" else k_stack[rows, :, :]
                            eng.dma_start(dst, src[par]).then_inc(sem("stacks"), 16)

            write("h")
            write("m")
            if a == "q":
                eng.wait_ge(sem("stack_clear"), 4)
            else:
                eng.wait_ge(sem("k_clear"), 3)
                write("l")
            spread("h")
            if a == "q":
                write("l")
            spread("m")
            spread("l")

        block = ctx.enter_context(nc.Block())

        @block.sync
        def _(sp):
            def load(dst, src, s="setup_loads"):
                sp.dma_start(dst, src, allow_slow_non_contiguous=True).then_inc(sem(s), 16)
                SETUP_LOADS.append(1)

            load(consts[:, :], const_dram[:])
            for l in range(2):
                load(wmod[:, l, :], i[f"L{l}_wmod"])
                load(c_raw[:, l, :], i[f"L{l}_c"].rearrange("b d -> d b"))
            load(pos_int[:, :], i["L0_ffn_position_ids"].rearrange("b (c p) -> p (b c)", p=P))
            load(w_out0[:, :, :], i["L0_attn_w_out"].rearrange("(g a) d e -> (a d) g e", a=2))
            load(router0[:, :], i["L0_ffn_router_w"])
            load(router0_b[:, :], i["L0_ffn_router_b"].rearrange("(a n) -> a n", a=1).broadcast_to([P, 1]))
            for n, name in enumerate(["L0_ffn_ln1", "L0_ffn_ln2"]):
                load(ln_rows[:, n, :], i[name].rearrange("(a n) -> a n", a=1).broadcast_to([P, D]))
            for n, name in enumerate(["L0_ffn_wq", "L0_ffn_wk", "L0_ffn_wv", "L0_ffn_wo"]):
                load(ffn_w[:, n, :], i[name])
            load(w1[:, :], i["L0_ffn_w1"])
            load(w2[:, :, :], i["L0_ffn_w2"].rearrange("(c p) n -> p c n", p=P))
            for n, name in enumerate(["L1_attn_Wq", "L1_attn_Wk", "L1_attn_Wv", "L1_attn_Wo"]):
                load(attn_w[:, n, :], i[name])
            for n, name in enumerate(["L1_attn_bq", "L1_attn_bk"]):
                load(qk_bias[:, n:n + 1], i[name].rearrange("(p a) -> p a", a=1))
            for n, name in enumerate(["L1_attn_bv", "L1_attn_bo"]):
                load(vo_bias[:, n, :], i[name].rearrange("(a n) -> a n", a=1).broadcast_to([P, D]))
            load(router1[:, :], i["L1_ffn_router_w"].rearrange("e d -> d e"))
            load(experts[:, :, :], i["L1_ffn_expert_weights"].rearrange("e h o -> h e o"))

            w_heads = i["L0_attn_w_qkv"].rearrange("e h n -> h e n")
            w_pairs = i["L0_attn_w_qkv"].rearrange("e (p h) n -> p e h n", h=2)

            def load_qk_weights(hh, s, first):
                if not first:
                    sp.wait_ge(sem("qk_proj"), 2 * hh - 2)
                sp.dma_start(w_qk[s][:, :], w_heads[hh, :, 0:2 * HD0]).then_inc(sem(f"w_head{s}"), 16)

            def load_v_weights(p, q, first):
                if not first:
                    sp.wait_ge(sem("v_proj"), 2 * p - 2)
                sp.dma_start(w_v[q][:, :].rearrange("e (h d) -> e h d", h=2), w_pairs[p, :, :, 2 * HD0:]).then_inc(sem(f"w_pair{q}"), 16)

            with sp.Fori(0, B) as b:
                sp.dma_start(x[:, :, :], i["L0_attn_x"][b, :, :].rearrange("(t p) d -> p t d", p=P)).then_inc(sem("x_in"), 16)
                sp.dma_start(pair_rows[:, :, :], pair_dram[:]).then_inc(sem("pair_rows"), 16)
                for s in range(2):
                    load_qk_weights(s, s, True)
                    load_v_weights(s, s, True)
                sp.dma_start(mask_in[:, :, :], i["L0_ffn_attention_mask"][b, 0, :, :].rearrange("(c p) n -> p c n", p=P)).then_inc(sem("mask_in"), 16)
                with sp.Fori(0, H // 4 - 1) as g:
                    for q in range(2):
                        for s in range(2):
                            load_qk_weights(4 * g + 2 + 2 * q + s, s, False)
                        load_v_weights(2 * g + 2 + q, q, False)
                for s in range(2):
                    load_qk_weights(H - 2 + s, s, False)
                to_stack(sp, 0)
                for r in range(T // 2):
                    sp.wait_ge(sem("x_final"), r + 1)
                    sp.dma_start(out[b, 2 * r * P:2 * (r + 1) * P, :].rearrange("(k p) d -> p k d", p=P), x[:, 2 * r:2 * r + 2, :]).then_inc(sem("stored"), 16)
                sp.wait_ge(sem("stored"), 16 * (T // 2))
                end_of_batch(sp, 1)

        N_SETUP_LOADS = 16 * len(SETUP_LOADS)

        @block.gpsimd
        def _(pool):
            def set_once(count, ap, value):
                if count:
                    pool.wait_ge(sem("setup_pool"), count)
                pool.memset(ap, value).then_inc(sem("setup_pool"), 1)

            fills = [(ones[:, :], 1.0)]
            for s in range(2):
                fills += [(qT[s][HD0:P, :], 0.0), (kT[s][HD0:P, :], 0.0), (kT[s][HD0:HD0 + 1, :], 1.0)]
            fills += [(q_bf[HD0:P, :], 0.0), (k_bf[HD0:P, :], 0.0), (part_max[:, 0:4, 1:2], -3e38),
                      (q_stack[:, :, :].rearrange("p h s -> p (h s)").bitcast(F32), 0.0)]
            for count, (ap, value) in enumerate(fills):
                set_once(count, ap, value)
            pool.wait_ge(sem("setup_pool"), len(fills))

            def cast_head(hh, s):
                for c in range(C):
                    cols = slice(c * HALF, (c + 1) * HALF)
                    pool.wait_ge(sem("s_mm"), NI * hh)
                    pool.wait_ge(sem("q_evac"), 2 * hh + c + 1)
                    pool.sem_inc(sem("cast_go"), 1)
                    pool.tensor_copy(q_bf[0:HD0, cols], qT[s][0:HD0, cols]).then_inc(sem("qb_cast"), 1)
                    pool.wait_ge(sem("k_evac"), 2 * hh + c + 1)
                    pool.sem_inc(sem("cast_go"), 1)
                    pool.tensor_copy(k_bf[0:HD0, cols], kT[s][0:HD0, cols]).then_inc(sem("kb_cast"), 1)

            with pool.Fori(0, B) as b:
                with pool.Fori(0, H // 2 - 1) as g:
                    cast_head(2 * g + 1, 1)
                    cast_head(2 * g + 2, 0)
                cast_head(H - 1, 1)
                pool.wait_ge(sem("kb_cast"), 2 * H)
                for par in range(2):
                    for hf in range(2):
                        rows = slice(par * HM + M_ROW, par * HM + M_ROW + 2)
                        heads = slice(par + 8 * hf, par + 8 * hf + 7, 2)
                        if par + hf:
                            pool.wait_ge(sem("stack_clear"), 2 * par + hf)
                        pool.memset(q_stack[rows, heads, :], 0.0).then_inc(sem("stack_clear"), 1)
                pool.wait_ge(sem("stack_clear"), 4)
                pool.wait_ge(sem("attn0_mm"), 2)
                pool.memset(room[:, 0:4 * S], 0.0).then_inc(sem("k_clear"), 1)
                for par in range(2):
                    pool.wait_ge(sem("k_clear"), par + 1)
                    pool.memset(k_stack[par * HM + M_ROW:par * HM + M_ROW + 2, :, :], 1.0).then_inc(sem("k_clear"), 1)
                pool.wait_ge(sem("k_clear"), 3)
                for a in "qk":
                    for part in "hml":
                        pool.wait_ge(sem(f"scratch_{a}{part}"), 16)
                pool.memset(room[:, 4 * S:8 * S], 0.0).then_inc(sem("v_clear"), 1)
                pool.wait_ge(sem("v_clear"), 1)
                pool.memset(v1[:, :, :, HD:HD + 1], 1.0).then_inc(sem("v_clear"), 1)
                pool.wait_ge(sem("v_clear"), 2)
                clear_share(pool, 0)
                pool.wait_ge(sem("batch_shares"), ENGINES)
                pool.sem_clear(arrived)
                pool.sem_clear(sem("batch_shares"))
                pool.drain()
                pool.sem_inc(cleared, 1)
                pool.wait_ge(left, 4)
                pool.sem_clear(left)
                pool.sem_clear(cleared)

        @block.scalar
        def _(act):
            act.wait_ge(sem("setup_loads"), N_SETUP_LOADS)
            act.activation(c_den[:, :, :], c_raw[:, :, :], ACT.Exp, scale=-1.0).then_inc(sem("setup_c_exp"), 1)
            act.wait_ge(sem("setup_dve"), 1)
            act.activation(trig[:, :, :, :, :].rearrange("p a b c f -> p (a b c f)"), angle[:, :, :, :].rearrange("p a n f -> p (a n f)"), ACT.Sin).then_inc(sem("setup_trig"), 1)

            def copy(dst, src):
                return act.activation(dst, src, ACT.Copy)

            def evac_hT(name, b, l, shift, scale1):
                for c in range(C):
                    act.wait_ge(sem(name + "_tr"), c + 1)
                    act.activation(hT[:, c * HALF:(c + 1) * HALF], bank[6 + c][:, :], ACT.Identity,
                                   bias=mod_col[:, l, shift, bass.ds(b, 1)], scale=mod_col[:, l, scale1, bass.ds(b, 1)]).then_inc(sem(name + "_hT"), 1)

            def prep_early(hh, s, first):
                for c in range(C):
                    act.wait_ge(sem("qk_proj"), 2 * hh + c + 1)
                    if not first:
                        act.wait_ge(sem("st_mm"), NI * (hh - 1))
                    elif hh == 0:
                        copy(q_bf[0:HD0, c * HALF:(c + 1) * HALF], bank[6 + c][0:HD0, :]).then_inc(sem("qb_cast"), 1)
                    copy(qT[s][0:HD0, c * HALF:(c + 1) * HALF], bank[6 + c][0:HD0, :]).then_inc(sem("q_evac"), 1)

            def prep_v(p, q, c):
                act.wait_ge(sem("v_proj"), 2 * p + c + 1)
                if not (isinstance(p, int) and p < 2):
                    act.wait_ge(sem("pv"), 2 * NI * (p - 1))
                copy(v0[q][:, 4 * c:4 * c + 4, :], bank[6 + c][:, :].rearrange("p (t d) -> p t d", t=4)).then_inc(sem("v_evac"), 1)

            def prep_max(hh, s, c):
                act.wait_ge(sem("mrow_mm"), 2 * hh + c + 1)
                copy(qT[s][HD0:HD0 + 1, c * HALF:(c + 1) * HALF], bank[6 + c][HD0:HD0 + 1, :]).then_inc(sem("mrow_evac"), 1)

            def exps(hh, s, p, q, nxt, first=False):
                for n, (c, j, lo) in enumerate(EXP_ITEMS):
                    act.wait_ge(sem("st_mm"), NI * hh + n + 1)
                    if not (first and n < 4):
                        act.wait_ge(sem("pv"), NI * hh + n - 3)
                    act.activation(probs[n % 4][:, 0:HALF - lo], bank[2 + n % 2][:, lo:HALF], ACT.Exp, scale=SCALE0).then_inc(sem("expd"), 1)
                    if n == 0 and not first:
                        prep_max(hh, s, 1)
                    if nxt:
                        if n == 0:
                            prep_early(hh + 1, 1 - s, first)
                        if s == 1 and n in (2, 3):
                            prep_v(p + 1, 1 - q, n - 2)
                        if n == 10:
                            prep_max(hh + 1, 1 - s, 0)

            with act.Fori(0, B) as b:
                evac_hT("ln_a", b, 0, 0, 1)
                for l in range(2):
                    for a in range(2):
                        act.wait_ge(sem("mod_mm"), 2 * l + a + 1)
                        copy(mod[:, l, 3 * a:3 * a + 3, :].rearrange("p a d -> p (a d)"), bank[2 * l + a][:, 0:3 * D]).then_inc(sem("mod_evac"), 1)
                prep_early(0, 0, True)
                for c in range(C):
                    prep_v(0, 0, c)
                for c in range(C):
                    prep_max(0, 0, c)
                exps(0, 0, 0, 0, True, first=True)
                exps(1, 1, 0, 0, True)
                with act.Fori(0, H // 4 - 1) as g:
                    for q in range(2):
                        for s in range(2):
                            exps(4 * g + 2 + 2 * q + s, s, 2 * g + 1 + q, 1 - q, True)
                exps(H - 2, 0, H // 2 - 1, 1, True)
                exps(H - 1, 1, H // 2 - 1, 1, False)
                evac_hT("ln_b", b, 0, 3, 4)
                for c in range(C):
                    act.wait_ge(sem("w_mm"), c + 1)
                    act.activation(w_row[:, c * HALF:(c + 1) * HALF], bank[1 + c][:, :], ACT.Identity, bias=router0_b[:, 0:1]).then_inc(sem("w_row"), 1)
                for c in range(C):
                    act.wait_ge(sem("pickT_tr"), c + 1)
                    copy(pickT[:, c * HALF:(c + 1) * HALF], bank[1 + c][:, :]).then_inc(sem("pickT"), 1)
                act.wait_ge(sem("select_mm"), 1)
                copy(mask_rows[:, :, :], bank[0][:, :].rearrange("p (c s) -> p c s", c=MC)).then_inc(sem("mask_rows"), 1)
                act.wait_ge(sem("hn_tr"), 1)
                copy(hnT[:, :], bank[4][:, 0:SLOTS]).then_inc(sem("hnT"), 1)
                act.wait_ge(sem("select_mm"), 2)
                copy(trig_sel[:, :, :], bank[2][:, 0:2 * SLOTS].rearrange("p (a s) -> p a s", a=2)).then_inc(sem("trig_sel"), 1)
                act.wait_ge(sem("qkv_s_mm"), 1)
                copy(qk_s[:, :, :], bank[5][:, 0:2 * SLOTS].rearrange("p (a s) -> p a s", a=2)).then_inc(sem("qk_s"), 1)
                act.wait_ge(sem("qkv_s_mm"), 2)
                copy(v_s[:, :], bank[6][:, 0:D]).then_inc(sem("v_s"), 1)
                for n in range(5):
                    if n < 4:
                        act.wait_ge(sem("sc_sub"), n + 1)
                        act.activation(sc[:, 4 * n:4 * n + 4, :], sc[:, 4 * n:4 * n + 4, :], ACT.Exp).then_inc(sem("sc_exp"), 1)
                    if n:
                        act.wait_ge(sem("p_tr"), n)
                        copy(pT[:, 4 * n - 4:4 * n, :], bank[3 + n][:, :].rearrange("p (a s) -> p a s", a=4)).then_inc(sem("pT"), 1)
                act.wait_ge(sem("o_s_tr"), 1)
                copy(o_sT[:, :], bank[1][:, 0:SLOTS]).then_inc(sem("o_sT"), 1)
                act.wait_ge(sem("hn_tr"), 2)
                copy(hnT[:, :], bank[3][:, 0:SLOTS]).then_inc(sem("hnT"), 1)
                act.wait_ge(sem("w1_mm"), 1)
                act.activation(gelu[:, :, :], bank[4][:, :].rearrange("p (c s) -> p c s", c=FC), ACT.Gelu_apprx_tanh).then_inc(sem("gelu"), 1)
                evac_hT("ln_c", b, 1, 0, 1)
                for n in range(2):
                    for c in range(C):
                        act.wait_ge(sem("qk1_mm"), 2 * n + c + 1)
                        act.activation(qk_f[:, n, c * HALF:(c + 1) * HALF], bank[2 * n + c][:, :], ACT.Identity, bias=qk_bias[:, n:n + 1]).then_inc(sem("qk1"), 1)

                for k in range(5):
                    for part, m in (("h", k), ("m", k - 1)):
                        if 0 <= m < 4:
                            n, c = divmod(m, C)
                            act.wait_ge(sem("rope1" if part == "h" else "rest1"), m + 1)
                            copy(split["qk"[n]][part][:, c * HALF:(c + 1) * HALF], qk_f[:, n, c * HALF:(c + 1) * HALF]).then_inc(sem("split_" + part), 1)

                to_stack(act, 1)

                def max_row(u, a):
                    r = (a % 2) * HM + M_ROW
                    act.wait_ge(sem("mrow1_mm"), GH * u + a + 1)
                    copy(q_stack[r:r + 2, GH * (u // C) + a, (u % C) * HALF:(u % C + 1) * HALF], bank[6][ROW_AT[a]:ROW_AT[a] + 2, :]).then_inc(sem("mrow1"), 1)

                for n in range(-UI, NI1):
                    if n >= 0:
                        act.wait_ge(sem("st1_mm"), n + 1)
                        if n >= 8:
                            act.wait_ge(sem("pv1"), n // GH - 1)
                        act.activation(ring1[n % 8][:, :], bank[ST1_BANK[n % 3]][:, :], ACT.Exp, scale=SCALE).then_inc(sem("expd1"), 1)
                    for a in range(GH):
                        if n - 1 - a in ROWS_AT:
                            max_row(ROWS_AT[n - 1 - a], a)
                for c in range(C):
                    act.wait_ge(sem("ctx_tr"), c + 1)
                    copy(ctxT[:, c * HALF:(c + 1) * HALF], bank[c][:, :]).then_inc(sem("ctxT"), 1)
                evac_hT("ln_d", b, 1, 3, 4)
                act.wait_ge(sem("lg_sub"), 1)
                act.activation(lg[:, :, :], lg[:, :, :], ACT.Exp).then_inc(sem("lg_exp"), 1)
                act.wait_ge(sem("coef"), 2)
                for t in range(T):
                    if t >= 4:
                        act.wait_ge(sem("moe"), t - 3)
                    for e in range(E):
                        if e % 4 == 0:
                            act.wait_ge(sem("ex_mm"), 2 * t + e // 4 + 1)
                        src = bank[(2 * t + 4) % 8 + e // 4][:, (e % 4) * D:(e % 4 + 1) * D]
                        bias = bias_tok[:, t:t + 1] if e == 0 else 0.0
                        act.activation(prod[:, t % 4, e, :], src, ACT.Identity, bias=bias, scale=coef[:, t, e:e + 1]).then_inc(sem("prod"), 1)
                end_of_batch(act, 2)

        @block.tensor
        def _(pe):
            def mm(dst, lhsT, rhs, start=True, stop=True):
                return pe.matmul(dst, lhsT, rhs, start=start, stop=stop)

            pe.wait_ge(sem("setup_pool"), 11)
            pe.wait_ge(sem("setup_dve"), 1)
            pe.wait_ge(sem("setup_masks"), 6)
            for l in range(2):
                for a in range(6):
                    last = mm(bank[0][:, (6 * l + a) * B:(6 * l + a + 1) * B], wmod[:, l, a * D:(a + 1) * D], silu_c[:, l, :])
            last.then_inc(sem("setup_mod_mm"), 1)

            def transpose_h(name):
                for c in range(C):
                    for t in range(4 * c, 4 * c + 4):
                        pe.wait_ge(sem(name + "_h"), t + 1)
                        last = pe.transpose(bank[6 + c][:, (t % 4) * P:(t % 4 + 1) * P], h[:, t, :], eye)
                    last.then_inc(sem(name + "_tr"), 1)

            def project(hh, s, first):
                pe.wait_ge(sem(f"w_head{s}"), 16 * (hh // 2 + 1) if isinstance(hh, int) else 16 * w_round(hh, s))
                for c in range(C):
                    if not first:
                        pe.wait_ge(sem("mrow_evac"), 2 * hh - 1 + c)
                    mm(bank[6 + c][:, :], w_qk[s][:, :], hT[:, c * HALF:(c + 1) * HALF]).then_inc(sem("qk_proj"), 1)

            def w_round(hh, s):
                return (hh - s) // 2 + 1

            def project_v(hh, p, q, c):
                pe.wait_ge(sem(f"w_pair{q}"), 16 * ((p - q) // 2 + 1))
                pe.wait_ge(sem("q_evac"), 2 * hh + c + 1)
                pe.wait_ge(sem("k_evac"), 2 * hh + c + 1)
                for t in range(4 * c, 4 * c + 4):
                    last = mm(bank[6 + c][:, (t % 4) * P:(t % 4 + 1) * P], hT[:, t * P:(t + 1) * P], w_v[q][:, :])
                last.then_inc(sem("v_proj"), 1)

            def max_item(hh, n, first):
                t, c, w = MAX_ITEMS[n]
                dst = bank[n % 2]
                pe.wait_ge(sem("qb_cast"), 2 * hh + t // 4 + 1)
                pe.wait_ge(sem("kb_cast"), 2 * hh + c + 1)
                if not (first and n < 2):
                    pe.wait_ge(sem("row_max"), NI * hh + n - 1)
                diag = c == t // 4
                last = mm(dst[:, 0:w], q_bf[:, t * P:(t + 1) * P], k_bf[:, c * HALF:c * HALF + w], stop=not diag)
                if diag:
                    last = mm(dst[:, w - P:w], eye_bf[:, :], mask_q[:, :], start=False)
                last.then_inc(sem("s_mm"), 1)

            def max_to_row(hh, p):
                pe.wait_ge(sem("neg_max"), hh + 1)
                pe.wait_ge(sem("v_evac"), 2 * p + 2)
                pe.wait_ge(sem("q_evac"), 2 * hh + 2)
                pe.wait_ge(sem("k_evac"), 2 * hh + 2)
                for c in range(C):
                    for t in range(4):
                        last = mm(bank[6 + c][HD0:HD0 + 1, t * P:(t + 1) * P], neg_max[:, 4 * c + t:4 * c + t + 1], eye)
                    last.then_inc(sem("mrow_mm"), 1)

            def st_item(hh, s, n, first):
                c, j, lo = EXP_ITEMS[n]
                dst = bank[2 + n % 2]
                if first and n == 0:
                    pe.wait_ge(sem("mod_evac"), 4)
                if j == 0:
                    pe.wait_ge(sem("mrow_evac"), 2 * hh + c + 1)
                if not (first and n < 2):
                    pe.wait_ge(sem("expd"), NI * hh + n - 1)
                diag = j * P >= c * HALF
                last = mm(dst[:, lo:], kT[s][:, j * P:(j + 1) * P], qT[s][:, c * HALF + lo:(c + 1) * HALF], stop=not diag)
                if diag:
                    last = mm(dst[:, lo:lo + P], eye_bf[:, :], mask_k[:, :], start=False)
                last.then_inc(sem("st_mm"), 1)

            def pv_item(hh, s, q, n, first, last_head):
                c, j, lo = EXP_ITEMS[n]
                pe.wait_ge(sem("expd"), NI * hh + n + 1)
                if j == 0:
                    if not first:
                        pe.wait_ge(sem("o_out"), 2 * hh - 1 + c)
                    if c == 0:
                        pe.wait_ge(sem("den_sel"), hh + 1)
                p = probs[n % 4][:, 0:HALF - lo]
                end = j == 4 * c + 3
                mm(bank[4 + c][0:HD0, lo:], v0[q][:, j, s * HD0:(s + 1) * HD0], p, start=j == 0, stop=end)
                mm(bank[4 + c][DEN_ROW:DEN_ROW + H, lo:], den_sel[s][:, :], p, start=first and j == 0, stop=last_head and end).then_inc(sem("pv"), 1)

            def inv_to_rows(c, g):
                if g == 0:
                    pe.wait_ge(sem("inv_den"), c + 1)
                n = c * (H // 2) + g
                if n >= 2:
                    pe.wait_ge(sem("o_norm"), n - 1)
                mm(bank[n % 2][:, :], pair_rows[:, g, :], inv_den[c][:, :]).then_inc(sem("inv_rows"), 1)

            def head(hh, s, p, q, nxt, first=False):
                if first:
                    st_item(hh, s, 0, first)
                for n in range(NI):
                    if n + 1 < NI:
                        st_item(hh, s, n + 1, first)
                    elif nxt:
                        st_item(hh + 1, 1 - s, 0, False)
                    if nxt and n == 0:
                        project(hh + 1, 1 - s, False)
                    if nxt and s == 1 and n in (1, 2):
                        project_v(hh + 1, p + 1, 1 - q, n - 1)
                    if nxt:
                        for m in MAX_AT.get(n, ()):
                            max_item(hh + 1, m, False)
                    if nxt and n == 10:
                        max_to_row(hh + 1, p + s)
                    pv_item(hh, s, q, n, first, not nxt)
                    if not nxt and n >= 7:
                        for g in range(2 * n - 14, min(2 * n - 12, H // 2)):
                            inv_to_rows(0, g)

            with pe.Fori(0, B) as b:
                for l in range(2):
                    pe.wait_ge(sem("cond"), l + 1)
                    for a in range(2):
                        mm(bank[2 * l + a][:, 0:3 * D], cond[:, l, :], wmod[:, l, 3 * a * D:3 * (a + 1) * D]).then_inc(sem("mod_mm"), 1)
                transpose_h("ln_a")
                pe.wait_ge(sem("ln_a_hT"), 2)
                project(0, 0, True)
                for c in range(C):
                    project_v(0, 0, 0, c)
                pe.wait_ge(sem("mod_evac"), 2)
                for n in range(NI):
                    max_item(0, n, True)
                max_to_row(0, 0)
                head(0, 0, 0, 0, True, first=True)
                head(1, 1, 0, 0, True)
                with pe.Fori(0, H // 4 - 1) as g:
                    for q in range(2):
                        for s in range(2):
                            head(4 * g + 2 + 2 * q + s, s, 2 * g + 1 + q, 1 - q, True)
                head(H - 2, 0, H // 2 - 1, 1, True)
                head(H - 1, 1, H // 2 - 1, 1, False)
                pe.wait_ge(sem("expd"), NI * H)
                for c in range(C):
                    for g in range(H // 2):
                        if c == 1:
                            inv_to_rows(1, g)
                    for t in range(4 * c, 4 * c + 4):
                        for g in range(H // 2):
                            pe.wait_ge(sem("o_norm"), 8 * c + g + 1)
                            last = mm(bank[2 + c][:, (t % 4) * P:(t % 4 + 1) * P], oT[:, g, t * P:(t + 1) * P], w_out0[:, g, :], start=g == 0, stop=g == H // 2 - 1)
                    last.then_inc(sem("attn0_mm"), 1)
                transpose_h("ln_b")
                for c in range(C):
                    pe.wait_ge(sem("ln_b_hT"), c + 1)
                    mm(bank[1 + c][:, :], router0_rep[:, :], hT[:, c * HALF:(c + 1) * HALF]).then_inc(sem("w_mm"), 1)
                pe.wait_ge(sem("res_a"), 2)
                for u in range(1, T):
                    pe.wait_ge(sem("larger"), u)
                    for t in range(u):
                        last = mm(bank[3][:, u:u + 1], larger[t][:, (u - t) * P:(u - t + 1) * P], ones_bf[:, 0:1], start=t == 0, stop=t == u - 1)
                last.then_inc(sem("not_before"), 1)
                pe.wait_ge(sem("thr_part"), 1)
                mm(bank[3][:, 0:1], ones[:, :], thr_part[:, :]).then_inc(sem("slot_mm"), 1)
                pe.wait_ge(sem("sel"), 1)
                last = mm(bank[4][:, 0:T], before_bf[:, :], sel_bf[:, :], stop=False)
                for t in range(T - 1):
                    last = mm(bank[4][:, t + 1:T], ones_bf[:, :], sel_bf[:, t:t + 1].to_broadcast([P, T - 1 - t]), start=False, stop=t == T - 2)
                last.then_inc(sem("slot_mm"), 1)
                pe.wait_ge(sem("pick"), T)
                for t in range(T):
                    last = mm(bank[5][:, 0:D + 2], pick[:, t, :], h_room[:, t, :], start=t == 0, stop=t == T - 1)
                last.then_inc(sem("gather_mm"), 1)
                pe.wait_ge(sem("ws_idx"), 1)
                pe.transpose(bank[7][:, 0:SLOTS], ws_idx[:, 1:2].to_broadcast([P, P]), eye).then_inc(sem("idx_tr"), 1)
                for c in range(C):
                    for t in range(4 * c, 4 * c + 4):
                        last = pe.transpose(bank[1 + c][:, (t % 4) * P:(t % 4 + 1) * P], pick[:, t, :], eye)
                    last.then_inc(sem("pickT_tr"), 1)
                pe.wait_ge(sem("mask_pick"), MC)
                pe.wait_ge(sem("mask_in"), 16)
                for c in range(MC):
                    for r in range(MC):
                        last = mm(bank[0][:, c * P:(c + 1) * P], mask_in[:, r, c * P:(c + 1) * P], mask_pick[:, r, :], start=r == 0, stop=r == MC - 1)
                last.then_inc(sem("select_mm"), 1)
                pe.wait_ge(sem("hn"), 1)
                pe.wait_ge(sem("slot_of"), 1)
                pe.transpose(bank[4][:, 0:SLOTS], hn[:, :], eye).then_inc(sem("hn_tr"), 1)
                pe.wait_ge(sem("trig_rep"), 2)
                pe.wait_ge(sem("pickT"), 2)
                for a in range(2):
                    for c in range(MC):
                        last = mm(bank[2][:, a * SLOTS:(a + 1) * SLOTS], trig_rep[:, a, c, :, :].rearrange("p h d -> p (h d)"), mask_pick[:, c, :], start=c == 0, stop=c == MC - 1)
                last.then_inc(sem("select_mm"), 1)
                pe.wait_ge(sem("hnT"), 1)
                for n in range(2):
                    last = mm(bank[5][:, n * SLOTS:(n + 1) * SLOTS], ffn_w[:, n, :], hnT[:, :])
                last.then_inc(sem("qkv_s_mm"), 1)
                mm(bank[6][:, 0:D], hnT[:, :], ffn_w[:, 2, :]).then_inc(sem("qkv_s_mm"), 1)
                pe.wait_ge(sem("qk_s"), 1)
                pe.wait_ge(sem("idx_row"), 1)
                mm(bank[7][:, 0:2 * SLOTS], const("rot0"), qk_s[:, :, :].rearrange("p a s -> p (a s)")).then_inc(sem("rot0_mm"), 1)
                pe.wait_ge(sem("mask_rows"), 1)
                for c in range(MC):
                    last = mm(bank[1][:, 0:SLOTS], mask_rows[:, c, :], mask_pick[:, c, :], start=c == 0, stop=c == MC - 1)
                last.then_inc(sem("select_mm"), 1)
                pe.wait_ge(sem("mask_sel"), 1)
                pe.wait_ge(sem("trig_sel"), 1)
                for n in range(4):
                    pe.wait_ge(sem("k_diag"), n + 1)
                    mm(bank[n][:, :], qk_s[:, 0, :], k_diag[:, 4 * n:4 * n + 4, :].rearrange("p a s -> p (a s)")).then_inc(sem("sc_mm"), 1)
                pe.wait_ge(sem("v_s"), 1)
                pe.wait_ge(sem("rot_s"), 1)
                for n in range(5):
                    if n < 4:
                        pe.wait_ge(sem("sc_exp"), n + 1)
                        for a in range(4):
                            last = pe.transpose(bank[4 + n][:, a * P:(a + 1) * P], sc[:, 4 * n + a, :], eye)
                        last.then_inc(sem("p_tr"), 1)
                    if n:
                        pe.wait_ge(sem("pT"), n)
                        for hh in range(4 * n - 4, 4 * n):
                            last = mm(bank[0][:, hh * HD:(hh + 1) * HD], pT[:, hh, :], v_s[:, hh * HD:(hh + 1) * HD])
                last.then_inc(sem("o_s_mm"), 1)
                pe.wait_ge(sem("o_s"), 1)
                pe.transpose(bank[1][:, 0:SLOTS], o_s[:, :], eye).then_inc(sem("o_s_tr"), 1)
                pe.wait_ge(sem("o_sT"), 1)
                mm(bank[2][:, 0:D], o_sT[:, :], ffn_w[:, 3, :]).then_inc(sem("wo_mm"), 1)
                pe.wait_ge(sem("hn"), 2)
                pe.transpose(bank[3][:, 0:SLOTS], hn[:, :], eye).then_inc(sem("hn_tr"), 1)
                pe.wait_ge(sem("hnT"), 2)
                for c in range(FC):
                    last = mm(bank[4][:, c * SLOTS:(c + 1) * SLOTS], w1[:, c * P:(c + 1) * P], hnT[:, :])
                last.then_inc(sem("w1_mm"), 1)
                pe.wait_ge(sem("gelu"), 1)
                for c in range(FC):
                    last = mm(bank[5][:, 0:D], gelu[:, c, :], w2[:, c, :], start=c == 0, stop=c == FC - 1)
                last.then_inc(sem("w2_mm"), 1)
                pe.wait_ge(sem("proc"), 1)
                for c in range(C):
                    for t in range(4 * c, 4 * c + 4):
                        last = mm(bank[c][:, (t % 4) * P:(t % 4 + 1) * P], pickT[:, t * P:(t + 1) * P], proc[:, :])
                    last.then_inc(sem("scatter_mm"), 1)
                transpose_h("ln_c")
                pe.wait_ge(sem("ln_c_hT"), 2)
                pe.wait_ge(sem("res_b"), 2)
                def project1(k):
                    n, c = divmod(k, C)
                    mm(bank[k][:, :], attn_w[:, n, :], hT[:, c * HALF:(c + 1) * HALF]).then_inc(sem("qk1_mm"), 1)

                def rotate1(k):
                    n, c = divmod(k, C)
                    pe.wait_ge(sem("qk1"), k + 1)
                    mm(bank[4 + k][:, :], const("rot1"), qk_f[:, n, c * HALF:(c + 1) * HALF]).then_inc(sem("rot1_mm"), 1)

                project1(0)
                project1(1)
                for k in range(4):
                    rotate1(k)
                    if k < 2:
                        project1(k + 2)
                pe.wait_ge(sem("rot1_done"), 3)
                for c in range(C):
                    for t in range(4 * c, 4 * c + 4):
                        last = mm(bank[4 + 2 * c][:, (t % 4) * P:(t % 4 + 1) * P], hT[:, t * P:(t + 1) * P], attn_w[:, 2, :])
                    last.then_inc(sem("v1_mm"), 1)
                pe.wait_ge(sem("stacks"), 16 * 4 * len(TERMS))
                pe.wait_ge(sem("rot1_done"), 4)

                def max1_item(m):
                    u, t, hh, c = max_item1(m)
                    if m >= 3:
                        pe.wait_ge(sem("row_max1"), m - 2)
                    mm(bank[MAX1_BANK[m % 3]][:, :], q_stack[:, hh, t * P:(t + 1) * P], k_stack[:, hh // 2, c * HALF:(c + 1) * HALF]).then_inc(sem("s1_mm"), 1)

                def max1_to_rows(u):
                    pe.wait_ge(sem("nmax_hl"), u + 1)
                    if u >= 2:
                        pe.wait_ge(sem("ctx1"), u - 1)
                    for a in range(GH):
                        r = ROW_AT[a]
                        for t in range(4):
                            last = pe.matmul(bank[6][r:r + 2, t * P:(t + 1) * P], nmax_hl[:, a, 4 * (u % C) + t, :], eye_bf[:, :], start=True, stop=True)
                        last.then_inc(sem("mrow1_mm"), 1)

                def st1_item(n):
                    u, j, hh = exp_item1(n)
                    if n % UI == 0:
                        pe.wait_ge(sem("mrow1"), GH * (u + 1))
                    if n >= 3:
                        pe.wait_ge(sem("expd1"), n - 2)
                    mm(bank[ST1_BANK[n % 3]][:, :], k_stack[:, hh // 2, j * P:(j + 1) * P], q_stack[:, hh, (u % C) * HALF:(u % C + 1) * HALF]).then_inc(sem("st1_mm"), 1)

                def pv1_items(k):
                    for n in range(GH * k, GH * k + GH):
                        u, j, hh = exp_item1(n)
                        a = hh % GH
                        pe.wait_ge(sem("expd1"), n + 1)
                        if n == 0:
                            pe.wait_ge(sem("v1"), 2)
                        if j == 0 and a == 0 and u:
                            pe.wait_ge(sem("o1_raw"), u)
                        last = mm(bank[4][32 * a:32 * a + 32, :], v1[:, j, hh, :], ring1[n % 8][:, :], start=j == 0, stop=j == T - 1)
                    last.then_inc(sem("pv1"), 1)

                def ctx_transposes(u):
                    pe.wait_ge(sem("o1_raw"), u + 1)
                    pe.wait_ge(sem("mrow1"), GH * min(u + 2, UNITS))
                    if u:
                        pe.wait_ge(sem("ctx1"), u)
                    for t in range(4):
                        last = pe.transpose(bank[6][:, t * P:(t + 1) * P], o_raw[u % C][:, t * P:(t + 1) * P], eye)
                    last.then_inc(sem("ctx_raw"), 1)

                for m in range(LEAD):
                    max1_item(m)
                    if m - LEAD + 1 in ROWS_AT:
                        max1_to_rows(ROWS_AT[m - LEAD + 1])
                st1_item(0)
                st1_item(1)
                for n in range(NI1):
                    if n + LEAD < NI1:
                        max1_item(n + LEAD)
                    if n + 2 < NI1:
                        st1_item(n + 2)
                    if n and n % GH == 0:
                        pv1_items(n // GH - 1)
                    if n > 0 and n in ROWS_AT:
                        max1_to_rows(ROWS_AT[n])
                    if n in CTX_AT:
                        ctx_transposes(CTX_AT[n])
                pv1_items(NI1 // GH - 1)
                ctx_transposes(UNITS - 1)
                for c in range(C):
                    pe.wait_ge(sem("ctx1"), UNITS - 1 + c)
                    for t in range(4 * c, 4 * c + 4):
                        last = pe.transpose(bank[c][:, (t % 4) * P:(t % 4 + 1) * P], ctx1[:, t, :], eye)
                    last.then_inc(sem("ctx_tr"), 1)
                for c in range(C):
                    pe.wait_ge(sem("ctxT"), c + 1)
                    for t in range(4 * c, 4 * c + 4):
                        last = mm(bank[2 + c][:, (t % 4) * P:(t % 4 + 1) * P], ctxT[:, t * P:(t + 1) * P], attn_w[:, 3, :])
                    last.then_inc(sem("attn1_mm"), 1)
                transpose_h("ln_d")
                pe.wait_ge(sem("ln_d_hT"), 2)
                for t in range(T):
                    last = mm(bank[0][:, t * E:(t + 1) * E], hT[:, t * P:(t + 1) * P], router1[:, :])
                last.then_inc(sem("lg_mm"), 1)
                pe.wait_ge(sem("res_c"), 2)
                for t in range(T):
                    if t == 2:
                        pe.wait_ge(sem("lg_sub"), 1)
                    for a in range(2):
                        if t >= 4:
                            pe.wait_ge(sem("prod"), E * (t - 4) + 4 * (a + 1))
                        mm(bank[(2 * t + 4) % 8 + a][:, :], hT[:, t * P:(t + 1) * P], experts[:, 4 * a:4 * a + 4, :].rearrange("p e d -> p (e d)")).then_inc(sem("ex_mm"), 1)
                end_of_batch(pe, 3)

        @block.vector
        def _(dve):
            links = {}

            def link(ins, s="dve_chain", base=0):
                links[s] = links.get(s, 0) + 1
                ins.then_inc(sem(s), 1)
                dve.wait_ge(sem(s), links[s])

            def tt(dst, a, b_, op):
                return dve.tensor_tensor(dst, a, b_, op)

            dve.wait_ge(sem("setup_loads"), N_SETUP_LOADS)
            dve.tensor_copy(eye_bf[:, :], eye).then_inc(sem("setup_masks"), 1)
            dve.tensor_copy(ones_bf[:, :], const("den_sel")[:, H - 1:H].to_broadcast([P, P])).then_inc(sem("setup_masks"), 1)
            dve.tensor_copy(before_bf[:, :], const("before")).then_inc(sem("setup_masks"), 1)
            dve.tensor_copy(router0_rep[:, :], router0[:, :].to_broadcast([P, P])).then_inc(sem("setup_masks"), 1)
            dve.tensor_copy(mask_q[:, :], const("mask_q")).then_inc(sem("setup_masks"), 1)
            dve.tensor_copy(mask_k[:, :], const("mask_k")).then_inc(sem("setup_masks"), 1)
            dve.wait_ge(sem("setup_c_exp"), 1)
            SC = "setup_chain"
            link(dve.tensor_scalar(c_den[:, :, :], c_den[:, :, :], 1.0, None, ALU.add), SC)
            link(dve.reciprocal(c_den[:, :, :], c_den[:, :, :]), SC)
            link(tt(silu_c[:, :, :], c_raw[:, :, :], c_den[:, :, :], ALU.mult), SC)
            link(dve.tensor_copy(pos_f[:, :], pos_int[:, :]), SC)
            link(tt(angle[:, 1, :, :], pos_f[:, :].unsqueeze(2).to_broadcast([P, B * MC, HD // 2]),
                    const("invf").unsqueeze(1).to_broadcast([P, B * MC, HD // 2]), ALU.mult), SC)
            link(dve.tensor_copy(angle[:, 0, :, :], angle[:, 1, :, :]), SC)
            round_to = 12582912.0
            for a in range(2):
                link(dve.tensor_scalar(turns[:, a, :, :], angle[:, a, :, :], 1.0 / (2.0 * np.pi), 0.25 * (1 - a), ALU.mult, ALU.add), SC)
            link(dve.tensor_scalar(turns[:, :, :, :], turns[:, :, :, :], round_to, None, ALU.add), SC)
            link(dve.tensor_scalar(turns[:, :, :, :], turns[:, :, :, :], -round_to, None, ALU.add), SC)
            two_pi = 2.0 * np.pi
            part1 = 6.28125
            part2 = float(np.float32(round((two_pi - part1) * 2 ** 21) / 2 ** 21))
            part3 = two_pi - part1 - part2
            tn, an = turns[:, :, :, :].rearrange("p a n f -> p (a n f)"), angle[:, :, :, :].rearrange("p a n f -> p (a n f)")
            for part in (part1, part2, part3):
                link(dve.scalar_tensor_tensor(an, tn, -part, an, ALU.mult, ALU.add), SC)
            link(dve.tensor_scalar(angle[:, 0, :, :], angle[:, 0, :, :], float(np.pi / 2), None, ALU.add), SC)
            link(dve.tensor_scalar(an, an, 3.1415925, -3.1415925, ALU.min, ALU.max), SC)
            dve.memset(extra[:, :, 0:1], 0.0).then_inc(sem("setup_dve"), 1)

            def rsqrt(dst, src, bits, t_):
                link(dve.tensor_scalar(bits, src.bitcast(I32), 1, None, ALU.logical_shift_right))
                link(dve.tensor_scalar(bits, bits, -1.0, RSQRT_MAGIC, ALU.mult, ALU.add))
                cur = bits.bitcast(F32)
                for _ in range(3):
                    link(dve.scalar_tensor_tensor(t_, cur, -0.5, cur, ALU.mult, ALU.mult))
                    link(tt(t_, t_, src, ALU.mult))
                    link(dve.scalar_tensor_tensor(dst, t_, 1.5, cur, ALU.add, ALU.mult))
                    cur = dst

            def layernorm(name, c):
                stat = sem(name + "_stats")
                half, tiles = slice(4 * c, 4 * c + 4), range(4 * c, 4 * c + 4)
                for t in tiles:
                    dve.bn_stats(stats[:, t, :], x[:, t, :]).then_inc(stat, 1)
                for t in tiles:
                    dve.wait_ge(stat, 4 * c + t + 1)
                    ins = dve.bn_aggr(mv[:, t, :], stats[:, t, :])
                    ins.then_inc(stat, 1)
                dve.wait_ge(stat, 8 * (c + 1))
                link(dve.tensor_scalar(nvar[:, half], mv[:, half, 1], LN_EPS, None, ALU.add))
                rsqrt(rstd[:, half], nvar[:, half], nbits[:, half], ntmp[:, half])
                for t in tiles:
                    dve.tensor_scalar(h[:, t, :], x[:, t, :], mv[:, t, 0:1], rstd[:, t:t + 1], ALU.subtract, ALU.mult).then_inc(sem(name + "_h"), 1)

            def residual(c, src, l, gate, done, bias=None):
                if c:
                    dve.wait_ge(sem(done), c)
                tv = tmp[:, :].rearrange("p (t d) -> p t d", t=4)
                sv = src[:, :].rearrange("p (t d) -> p t d", t=4)
                g_ = mod[:, l, gate, :].unsqueeze(1).to_broadcast([P, 4, D])
                if bias is not None:
                    link(tt(tv, sv, bias.unsqueeze(1).to_broadcast([P, 4, D]), ALU.add))
                    link(tt(tv, tv, g_, ALU.mult))
                else:
                    link(tt(tv, sv, g_, ALU.mult))
                xv = x[:, 4 * c:4 * c + 4, :]
                ins = tt(xv, xv, tv, ALU.add)
                ins.then_inc(sem(done), 1)

            def prep_k(hh, s, first):
                for c in range(C):
                    dve.wait_ge(sem("qk_proj"), 2 * hh + c + 1)
                    if not first:
                        dve.wait_ge(sem("st_mm"), NI * (hh - 1))
                    elif hh == 0:
                        dve.tensor_copy(k_bf[0:HD0, c * HALF:(c + 1) * HALF], bank[6 + c][HD0:P, :]).then_inc(sem("kb_cast"), 1)
                    dve.tensor_copy(kT[s][0:HD0, c * HALF:(c + 1) * HALF], bank[6 + c][HD0:P, :]).then_inc(sem("k_evac"), 1)

            def row_max(hh, n):
                t, c, w = MAX_ITEMS[n]
                dve.wait_ge(sem("s_mm"), NI * hh + n + 1)
                dve.reduce_max(part_max[:, t, c:c + 1], bank[n % 2][:, 0:w], AX).then_inc(sem("row_max"), 1)

            def final_max(hh, first):
                dve.wait_ge(sem("row_max"), NI * hh + NI)
                if not first:
                    dve.wait_ge(sem("mrow_mm"), 2 * hh)
                dve.tensor_reduce(neg_max[:, :], part_max[:, :, :], AX, ALU.max, negate=True).then_inc(sem("neg_max"), 1)

            def select_sum(hh, s):
                if not isinstance(hh, int) or hh >= 2:
                    dve.wait_ge(sem("pv"), NI * (hh - 1))
                src = const("den_sel")[:, hh:hh + H] if isinstance(hh, int) else const("den_sel")[:, bass.ds(hh, H)]
                dve.tensor_copy(den_sel[s][:, :], src).then_inc(sem("den_sel"), 1)

            def o_out(hh, s, c):
                dve.wait_ge(sem("pv"), NI * hh + (4 if c == 0 else NI))
                g_ = (hh - s) // 2
                dve.tensor_copy(oT[s * HD0:(s + 1) * HD0, g_, c * HALF:(c + 1) * HALF], bank[4 + c][0:HD0, :]).then_inc(sem("o_out"), 1)

            def invert_sums(c):
                dve.wait_ge(sem("pv"), NI * (H - 1) + (4 if c == 0 else NI))
                dve.wait_ge(sem("den_zero"), 2)
                dve.reciprocal(inv_den[c][DEN_ROW:DEN_ROW + H, :], bank[4 + c][DEN_ROW:DEN_ROW + H, :]).then_inc(sem("inv_den"), 1)

            def o_norm(c, g):
                n = c * (H // 2) + g
                dve.wait_ge(sem("inv_rows"), n + 1)
                dve.wait_ge(sem("o_out"), 2 * H - 1 + c)
                ov = oT[:, g, c * HALF:(c + 1) * HALF]
                tt(ov, ov, bank[n % 2][:, :], ALU.mult).then_inc(sem("o_norm"), 1)

            def head(hh, s, nxt, first=False):
                for n in range(NI):
                    if nxt and n == 0:
                        prep_k(hh + 1, 1 - s, first)
                    if nxt and n == 2:
                        select_sum(hh + 1, 1 - s)
                    if nxt:
                        for m in MAX_AT.get(n, ()):
                            row_max(hh + 1, m)
                    if n == 4:
                        o_out(hh, s, 0)
                        if not nxt:
                            invert_sums(0)
                            for g in range(H // 2):
                                o_norm(0, g)
                    if nxt and n == 9:
                        final_max(hh + 1, False)
                o_out(hh, s, 1)
                if not nxt:
                    invert_sums(1)

            dve.wait_ge(sem("setup_mod_mm"), 1)
            link(dve.tensor_copy(mod_col[:, :, :, :].rearrange("p l a b -> p (l a b)"), bank[0][:, 0:12 * B]), SC)
            link(dve.tensor_scalar(mod_col[:, :, 1::3, :], mod_col[:, :, 1::3, :], 1.0, None, ALU.add), SC)
            dve.wait_ge(sem("setup_trig"), 1)
            with dve.Fori(0, B) as b:
                links["dve_chain"] = 0
                for l in range(2):
                    dve.tensor_copy(cond[:, l, :], silu_c[:, l, bass.ds(b, 1)].to_broadcast([P, P])).then_inc(sem("cond"), 1)
                dve.wait_ge(sem("x_in"), 16)
                for c in range(C):
                    layernorm("ln_a", c)
                prep_k(0, 0, True)
                for c in range(C):
                    dve.memset(inv_den[c][:, :], 0.0).then_inc(sem("den_zero"), 1)
                select_sum(0, 0)
                for n in range(NI):
                    row_max(0, n)
                final_max(0, True)
                head(0, 0, True, first=True)
                for a in range(2):
                    for hf in range(2):
                        ins = dve.tensor_copy(trig_rep[:, a, :, :, hf * (HD // 2):(hf + 1) * (HD // 2)],
                                              trig[:, a, bass.ds(b, 1), :, :].rearrange("p o c f -> p (o c) f").unsqueeze(2).to_broadcast([P, MC, H, HD // 2]))
                    ins.then_inc(sem("trig_rep"), 1)
                dve.wait_ge(sem("mod_evac"), 4)
                gates = mod[:, :, 2::3, :]
                link(dve.scalar_tensor_tensor(gate_abs.rearrange("p l a d -> p (l a) d"), gates_view(gates), -1.0, gates_view(gates), ALU.mult, ALU.max))
                link(dve.tensor_scalar(gate_abs, gate_abs, 0.25, None, ALU.max))
                link(dve.tensor_scalar(gates, gates, 0.0, 2.0, ALU.is_ge, ALU.mult))
                link(dve.tensor_scalar(gates, gates, -1.0, None, ALU.add))
                link(tt(gates, gates, gate_abs, ALU.mult))
                scales = mod[:, :, 1::3, :]
                link(dve.tensor_scalar(scales, scales, 1.0, None, ALU.add))
                head(1, 1, True)
                with dve.Fori(1, H // 2 - 1) as g:
                    head(2 * g, 0, True)
                    head(2 * g + 1, 1, True)
                head(H - 2, 0, True)
                head(H - 1, 1, False)
                for g in range(H // 2):
                    o_norm(1, g)
                for c in range(C):
                    dve.wait_ge(sem("attn0_mm"), c + 1)
                    residual(c, bank[2 + c], 0, 2, "res_a")
                    dve.wait_ge(sem("res_a"), c + 1)
                    dve.wait_ge(sem("ln_a_tr"), 2)
                    layernorm("ln_b", c)
                dve.wait_ge(sem("ln_b_h"), T)
                dve.wait_ge(sem("ln_b_tr"), 2)
                mod_b = [mod[:, 0, a, :].unsqueeze(1).to_broadcast([P, T, D]) for a in (4, 3)]
                link(tt(h[:, :, :], h[:, :, :], mod_b[0], ALU.mult))
                link(tt(h[:, :, :], h[:, :, :], mod_b[1], ALU.add))
                for t in range(T):
                    dve.wait_ge(sem("w_row"), t // 4 + 1)
                    dve.scalar_tensor_tensor(ties[:, t, :], w_row[:, t * P:(t + 1) * P], 1.0, eye, ALU.mult, ALU.mult, accum_out=w_col[:, t:t + 1]).then_inc(sem("w_col"), 1)
                dve.wait_ge(sem("w_col"), T)
                link(dve.tensor_copy(extra[:, :, 0], w_col[:, :]))
                link(dve.tensor_copy(extra[:, :, 1], const("row")))
                for t in range(T):
                    wt = w_col[:, t:t + 1]
                    dve.tensor_scalar(larger[t], w_row[:, t * P:], wt, None, ALU.is_gt, ALU.add, accum_out=cnt[:, t, 0:1]).then_inc(sem("larger"), 1)
                for t in range(T):
                    wt = w_col[:, t:t + 1]
                    ins = dve.scalar_tensor_tensor(ties[:, t, :], w_row[:, t * P:(t + 1) * P], wt, const("lower"), ALU.is_equal, ALU.mult, accum_out=cnt[:, t, 1:2])
                    ins.then_inc(sem("larger"), 1)
                dve.wait_ge(sem("larger"), 2 * T)
                link(tt(rank[:, :], cnt[:, :, 0], cnt[:, :, 1], ALU.add))
                link(tt(rank[:, :], rank[:, :], const("tile"), ALU.add))
                dve.wait_ge(sem("not_before"), 1)
                link(tt(rank[:, 1:T], rank[:, 1:T], bank[3][:, 1:T], ALU.subtract))
                for dst in (sel_bf, sel):
                    dve.tensor_scalar(dst[:, :], rank[:, :], float(TOPK - 1), None, ALU.is_lt).then_inc(sem("sel"), 1)
                dve.scalar_tensor_tensor(tmp[:, 0:T], rank[:, :], float(TOPK - 1), w_col[:, :], ALU.is_equal, ALU.mult, accum_out=thr_part[:, :]).then_inc(sem("thr_part"), 1)
                dve.wait_ge(sem("slot_mm"), 1)
                link(dve.tensor_copy(thr[:, :], bank[3][:, 0:1]))
                link(dve.tensor_scalar(unpicked[:, :], w_col[:, :], thr[:, 0:1], None, ALU.is_le))
                dve.wait_ge(sem("slot_mm"), 2)
                dve.tensor_copy(slot_of[:, :], bank[4][:, 0:T]).then_inc(sem("slot_of"), 1)
                dve.wait_ge(sem("slot_of"), 1)
                dve.wait_ge(sem("sel"), 2)
                for t in range(T):
                    dve.tensor_scalar(pick[:, t, :], const("slot"), slot_of[:, t:t + 1], sel[:, t:t + 1], ALU.is_equal, ALU.mult).then_inc(sem("pick"), 1)
                dve.wait_ge(sem("gather_mm"), 1)
                dve.tensor_copy(ws_idx[:, :], bank[5][:, D:D + 2]).then_inc(sem("ws_idx"), 1)
                link(dve.tensor_copy(xs[:, :], bank[5][:, 0:D]))
                dve.wait_ge(sem("idx_tr"), 1)
                dve.tensor_scalar(idx_row[:, :], bank[7][:, 0:SLOTS], float(MS - 1), None, ALU.min).then_inc(sem("idx_row"), 1)
                dve.wait_ge(sem("idx_row"), 1)
                for c in range(MC):
                    dve.tensor_scalar(mask_pick[:, c, :], idx_row[:, :], const("row")[:, c:c + 1], None, ALU.is_equal).then_inc(sem("mask_pick"), 1)

                def rmsnorm(src, n):
                    link(dve.scalar_tensor_tensor(hn[:, :], src, 1.0 / D, src, ALU.mult, ALU.mult, accum_out=nvar[:, 0:1]))
                    link(dve.tensor_scalar(nvar[:, 0:1], nvar[:, 0:1], RMS_EPS, None, ALU.add))
                    rsqrt(rstd[:, 0:1], nvar[:, 0:1], nbits[:, 0:1], ntmp[:, 0:1])
                    dve.scalar_tensor_tensor(hn[:, :], src, rstd[:, 0:1], ln_rows[:, n, :], ALU.mult, ALU.mult).then_inc(sem("hn"), 1)

                rmsnorm(xs[:, :], 0)
                dve.wait_ge(sem("trig_sel"), 1)
                dve.wait_ge(sem("rot0_mm"), 1)
                dve.wait_ge(sem("qk_s"), 1)
                two = [P, 2, SLOTS]
                link(tt(rot_s[:, :, :], bank[7][:, 0:2 * SLOTS].rearrange("p (a s) -> p a s", a=2), trig_sel[:, 1, :].unsqueeze(1).to_broadcast(two), ALU.mult))
                link(tt(qk_s[:, :, :], qk_s[:, :, :], trig_sel[:, 0, :].unsqueeze(1).to_broadcast(two), ALU.mult))
                tt(qk_s[:, :, :], qk_s[:, :, :], rot_s[:, :, :], ALU.add).then_inc(sem("rot_s"), 1)
                dve.wait_ge(sem("rot_s"), 1)
                four = [P, 4, SLOTS]

                def heads4(n):
                    return slice(4 * n, 4 * n + 4)

                for n in range(4):
                    tt(k_diag[:, heads4(n), :], qk_s[:, 1, :].unsqueeze(1).to_broadcast(four), const("head")[:, heads4(n)].unsqueeze(2).to_broadcast(four), ALU.mult).then_inc(sem("k_diag"), 1)
                dve.wait_ge(sem("select_mm"), 3)
                link(dve.tensor_copy(mask_sel[:, :], bank[1][:, 0:SLOTS]))
                dve.memset(mask_sel[:, SLOTS - 1:SLOTS], BIG).then_inc(sem("mask_sel"), 1)
                dve.wait_ge(sem("mask_sel"), 1)

                def sum_heads(n):
                    dve.wait_ge(sem("sc_exp"), n + 1)
                    link(dve.reduce_sum(sc_sum[:, heads4(n)], sc[:, heads4(n), :], AX))

                for n in range(4):
                    dve.wait_ge(sem("sc_mm"), n + 1)
                    link(dve.scalar_tensor_tensor(sc[:, heads4(n), :], bank[n][:, :].rearrange("p (a s) -> p a s", a=4), SCALE, mask_sel[:, :].unsqueeze(1).to_broadcast(four), ALU.mult, ALU.add))
                    link(dve.reduce_max(sc_max[:, heads4(n)], sc[:, heads4(n), :], AX))
                    tt(sc[:, heads4(n), :], sc[:, heads4(n), :], sc_max[:, heads4(n)].unsqueeze(2).to_broadcast(four), ALU.subtract).then_inc(sem("sc_sub"), 1)
                    if n:
                        sum_heads(n - 1)
                sum_heads(3)
                link(dve.reciprocal(sc_sum[:, :], sc_sum[:, :]))
                dve.wait_ge(sem("o_s_mm"), 1)
                tt(o_s[:, :].rearrange("p (h d) -> p h d", h=H), bank[0][:, 0:D].rearrange("p (h d) -> p h d", h=H), sc_sum[:, :].unsqueeze(2).to_broadcast([P, H, HD]), ALU.mult).then_inc(sem("o_s"), 1)
                dve.wait_ge(sem("wo_mm"), 1)
                link(tt(x1[:, :], xs[:, :], bank[2][:, 0:D], ALU.add))
                dve.wait_ge(sem("hn_tr"), 1)
                rmsnorm(x1[:, :], 1)
                link(tt(h[:, :, :], h[:, :, :], unpicked[:, :].unsqueeze(2).to_broadcast([P, T, D]), ALU.mult))
                link(tt(h[:, :, :], h[:, :, :], mod[:, 0, 5, :].unsqueeze(1).to_broadcast([P, T, D]), ALU.mult))
                link(tt(x[:, :, :], x[:, :, :], h[:, :, :], ALU.add))
                dve.wait_ge(sem("w2_mm"), 1)
                link(tt(x1[:, :], x1[:, :], bank[5][:, 0:D], ALU.add))
                link(dve.tensor_scalar(x1[:, :], x1[:, :], ws_idx[:, 0:1], None, ALU.mult))
                tt(proc[:, :], x1[:, :], mod[:, 0, 5, :], ALU.mult).then_inc(sem("proc"), 1)
                for c in range(C):
                    xv = x[:, 4 * c:4 * c + 4, :]
                    dve.wait_ge(sem("scatter_mm"), c + 1)
                    tt(xv, xv, bank[c][:, :].rearrange("p (t d) -> p t d", t=4), ALU.add).then_inc(sem("res_b"), 1)
                    dve.wait_ge(sem("res_b"), c + 1)
                    layernorm("ln_c", c)
                parts1 = [(n, c) for n in range(2) for c in range(C)]

                def rope1(k):
                    n, c = parts1[k]
                    cols = slice(c * HALF, (c + 1) * HALF)
                    dve.wait_ge(sem("rot1_mm"), k + 1)
                    tt(rot_f[:, cols], bank[4 + k][:, :], const("sin1")[:, cols], ALU.mult).then_inc(sem("rot1_done"), 1)
                    dve.wait_ge(sem("qk1"), k + 1)
                    link(tt(qk_f[:, n, cols], qk_f[:, n, cols], const("cos1")[:, cols], ALU.mult))
                    dve.wait_ge(sem("rot1_done"), k + 1)
                    tt(qk_f[:, n, cols], qk_f[:, n, cols], rot_f[:, cols], ALU.add).then_inc(sem("rope1"), 1)
                    dve.wait_ge(sem("rope1"), k + 1)

                def rest1(k, part):
                    n, c = parts1[k]
                    cols = slice(c * HALF, (c + 1) * HALF)
                    a = "qk"[n]
                    dve.wait_ge(sem("split_" + part), k + 1)
                    if part == "h":
                        tt(qk_f[:, n, cols], qk_f[:, n, cols], split[a]["h"][:, cols], ALU.subtract).then_inc(sem("rest1"), 1)
                        dve.wait_ge(sem("rest1"), k + 1)
                    else:
                        tt(split[a]["l"][:, cols], qk_f[:, n, cols], split[a]["m"][:, cols], ALU.subtract).then_inc(sem("split_l"), 1)

                for k in range(len(parts1) + 2):
                    if k < 4:
                        rope1(k)
                    if 1 <= k < 5:
                        rest1(k - 1, "h")
                    if k >= 2:
                        rest1(k - 2, "m")
                def values1(c):
                    dve.wait_ge(sem("v_clear"), 2)
                    dve.wait_ge(sem("v1_mm"), c + 1)
                    tt(v1[:, 4 * c:4 * c + 4, :, 0:HD], bank[4 + 2 * c][:, :].rearrange("p (t h d) -> p t h d", t=4, h=H),
                       vo_bias[:, 0, :].rearrange("p (h d) -> p h d", h=H).unsqueeze(1).to_broadcast([P, 4, H, HD]), ALU.add).then_inc(sem("v1"), 1)

                def row_max1(m):
                    u, t, hh, c = max_item1(m)
                    dve.wait_ge(sem("s1_mm"), m + 1)
                    dve.reduce_max(pmax1[:, hh % GH, t, c:c + 1], bank[MAX1_BANK[m % 3]][:, :], AX).then_inc(sem("row_max1"), 1)
                    if m % UI == UI - 1:
                        final_max1(u)

                def final_max1(u):
                    half = slice(4 * (u % C), 4 * (u % C) + 4)
                    dve.wait_ge(sem("row_max1"), UI * (u + 1))
                    link(dve.tensor_reduce(nmax1[:, :, half], pmax1[:, :, half, :], AX, ALU.max, negate=True))
                    if u >= 2:
                        dve.wait_ge(sem("mrow1_mm"), GH * (u - 1))
                    link(dve.tensor_copy(nmax_hl[:, :, half, 0], nmax1[:, :, half]))
                    tt(nmax_hl[:, :, half, 1], nmax1[:, :, half], nmax_hl[:, :, half, 0], ALU.subtract).then_inc(sem("nmax_hl"), 1)

                def o1_raw(u):
                    dve.wait_ge(sem("pv1"), UI // GH * (u + 1))
                    if u >= 2:
                        dve.wait_ge(sem("ctx_raw"), u - 1)
                    dve.tensor_copy(o_raw[u % C][:, :], bank[4][:, :]).then_inc(sem("o1_raw"), 1)

                def ctx_out(u):
                    g, c = divmod(u, C)
                    dve.wait_ge(sem("ctx_raw"), u + 1)
                    bv = bank[6][:, :].rearrange("p (t a e) -> p t a e", t=4, a=GH)
                    link(dve.reciprocal(den1[:, :, :], bv[:, :, :, HD]))
                    tt(ctx1[:, 4 * c:4 * c + 4, GH * HD * g:GH * HD * (g + 1)].rearrange("p t (a d) -> p t a d", a=GH), bv[:, :, :, 0:HD],
                       den1[:, :, :].unsqueeze(3).to_broadcast([P, 4, GH, HD]), ALU.mult).then_inc(sem("ctx1"), 1)

                for m in range(LEAD):
                    row_max1(m)
                    if m in (16, 20):
                        values1((m - 16) // 4)
                for n in range(NI1):
                    if n + LEAD < NI1:
                        row_max1(n + LEAD)
                    if n - 1 in CTX_AT:
                        ctx_out(CTX_AT[n - 1])
                    if n + 3 in CTX_AT:
                        o1_raw(CTX_AT[n + 3])
                o1_raw(UNITS - 1)
                ctx_out(UNITS - 1)
                for c in range(C):
                    dve.wait_ge(sem("attn1_mm"), c + 1)
                    residual(c, bank[2 + c], 1, 2, "res_c", bias=vo_bias[:, 1, :])
                    dve.wait_ge(sem("res_c"), c + 1)
                    layernorm("ln_d", c)
                te = [P, T, E]

                def over_e(a):
                    return a.unsqueeze(2).to_broadcast(te)

                expert = const("expert").unsqueeze(1).to_broadcast(te)
                dve.wait_ge(sem("lg_mm"), 1)
                link(dve.tensor_copy(lg[:, :, :], bank[0][:, 0:T * E].rearrange("p (t e) -> p t e", t=T)))
                link(dve.reduce_max(m1[:, :], lg[:, :, :], AX))
                tt(lg[:, :, :], lg[:, :, :], over_e(m1[:, :]), ALU.subtract).then_inc(sem("lg_sub"), 1)
                dve.wait_ge(sem("lg_exp"), 1)
                link(dve.reduce_sum(m2[:, :], lg[:, :, :], AX))
                link(dve.reciprocal(m2[:, :], m2[:, :]))
                link(tt(lg[:, :, :], lg[:, :, :], over_e(m2[:, :]), ALU.mult))

                def best(p_, top, oh):
                    link(dve.reduce_max(top, p_, AX))
                    link(tt(oh, p_, over_e(top), ALU.is_equal))
                    link(tt(oh, oh, expert, ALU.mult))
                    link(dve.tensor_reduce(e1[:, :], oh, AX, ALU.min))
                    link(tt(oh, expert, over_e(e1[:, :]), ALU.is_equal))

                best(lg[:, :, :], m1[:, :], oh1[:, :, :])
                link(dve.scalar_tensor_tensor(lg2[:, :, :], oh1[:, :, :], -4.0, lg[:, :, :], ALU.mult, ALU.add))
                best(lg2[:, :, :], m2[:, :], oh2[:, :, :])
                link(tt(e1[:, :], m1[:, :], m2[:, :], ALU.add))
                link(dve.tensor_scalar(e1[:, :], e1[:, :], 1e-6, None, ALU.add))
                link(dve.reciprocal(e1[:, :], e1[:, :]))
                link(tt(nvar[:, :], m1[:, :], m1[:, :], ALU.mult))
                link(tt(ntmp[:, :], m2[:, :], m2[:, :], ALU.mult))
                link(tt(nvar[:, :], nvar[:, :], ntmp[:, :], ALU.add))
                tt(bias_tok[:, :], nvar[:, :], e1[:, :], ALU.mult).then_inc(sem("coef"), 1)
                link(tt(m1[:, :], m1[:, :], e1[:, :], ALU.mult))
                link(tt(m2[:, :], m2[:, :], e1[:, :], ALU.mult))
                link(tt(oh1[:, :, :], oh1[:, :, :], over_e(m1[:, :]), ALU.mult))
                link(tt(oh2[:, :, :], oh2[:, :, :], over_e(m2[:, :]), ALU.mult))
                tt(coef[:, :, :], oh1[:, :, :], oh2[:, :, :], ALU.add).then_inc(sem("coef"), 1)
                for r in range(T // 2):
                    pair = slice(2 * r, 2 * r + 2)
                    for t in (2 * r, 2 * r + 1):
                        dve.wait_ge(sem("prod"), E * (t + 1))
                        dve.tensor_reduce(moe[:, t, :], prod[:, t % 4, :, :].rearrange("p e d -> p d e"), AX, ALU.add).then_inc(sem("moe"), 1)
                    dve.wait_ge(sem("moe"), 2 * r + 2)
                    link(tt(moe[:, pair, :], moe[:, pair, :], mod[:, 1, 5, :].unsqueeze(1).to_broadcast([P, 2, D]), ALU.mult))
                    tt(x[:, pair, :], x[:, pair, :], moe[:, pair, :], ALU.add).then_inc(sem("x_final"), 1)
                end_of_batch(dve, 4)


def gates_view(a):
    return a.rearrange("p l a d -> p (l a) d")


_INS = ["L0_attn_x", "L0_attn_w_qkv", "L0_attn_w_out", "L0_ffn_attention_mask", "L0_ffn_position_ids", "L0_ffn_router_w", "L0_ffn_router_b",
        "L0_ffn_wq", "L0_ffn_wk", "L0_ffn_wv", "L0_ffn_wo", "L0_ffn_w1", "L0_ffn_w2", "L0_ffn_ln1", "L0_ffn_ln2", "L0_c", "L0_wmod",
        "L1_attn_Wq", "L1_attn_bq", "L1_attn_Wk", "L1_attn_bk", "L1_attn_Wv", "L1_attn_bv", "L1_attn_Wo", "L1_attn_bo",
        "L1_ffn_router_w", "L1_ffn_expert_weights", "L1_c", "L1_wmod"]


def kernel(**inputs):
    import numpy as _np
    import concourse.bacc as _bacc
    from concourse import mybir as _mybir
    from concourse.bass_utils import run_bass_kernel_spmd as _run

    nc = _bacc.Bacc("TRN2", target_bir_lowering=False, num_devices=1)
    arrays, aps = {}, {}
    for name in _INS:
        a = _np.ascontiguousarray(inputs[name])
        arrays[f"in_{name}"] = a
        aps[name] = nc.dram_tensor(f"in_{name}", a.shape, _mybir.dt.from_np(a.dtype), kind="ExternalInput").ap()
    out = nc.dram_tensor("out_0", (B, S, D), F32, kind="ExternalOutput").ap()
    adaln_kernel(nc, aps, out)
    r = _run(nc, [arrays], core_ids=[0])
    return r.results[0]["out_0"]
```

```python
from contextlib import ExitStack

import numpy as np

import concourse.bass as bass
from concourse import mybir
from concourse.alu_op_type import AluOpType as ALU

ACT = mybir.ActivationFunctionType
AX = mybir.AxisListType.X
F32 = mybir.dt.float32
BF16 = mybir.dt.bfloat16
I32 = mybir.dt.int32

P = 128
D = 128
B = 4
S = 1024
T = S // P
HALF = S // 2
C = 2
H = 16
HD0 = 64
HD = D // H
MS = 512
MC = MS // P
SLOTS = P
TOPK = S // 8
F = 512
FC = F // P
E = 8
GH = 4
NG = H // GH
SCALE0 = HD0 ** -0.5
SCALE = HD ** -0.5
BIG = -1e30
LN_EPS = 1e-5
RMS_EPS = 1e-6
RSQRT_MAGIC = float(0x5F3759DF)
DEN_ROW = HD0
HM = 64
M_ROW = 32
TERMS = [(0, "h", "h"), (8, "h", "m"), (16, "m", "h"), (24, "h", "l"), (40, "m", "m"), (48, "l", "h")]

MAX_ITEMS = [(t, c, min(HALF, (t + 1) * P - c * HALF)) for t in range(T) for c in range(t // 4 + 1)]
EXP_ITEMS = [(c, j, max(0, j * P - c * HALF)) for c in range(C) for j in range(4 * c + 4)]
NI = len(EXP_ITEMS)
assert len(MAX_ITEMS) == NI == 12
PROJECT_AT = {0: 0, 2: 1}
VALUES_AT = 4
MAX_AT = {3 + k: (0, range(3 * k, 3 * k + 3)) for k in range(4)} | {7 + k: (1, range(3 * k, 3 * k + 3)) for k in range(4)}
ROWS_AFTER = {8: 0, 11: 1}
RING_BEFORE = {1: 11 - NI, 2: 10 - NI, 3: 1, 5: 3, 6: 2, 7: 5, 8: 6, 9: 7, 10: 8, 11: 9}
ADDED = [sum(1 for _, j, _ in EXP_ITEMS[:n + 1] if j) for n in range(NI)]
NP = H // 2
LAST_DEN_AT = 4
LAST_ROWS_AT = {9: range(0, 3), 10: range(3, 6), 11: range(6, 8)}
DENS_AT = (11, 1)

UNITS = NG * C
UI = 32
NI1 = UNITS * UI
LEAD = 41
ROWS_AT = {UI * (u + 1) - LEAD + 2: u for u in range(UNITS)}
CTX_AT = {UI * (u + 1) + 4: u for u in range(UNITS - 1)}
assert UI + 2 < LEAD < 2 * UI


def max_item1(m):
    u, r = divmod(m, UI)
    return u, 4 * (u % C) + r // 8, GH * (u // C) + r // 2 % GH, r % 2


MAX1_BANK = (0, 1, 5)
ST1_BANK = (2, 3, 7)
ROW_AT = (32, 96, 0, 64)


def exp_item1(m):
    u, r = divmod(m, UI)
    return u, r // GH, GH * (u // C) + r % GH


def shape_constants():
    p = np.arange(P)
    eye = np.eye(P, dtype=np.float32)
    later = (p[None, :] > p[:, None]).astype(np.float32)
    rot0 = np.zeros((P, P), np.float32)
    rot1 = np.zeros((P, P), np.float32)
    for m in range(P):
        d = m % HD
        if d < HD // 2:
            rot0[m + HD // 2, m] = -1.0
        else:
            rot0[m - HD // 2, m] = 1.0
        if d < 6:
            rot1[m + 1 if d % 2 == 0 else m - 1, m] = -1.0 if d % 2 == 0 else 1.0
    tok = np.arange(S)
    frame, rest = tok // 256, tok % 256
    ids = np.stack([frame, rest // 16, rest % 16]).astype(np.float32)
    cos, sin = np.ones((P, S), np.float32), np.zeros((P, S), np.float32)
    for m in range(P):
        if m % HD < 6:
            cos[m], sin[m] = np.cos(ids[m % HD // 2]), np.sin(ids[m % HD // 2])
    parts = {
        "eye": eye,
        "mask_q": later * BIG,
        "mask_k": later.T * BIG,
        "before": later,
        "lower": later.T.copy(),
        "rot0": rot0,
        "rot1": rot1,
        "slot": np.broadcast_to(p.astype(np.float32), (P, P)),
        "tile": np.broadcast_to(P * np.arange(T, dtype=np.float32), (P, T)),
        "row": (p[:, None] + P * np.arange(T)[None, :]).astype(np.float32),
        "head": (p[:, None] // HD == np.arange(H)[None, :]).astype(np.float32),
        "invf": np.broadcast_to((1.0 / np.float32(10000.0) ** (np.arange(0, HD, 2, dtype=np.float32) / HD)).astype(np.float32), (P, HD // 2)),
        "expert": np.broadcast_to(np.arange(E, dtype=np.float32) - E, (P, E)),
        "cos1": cos,
        "sin1": sin,
    }
    pair_rows = np.zeros((P, H // 2, P), np.float32)
    for hh in range(H):
        pair_rows[DEN_ROW + hh, hh // 2, hh % 2 * HD0:(hh % 2 + 1) * HD0] = 1.0
    at, n = {}, 0
    for name, a in parts.items():
        at[name] = (n, n + a.shape[1])
        n += a.shape[1]
    return at, np.concatenate(list(parts.values()), axis=1).astype(np.float32), pair_rows


def adaln_kernel(nc, i, out):
    CONST_AT, const_values, pair_values = shape_constants()
    const_dram = nc.inline_tensor(const_values, "shape_constants")
    pair_dram = nc.inline_tensor(pair_values, "pair_rows")

    with ExitStack() as ctx:
        def sb(name, shape, dt=F32):
            return ctx.enter_context(nc.sbuf_tensor(name, shape, dt))

        consts = sb("consts", [P, const_values.shape[1]])

        def const(name):
            a, z = CONST_AT[name]
            return consts[:, a:z]

        eye = const("eye")
        eye_bf = sb("eye_bf", [P, P], BF16)
        mask_q = sb("mask_q_bf", [P, P], BF16)
        mask_k = sb("mask_k_bf", [P, P], BF16)
        ones = sb("ones", [P, P])
        silu_c = sb("silu_c", [P, 2, B])
        c_raw = sb("c_raw", [P, 2, B])
        c_den = sb("c_den", [P, 2, B])
        wmod = sb("wmod", [P, 2, 6 * D])
        w_out0 = sb("w_out0", [P, H // 2, D])
        router0 = sb("router0", [P, 1])
        router0_rep = sb("router0_rep", [P, P])
        router0_b = sb("router0_b", [P, 1])
        ln_rows = sb("ln_rows", [P, 2, D])
        ffn_w = sb("ffn_w", [P, 4, D])
        w1 = sb("w1", [P, F])
        w2 = sb("w2", [P, FC, D])
        attn_w = sb("attn_w", [P, 4, D])
        qk_bias = sb("qk_bias", [P, 2])
        vo_bias = sb("vo_bias", [P, 2, D])
        router1 = sb("router1", [P, E])
        experts = sb("experts", [P, E, D])
        pos_int = sb("pos_int", [P, B * MC], I32)
        pos_f = sb("pos_f", [P, B * MC])
        angle = sb("angle", [P, 2, B * MC, HD // 2])
        turns = sb("turns", [P, 2, B * MC, HD // 2])
        trig = sb("trig", [P, 2, B, MC, HD // 2])

        x = sb("x", [P, T, D])
        h_room = sb("h", [P, T, D + 2])
        h, extra = h_room[:, :, 0:D], h_room[:, :, D:D + 2]
        hT = sb("hT", [P, S])
        mod = sb("mod", [P, 2, 6, D])
        mod_col = sb("mod_col", [P, 2, 6, B])
        stats = sb("stats", [P, T, 6])
        mv = sb("mv", [P, T, 2])
        nvar = sb("nvar", [P, T])
        nbits = sb("nbits", [P, T], I32)
        ntmp = sb("ntmp", [P, T])
        rstd = sb("rstd", [P, T])
        tmp = sb("tmp", [P, HALF])
        gate_abs = tmp[:, :].rearrange("p (l a d) -> p l a d", l=2, a=2)

        w_qk = [sb(f"w_qk{s}", [P, 2 * HD0]) for s in range(2)]
        w_v = [sb(f"w_v{q}", [P, 2 * HD0]) for q in range(2)]
        q_stack = sb("q_stack", [P, H, S], BF16)
        stack_f32 = q_stack[:, :, :].rearrange("p h s -> p (h s)").bitcast(F32)
        second = [stack_f32[:, (4 + m) * S:(5 + m) * S] for m in range(4)]
        qT = [sb(f"qT{s}", [P, S]) for s in range(2)] + second[0:2]
        kT = [sb(f"kT{s}", [P, S]) for s in range(2)] + second[2:4]
        pickT = sb("pickT", [P, S])
        bf_room = pickT[:, :].bitcast(BF16)
        q_bf = [sb("q_bf", [P, S], BF16), bf_room[:, 0:S]]
        k_bf = [sb("k_bf", [P, S], BF16), bf_room[:, S:2 * S]]
        v0 = [sb(f"v0{q}", [P, T, 2 * HD0]) for q in range(2)]
        part_max = sb("part_max", [P, T, C])
        neg_max = sb("neg_max", [P, T])
        probs_room = sb("probs", [P, 4, HALF])
        probs = [probs_room[:, n, :] for n in range(4)]
        o_raw = [sb(f"o_raw{c}", [P, HALF]) for c in range(C)]
        mask_in = sb("mask_in", [P, MC, MS])
        p_sum = [[mask_in[:, 2 * s + c, :] for c in range(C)] for s in range(2)]
        w_row = sb("w_row", [P, S])
        den_rows = [w_row[:, c * HALF:(c + 1) * HALF] for c in range(C)]
        inv_den = o_raw
        room = sb("room", [P, 8 * S])
        oT = room[:, :].rearrange("p (g s) -> p g s", s=S)
        cond = room[:, 0:2 * P].rearrange("p (l s) -> p l s", l=2)

        w_col = sb("w_col", [P, T])
        larger = [room[:, 4 * S:8 * S].bitcast(BF16)[:, t * S:t * S + (T - t) * P] for t in range(T)]
        cnt = sb("cnt", [P, T, 2])
        ones_bf = sb("ones_bf", [P, P], BF16)
        before_bf = sb("before_bf", [P, P], BF16)
        sel_bf = sb("sel_bf", [P, T], BF16)
        rank = sb("rank", [P, T])
        sel = sb("sel", [P, T])
        thr_part = sb("thr_part", [P, 1])
        thr = sb("thr", [P, 1])
        unpicked = sb("unpicked", [P, T])
        slot_of = sb("slot_of", [P, T])
        pick = sb("pick", [P, T, SLOTS])
        ties = pick
        pair_rows = pick
        xs = sb("xs", [P, D])
        ws_idx = sb("ws_idx", [P, 2])
        idx_row = sb("idx_row", [P, SLOTS])
        mask_pick = sb("mask_pick", [P, MC, SLOTS])
        mask_rows = sb("mask_rows", [P, MC, SLOTS])
        mask_sel = sb("mask_sel", [P, SLOTS])
        trig_rep = sb("trig_rep", [P, 2, MC, H, HD // 2 * 2])
        trig_sel = sb("trig_sel", [P, 2, SLOTS])
        hn = sb("hn", [P, D])
        hnT = sb("hnT", [P, SLOTS])
        qk_s = sb("qk_s", [P, 2, SLOTS])
        rot_s = sb("rot_s", [P, 2, SLOTS])
        v_s = sb("v_s", [P, D])
        k_diag = room[:, 4 * S:6 * S].rearrange("p (h s) -> p h s", h=H)
        sc = room[:, 6 * S:8 * S].rearrange("p (h s) -> p h s", h=H)
        sc_max = sb("sc_max", [P, H])
        sc_sum = sb("sc_sum", [P, H])
        pT = probs_room[:, :, :].rearrange("p n (a s) -> p (n a) s", a=4)
        o_s = sb("o_s", [P, D])
        o_sT = sb("o_sT", [P, SLOTS])
        x1 = sb("x1", [P, D])
        gelu = sb("gelu", [P, FC, SLOTS])
        proc = sb("proc", [P, D])

        qk_f = room[:, 4 * S:6 * S].rearrange("p (a s) -> p a s", a=2)
        rot_f = w_row
        sc_room = room[:, 6 * S:8 * S].bitcast(BF16).rearrange("p (n s) -> p n s", s=S)
        pT_room = probs_room[:, :, :].rearrange("p n s -> p (n s)").bitcast(BF16).rearrange("p (n s) -> p n s", s=S)
        split = {"q": {n: sc_room[:, m, :] for m, n in enumerate("hml")}, "k": {n: pT_room[:, m, :] for m, n in enumerate("hml")}}
        ring1 = probs + [mask_in[:, n, :] for n in range(4)]
        k_stack = room[:, 0:4 * S].bitcast(BF16).rearrange("p (g s) -> p g s", s=S)
        v1 = room[:, 4 * S:8 * S].rearrange("p (t h c) -> p t h c", t=T, h=H)
        pmax1 = sb("pmax1", [P, GH, T, C])
        nmax1 = sb("nmax1", [P, GH, T])
        nmax_hl = sb("nmax_hl", [P, GH, T, 2], BF16)
        den1 = sb("den1", [P, 4, GH])
        ctx1 = pick
        ctxT = pickT

        lg = sb("lg", [P, T, E])
        m1 = sb("m1", [P, T])
        m2 = sb("m2", [P, T])
        e1 = sb("e1", [P, T])
        oh1 = sb("oh1", [P, T, E])
        oh2 = sb("oh2", [P, T, E])
        lg2 = sb("lg2", [P, T, E])
        coef = sb("coef", [P, T, E])
        bias_tok = sb("bias_tok", [P, T])
        prod = room[:, 0:4 * S].rearrange("p (n e d) -> p n e d", n=4, e=E)
        moe = w_row[:, :].rearrange("p (t d) -> p t d", t=T)

        bank = [ctx.enter_context(nc.psum_tensor(f"bank{n}", [P, HALF], F32)) for n in range(8)]

        den_dram = nc.dram_tensor("softmax_sums", [C, H, HALF], F32).ap()
        scratch = {a: {n: nc.dram_tensor(f"scratch_{a}{n}", [P, S], BF16).ap() for n in "hml"} for a in "qk"}

        ONCE = ("setup_loads setup_masks setup_pool setup_dve setup_c_exp setup_trig setup_chain setup_mod_mm "
                "stored x_free batch_arrived batch_shares batch_cleared batch_left").split()
        PER_BATCH = """
                 attn0_mm attn1_mm cast_go cond ctx1 ctxT ctx_raw ctx_tr den_zero den_mm den_evac den_stored den_loaded added slots_clear dve_chain ex_mm expd expd1 gather_mm gelu hn
                 hnT hn_tr idx_tr inv_den inv_rows k_clear k_diag larger not_before k_evac kb_cast lg_exp lg_mm lg_sub
                 mask_in mask_pick mask_rows mask_sel mod_evac mod_mm moe mrow1 mrow1_mm
                 mrow_evac mrow_mm neg_max nmax_hl o1_raw o_norm o_out o_s o_sT o_s_mm o_s_tr pT p_tr pair_rows pick pickT pickT_tr proc
                 pv pv1 q_evac qb_cast qk1 qk1_mm qk_proj qk_s qkv_s_mm res_a res_b res_c rot0_mm rot1_done rot1_mm rope1 rest1 rot_s
                 row_max row_max1 s1_mm s_mm sc_exp sc_mm sc_max scatter_mm sel slot_mm slot_of split_h split_m split_l
                 st1_mm st_mm stack_clear stacks thr_part select_mm trig_rep trig_sel v1 v1_mm v_evac
                 v_proj v_s w1_mm w2_mm w_col w_pair0 w_pair1 w_mm w_row wo_mm coef prod idx x_final x_in
        """.split() + [f"scratch_{a}{part}" for a in "qk" for part in "hml"] + [f"ln_{a}_{b_}" for a in "abcd" for b_ in ("stats", "h", "tr", "hT")]
        sems = {name: ctx.enter_context(nc.semaphore(name)) for name in ONCE + PER_BATCH}

        def sem(name):
            return sems[name]

        arrived, cleared, left = sem("batch_arrived"), sem("batch_cleared"), sem("batch_left")

        SETUP_LOADS = []

        ENGINES = 5

        def clear_share(eng, k):
            eng.drain().then_inc(arrived, 1)
            eng.wait_ge(arrived, ENGINES)
            for name in PER_BATCH[k::ENGINES]:
                eng.sem_clear(sem(name))
            eng.sem_inc(sem("batch_shares"), 1)

        def end_of_batch(eng, k):
            clear_share(eng, k)
            eng.wait_ge(cleared, 1)
            eng.sem_inc(left, 1)

        def to_stack(eng, n):
            a = "qk"[n]

            def write(part):
                eng.wait_ge(sem("split_" + part), C * (n + 1))
                eng.dma_start(scratch[a][part], split[a][part]).then_inc(sem(f"scratch_{a}{part}"), 16)

            def spread(part):
                eng.wait_ge(sem(f"scratch_{a}{part}"), 16)
                for row, *parts in TERMS:
                    if parts[n] == part:
                        src = scratch[a][part].rearrange("(g a d) t -> a d g t", a=2, d=HD)
                        for par in range(2):
                            rows = slice(par * HM + row, par * HM + row + HD)
                            dst = q_stack[rows, par::2, :] if a == "q" else k_stack[rows, :, :]
                            eng.dma_start(dst, src[par]).then_inc(sem("stacks"), 16)

            write("h")
            write("m")
            if a == "q":
                eng.wait_ge(sem("stack_clear"), 3)
            else:
                eng.wait_ge(sem("k_clear"), 3)
                write("l")
            spread("h")
            if a == "q":
                write("l")
            spread("m")
            spread("l")

        block = ctx.enter_context(nc.Block())

        @block.sync
        def _(sp):
            def load(dst, src, s="setup_loads"):
                sp.dma_start(dst, src, allow_slow_non_contiguous=True).then_inc(sem(s), 16)
                SETUP_LOADS.append(1)

            load(consts[:, :], const_dram[:])
            for l in range(2):
                load(wmod[:, l, :], i[f"L{l}_wmod"])
                load(c_raw[:, l, :], i[f"L{l}_c"].rearrange("b d -> d b"))
            load(pos_int[:, :], i["L0_ffn_position_ids"].rearrange("b (c p) -> p (b c)", p=P))
            load(w_out0[:, :, :], i["L0_attn_w_out"].rearrange("(g a) d e -> (a d) g e", a=2))
            load(router0[:, :], i["L0_ffn_router_w"])
            load(router0_b[:, :], i["L0_ffn_router_b"].rearrange("(a n) -> a n", a=1).broadcast_to([P, 1]))
            for n, name in enumerate(["L0_ffn_ln1", "L0_ffn_ln2"]):
                load(ln_rows[:, n, :], i[name].rearrange("(a n) -> a n", a=1).broadcast_to([P, D]))
            for n, name in enumerate(["L0_ffn_wq", "L0_ffn_wk", "L0_ffn_wv", "L0_ffn_wo"]):
                load(ffn_w[:, n, :], i[name])
            load(w1[:, :], i["L0_ffn_w1"])
            load(w2[:, :, :], i["L0_ffn_w2"].rearrange("(c p) n -> p c n", p=P))
            for n, name in enumerate(["L1_attn_Wq", "L1_attn_Wk", "L1_attn_Wv", "L1_attn_Wo"]):
                load(attn_w[:, n, :], i[name])
            for n, name in enumerate(["L1_attn_bq", "L1_attn_bk"]):
                load(qk_bias[:, n:n + 1], i[name].rearrange("(p a) -> p a", a=1))
            for n, name in enumerate(["L1_attn_bv", "L1_attn_bo"]):
                load(vo_bias[:, n, :], i[name].rearrange("(a n) -> a n", a=1).broadcast_to([P, D]))
            load(router1[:, :], i["L1_ffn_router_w"].rearrange("e d -> d e"))
            load(experts[:, :, :], i["L1_ffn_expert_weights"].rearrange("e h o -> h e o"))

            w_heads = i["L0_attn_w_qkv"].rearrange("e h n -> h e n")
            w_pairs = i["L0_attn_w_qkv"].rearrange("e (p h) n -> p e h n", h=2)

            def load_weights(p, q, first):
                if not first:
                    sp.wait_ge(sem("v_proj"), 2 * p - 2)
                sp.dma_start(w_v[q][:, :].rearrange("e (h d) -> e h d", h=2), w_pairs[p, :, :, 2 * HD0:]).then_inc(sem(f"w_pair{q}"), 16)
                for s in range(2):
                    if not (first and q == 0):
                        sp.wait_ge(sem("qk_proj"), 4 * p - 2 + 2 * s)
                    sp.dma_start(w_qk[s][:, :], w_heads[2 * p + s, :, 0:2 * HD0]).then_inc(sem(f"w_pair{q}"), 16)

            with sp.Fori(0, B) as b:
                sp.dma_start(x[:, :, :], i["L0_attn_x"][b, :, :].rearrange("(t p) d -> p t d", p=P)).then_inc(sem("x_in"), 16)
                sp.dma_start(pair_rows[:, :, :], pair_dram[:]).then_inc(sem("pair_rows"), 16)
                load_weights(0, 0, True)
                load_weights(1, 1, True)
                with sp.Fori(0, NP // 2 - 1) as g:
                    for q in range(2):
                        load_weights(2 * g + 2 + q, q, False)
                for c in range(C):
                    sp.wait_ge(sem("den_zero"), 2)
                    sp.wait_ge(sem("den_stored"), 16 * (2 * NP - 1 + c))
                    sp.dma_start(inv_den[c][DEN_ROW:DEN_ROW + H, :], den_dram[c]).then_inc(sem("den_loaded"), 16)
                sp.wait_ge(sem("den_mm"), 2 * NP)
                sp.dma_start(mask_in[:, :, :], i["L0_ffn_attention_mask"][b, 0, :, :].rearrange("(c p) n -> p c n", p=P)).then_inc(sem("mask_in"), 16)
                to_stack(sp, 0)
                for r in range(T // 2):
                    sp.wait_ge(sem("x_final"), r + 1)
                    sp.dma_start(out[b, 2 * r * P:2 * (r + 1) * P, :].rearrange("(k p) d -> p k d", p=P), x[:, 2 * r:2 * r + 2, :]).then_inc(sem("stored"), 16)
                end_of_batch(sp, 1)
                sp.wait_ge(sem("stored"), 8 * T * b + 8 * T)
                sp.sem_inc(sem("x_free"), 1)

        N_SETUP_LOADS = 16 * len(SETUP_LOADS)

        @block.gpsimd
        def _(pool):
            def set_once(count, ap, value):
                if count:
                    pool.wait_ge(sem("setup_pool"), count)
                pool.memset(ap, value).then_inc(sem("setup_pool"), 1)

            fills = [(ones[:, :], 1.0)]
            for s in range(2):
                fills += [(qT[s][HD0:P, :], 0.0), (kT[s][HD0:P, :], 0.0), (kT[s][HD0:HD0 + 1, :], 1.0)]
            fills += [(q_bf[0][HD0:P, :], 0.0), (k_bf[0][HD0:P, :], 0.0), (part_max[:, 0:4, 1:2], -3e38),
                      (q_stack[:, :, :].rearrange("p h s -> p (h s)").bitcast(F32), 0.0)]
            for count, (ap, value) in enumerate(fills):
                set_once(count, ap, value)
            pool.wait_ge(sem("setup_pool"), len(fills))

            def cast_head(hh, s, slot):
                for c in range(C):
                    cols = slice(c * HALF, (c + 1) * HALF)
                    pool.wait_ge(sem("s_mm"), NI * hh - NI)
                    pool.wait_ge(sem("q_evac"), 2 * hh + c + 1)
                    pool.sem_inc(sem("cast_go"), 1)
                    pool.tensor_copy(q_bf[s][0:HD0, cols], qT[slot][0:HD0, cols]).then_inc(sem("qb_cast"), 1)
                    pool.wait_ge(sem("k_evac"), 2 * hh + c + 1)
                    pool.sem_inc(sem("cast_go"), 1)
                    pool.tensor_copy(k_bf[s][0:HD0, cols], kT[slot][0:HD0, cols]).then_inc(sem("kb_cast"), 1)

            with pool.Fori(0, B) as b:
                pool.memset(pickT[HD0:P, :], 0.0).then_inc(sem("slots_clear"), 1)
                pool.wait_ge(sem("slots_clear"), 1)
                pool.memset(stack_f32[HD0:P, 4 * S:8 * S], 0.0).then_inc(sem("slots_clear"), 1)
                pool.wait_ge(sem("slots_clear"), 2)
                pool.memset(stack_f32[HD0:HD0 + 1, 6 * S:8 * S], 1.0).then_inc(sem("slots_clear"), 1)
                pool.wait_ge(sem("slots_clear"), 3)
                with pool.Fori(0, NP // 2 - 1) as g:
                    for q in (1, 0):
                        for s in range(2):
                            cast_head(4 * g + 4 - 2 * q + s, s, 2 * q + s)
                for s in range(2):
                    cast_head(H - 2 + s, s, 2 + s)
                pool.wait_ge(sem("kb_cast"), 2 * H)
                pool.wait_ge(sem("attn0_mm"), 2)
                pool.memset(stack_f32[:, 4 * S:8 * S], 0.0).then_inc(sem("stack_clear"), 1)
                for par in range(2):
                    pool.wait_ge(sem("stack_clear"), par + 1)
                    pool.memset(q_stack[par * HM + M_ROW:par * HM + M_ROW + 2, par:8:2, :], 0.0).then_inc(sem("stack_clear"), 1)
                pool.wait_ge(sem("stack_clear"), 3)
                pool.memset(room[:, 0:4 * S], 0.0).then_inc(sem("k_clear"), 1)
                for par in range(2):
                    pool.wait_ge(sem("k_clear"), par + 1)
                    pool.memset(k_stack[par * HM + M_ROW:par * HM + M_ROW + 2, :, :], 1.0).then_inc(sem("k_clear"), 1)
                pool.wait_ge(sem("k_clear"), 3)
                for a in "qk":
                    for part in "hml":
                        pool.wait_ge(sem(f"scratch_{a}{part}"), 16)
                pool.memset(room[:, 4 * S:8 * S], 0.0).then_inc(sem("k_clear"), 1)
                pool.wait_ge(sem("k_clear"), 4)
                pool.memset(v1[:, :, :, HD:HD + 1], 1.0).then_inc(sem("k_clear"), 1)
                pool.wait_ge(sem("k_clear"), 5)
                clear_share(pool, 0)
                pool.wait_ge(sem("batch_shares"), ENGINES)
                pool.sem_clear(arrived)
                pool.sem_clear(sem("batch_shares"))
                pool.drain()
                pool.sem_inc(cleared, 1)
                pool.wait_ge(left, 4)
                pool.sem_clear(left)
                pool.sem_clear(cleared)

        @block.scalar
        def _(act):
            act.wait_ge(sem("setup_loads"), N_SETUP_LOADS)
            act.activation(c_den[:, :, :], c_raw[:, :, :], ACT.Exp, scale=-1.0).then_inc(sem("setup_c_exp"), 1)
            act.wait_ge(sem("setup_dve"), 1)
            act.activation(trig[:, :, :, :, :].rearrange("p a b c f -> p (a b c f)"), angle[:, :, :, :].rearrange("p a n f -> p (a n f)"), ACT.Sin).then_inc(sem("setup_trig"), 1)

            def copy(dst, src):
                return act.activation(dst, src, ACT.Copy)

            def evac_hT(name, b, l, shift, scale1):
                for c in range(C):
                    act.wait_ge(sem(name + "_tr"), c + 1)
                    act.activation(hT[:, c * HALF:(c + 1) * HALF], bank[6 + c][:, :], ACT.Identity,
                                   bias=mod_col[:, l, shift, bass.ds(b, 1)], scale=mod_col[:, l, scale1, bass.ds(b, 1)]).then_inc(sem(name + "_hT"), 1)

            def queries(hh, s, slot, first):
                for c in range(C):
                    act.wait_ge(sem("qk_proj"), 2 * hh + c + 1)
                    if first:
                        copy(q_bf[s][0:HD0, c * HALF:(c + 1) * HALF], bank[6 + c][0:HD0, :]).then_inc(sem("qb_cast"), 1)
                    copy(qT[slot][0:HD0, c * HALF:(c + 1) * HALF], bank[6 + c][0:HD0, :]).then_inc(sem("q_evac"), 1)

            def values(p, q, c):
                act.wait_ge(sem("v_proj"), 2 * p + c + 1)
                copy(v0[q][:, 4 * c:4 * c + 4, :], bank[6 + c][:, :].rearrange("p (t d) -> p t d", t=4)).then_inc(sem("v_evac"), 1)

            def max_to_queries(hh, slot, c):
                act.wait_ge(sem("mrow_mm"), 2 * hh + c + 1)
                copy(qT[slot][HD0:HD0 + 1, c * HALF:(c + 1) * HALF], bank[6 + c][HD0:HD0 + 1, :]).then_inc(sem("mrow_evac"), 1)

            def sums_out(p, c):
                act.wait_ge(sem("den_mm"), 2 * p + c + 1)
                if not (isinstance(p, int) and p == 0 and c == 0):
                    act.wait_ge(sem("den_stored"), 16 * (2 * p + c))
                copy(den_rows[c][0:33, :], bank[1 - c][0:33, :]).then_inc(sem("den_evac"), 1)

            def store_sums(p, c):
                act.wait_ge(sem("den_evac"), 2 * p + c + 1)
                dst = den_dram.rearrange("c (p s) n -> p c s n", s=2)
                act.dma_start(dst[p, c], den_rows[c][0:33:32, :]).then_inc(sem("den_stored"), 16)

            def exps(p, q, nxt, first=False):
                for n, (c, j, lo) in enumerate(EXP_ITEMS):
                    for s in range(2):
                        act.wait_ge(sem("st_mm"), 2 * NI * p + 2 * n + s + 1)
                        if j == 0:
                            if not first:
                                act.wait_ge(sem("den_mm"), 2 * p - 1 + c)
                            dst = p_sum[s][c][:, :]
                        else:
                            if not (first and RING_BEFORE[n] < 0):
                                act.wait_ge(sem("pv"), NI * p + RING_BEFORE[n] + 1)
                                if RING_BEFORE[n] >= 0:
                                    act.wait_ge(sem("added"), 20 * p + 2 * ADDED[RING_BEFORE[n]])
                                else:
                                    act.wait_ge(sem("added"), 20 * p - 20 + 2 * ADDED[RING_BEFORE[n] + NI])
                            dst = probs[2 * (n % 2) + s][:, 0:HALF - lo]
                        act.activation(dst, bank[2 + s][:, lo:HALF], ACT.Exp, scale=SCALE0).then_inc(sem("expd"), 1)
                    if n == 0:
                        max_to_queries(2 * p + 1, 2 * q + 1, 1)
                        if not first:
                            store_sums(p - 1, 0)
                    if not first:
                        if n == DENS_AT[1] + 1:
                            sums_out(p - 1, 1)
                        if n == DENS_AT[1] + 3:
                            store_sums(p - 1, 1)
                    if nxt:
                        if n - 1 in PROJECT_AT:
                            s = PROJECT_AT[n - 1]
                            queries(2 * p + 2 + s, s, 2 * (1 - q) + s, False)
                        if n - 1 == VALUES_AT:
                            for c_ in range(C):
                                values(p + 1, 1 - q, c_)
                        if n - 1 in ROWS_AFTER:
                            if first:
                                act.wait_ge(sem("slots_clear"), 3)
                            for c_ in range(C):
                                max_to_queries(2 * p + 2, 2 * (1 - q), c_)
                        if n == NI - 1:
                            max_to_queries(2 * p + 3, 2 * (1 - q) + 1, 0)
                            sums_out(p, 0)
                    else:
                        if n == LAST_DEN_AT + 1:
                            sums_out(p, 0)
                        if n == LAST_DEN_AT + 2:
                            store_sums(p, 0)
                if not nxt:
                    sums_out(p, 1)
                    store_sums(p, 1)

            with act.Fori(0, B) as b:
                evac_hT("ln_a", b, 0, 0, 1)
                for l in range(2):
                    for a in range(2):
                        act.wait_ge(sem("mod_mm"), 2 * l + a + 1)
                        copy(mod[:, l, 3 * a:3 * a + 3, :].rearrange("p a d -> p (a d)"), bank[2 * l + a][:, 0:3 * D]).then_inc(sem("mod_evac"), 1)
                for s in range(2):
                    queries(s, s, s, True)
                for c in range(C):
                    values(0, 0, c)
                for c in range(C):
                    max_to_queries(0, 0, c)
                max_to_queries(1, 1, 0)
                exps(0, 0, True, first=True)
                with act.Fori(0, NP // 2 - 1) as g:
                    for q in (1, 0):
                        exps(2 * g + 2 - q, q, True)
                exps(NP - 1, 1, False)
                evac_hT("ln_b", b, 0, 3, 4)
                for c in range(C):
                    act.wait_ge(sem("w_mm"), c + 1)
                    act.activation(w_row[:, c * HALF:(c + 1) * HALF], bank[1 + c][:, :], ACT.Identity, bias=router0_b[:, 0:1]).then_inc(sem("w_row"), 1)
                for c in range(C):
                    act.wait_ge(sem("pickT_tr"), c + 1)
                    copy(pickT[:, c * HALF:(c + 1) * HALF], bank[1 + c][:, :]).then_inc(sem("pickT"), 1)
                act.wait_ge(sem("select_mm"), 1)
                copy(mask_rows[:, :, :], bank[0][:, :].rearrange("p (c s) -> p c s", c=MC)).then_inc(sem("mask_rows"), 1)
                act.wait_ge(sem("hn_tr"), 1)
                copy(hnT[:, :], bank[4][:, 0:SLOTS]).then_inc(sem("hnT"), 1)
                act.wait_ge(sem("select_mm"), 2)
                copy(trig_sel[:, :, :], bank[2][:, 0:2 * SLOTS].rearrange("p (a s) -> p a s", a=2)).then_inc(sem("trig_sel"), 1)
                act.wait_ge(sem("qkv_s_mm"), 1)
                copy(qk_s[:, :, :], bank[5][:, 0:2 * SLOTS].rearrange("p (a s) -> p a s", a=2)).then_inc(sem("qk_s"), 1)
                act.wait_ge(sem("qkv_s_mm"), 2)
                copy(v_s[:, :], bank[6][:, 0:D]).then_inc(sem("v_s"), 1)
                for n in range(5):
                    if n < 4:
                        act.wait_ge(sem("sc_max"), n + 1)
                        for hh in range(4 * n, 4 * n + 4):
                            ins = act.activation(sc[:, hh, :], sc[:, hh, :], ACT.Exp, bias=sc_max[:, hh:hh + 1], accum_out=sc_sum[:, hh:hh + 1])
                        ins.then_inc(sem("sc_exp"), 1)
                    if n:
                        act.wait_ge(sem("p_tr"), n)
                        copy(pT[:, 4 * n - 4:4 * n, :], bank[3 + n][:, :].rearrange("p (a s) -> p a s", a=4)).then_inc(sem("pT"), 1)
                act.wait_ge(sem("o_s_tr"), 1)
                copy(o_sT[:, :], bank[1][:, 0:SLOTS]).then_inc(sem("o_sT"), 1)
                act.wait_ge(sem("hn_tr"), 2)
                copy(hnT[:, :], bank[3][:, 0:SLOTS]).then_inc(sem("hnT"), 1)
                act.wait_ge(sem("w1_mm"), 1)
                act.activation(gelu[:, :, :], bank[4][:, :].rearrange("p (c s) -> p c s", c=FC), ACT.Gelu_apprx_tanh).then_inc(sem("gelu"), 1)
                evac_hT("ln_c", b, 1, 0, 1)
                for n in range(2):
                    for c in range(C):
                        act.wait_ge(sem("qk1_mm"), 2 * n + c + 1)
                        act.activation(qk_f[:, n, c * HALF:(c + 1) * HALF], bank[2 * n + c][:, :], ACT.Identity, bias=qk_bias[:, n:n + 1]).then_inc(sem("qk1"), 1)

                for k in range(5):
                    for part, m in (("h", k), ("m", k - 1)):
                        if 0 <= m < 4:
                            n, c = divmod(m, C)
                            act.wait_ge(sem("rope1" if part == "h" else "rest1"), m + 1)
                            copy(split["qk"[n]][part][:, c * HALF:(c + 1) * HALF], qk_f[:, n, c * HALF:(c + 1) * HALF]).then_inc(sem("split_" + part), 1)

                to_stack(act, 1)

                def max_row(u, a):
                    r = (a % 2) * HM + M_ROW
                    act.wait_ge(sem("mrow1_mm"), GH * u + a + 1)
                    copy(q_stack[r:r + 2, GH * (u // C) + a, (u % C) * HALF:(u % C + 1) * HALF], bank[6][ROW_AT[a]:ROW_AT[a] + 2, :]).then_inc(sem("mrow1"), 1)

                for n in range(-UI, NI1):
                    if n >= 0:
                        act.wait_ge(sem("st1_mm"), n + 1)
                        if n >= 8:
                            act.wait_ge(sem("pv1"), n // GH - 1)
                        act.activation(ring1[n % 8][:, :], bank[ST1_BANK[n % 3]][:, :], ACT.Exp, scale=SCALE).then_inc(sem("expd1"), 1)
                    for a in range(GH):
                        if n - 1 - a in ROWS_AT:
                            max_row(ROWS_AT[n - 1 - a], a)
                for c in range(C):
                    act.wait_ge(sem("ctx_tr"), c + 1)
                    copy(ctxT[:, c * HALF:(c + 1) * HALF], bank[c][:, :]).then_inc(sem("ctxT"), 1)
                evac_hT("ln_d", b, 1, 3, 4)
                act.wait_ge(sem("lg_sub"), 1)
                act.activation(lg[:, :, :], lg[:, :, :], ACT.Exp).then_inc(sem("lg_exp"), 1)
                act.wait_ge(sem("coef"), 2)
                for t in range(T):
                    if t >= 4:
                        act.wait_ge(sem("moe"), t - 3)
                    for e in range(E):
                        if e % 4 == 0:
                            act.wait_ge(sem("ex_mm"), 2 * t + e // 4 + 1)
                        src = bank[(2 * t + 4) % 8 + e // 4][:, (e % 4) * D:(e % 4 + 1) * D]
                        bias = bias_tok[:, t:t + 1] if e == 0 else 0.0
                        act.activation(prod[:, t % 4, e, :], src, ACT.Identity, bias=bias, scale=coef[:, t, e:e + 1]).then_inc(sem("prod"), 1)
                end_of_batch(act, 2)

        @block.tensor
        def _(pe):
            def mm(dst, lhsT, rhs, start=True, stop=True):
                return pe.matmul(dst, lhsT, rhs, start=start, stop=stop)

            pe.wait_ge(sem("setup_pool"), 11)
            pe.wait_ge(sem("setup_dve"), 1)
            pe.wait_ge(sem("setup_masks"), 6)
            for l in range(2):
                for a in range(6):
                    last = mm(bank[0][:, (6 * l + a) * B:(6 * l + a + 1) * B], wmod[:, l, a * D:(a + 1) * D], silu_c[:, l, :])
            last.then_inc(sem("setup_mod_mm"), 1)

            def transpose_h(name):
                for c in range(C):
                    for t in range(4 * c, 4 * c + 4):
                        pe.wait_ge(sem(name + "_h"), t + 1)
                        last = pe.transpose(bank[6 + c][:, (t % 4) * P:(t % 4 + 1) * P], h[:, t, :], eye)
                    last.then_inc(sem(name + "_tr"), 1)

            def project(hh, p, s, q):
                if s == 0:
                    pe.wait_ge(sem(f"w_pair{q}"), 48 * ((p - q) // 2 + 1))
                for c in range(C):
                    if s:
                        pe.wait_ge(sem("q_evac"), 2 * hh - 1 + c)
                        pe.wait_ge(sem("k_evac"), 2 * hh - 1 + c)
                    elif not (isinstance(p, int) and p == 0):
                        pe.wait_ge(sem("mrow_evac"), 2 * hh - 1 + c)
                    mm(bank[6 + c][:, :], w_qk[s][:, :], hT[:, c * HALF:(c + 1) * HALF]).then_inc(sem("qk_proj"), 1)

            def project_v(p, q):
                for c in range(C):
                    pe.wait_ge(sem("q_evac"), 4 * p + 3 + c)
                    pe.wait_ge(sem("k_evac"), 4 * p + 3 + c)
                    for t in range(4 * c, 4 * c + 4):
                        last = mm(bank[6 + c][:, (t % 4) * P:(t % 4 + 1) * P], hT[:, t * P:(t + 1) * P], w_v[q][:, :])
                    last.then_inc(sem("v_proj"), 1)

            def max_item(hh, s, n, first, p=0):
                t, c, w = MAX_ITEMS[n]
                dst = bank[n % 2]
                pe.wait_ge(sem("qb_cast"), 2 * hh + t // 4 + 1)
                pe.wait_ge(sem("kb_cast"), 2 * hh + c + 1)
                if not (first and s == 0 and n < 2):
                    pe.wait_ge(sem("row_max"), NI * hh + n - 1)
                if s == 0 and n < 2 and not (isinstance(p, int) and p == 0):
                    pe.wait_ge(sem("den_evac"), 2 * p)
                diag = c == t // 4
                last = mm(dst[:, 0:w], q_bf[s][:, t * P:(t + 1) * P], k_bf[s][:, c * HALF:c * HALF + w], stop=not diag)
                if diag:
                    last = mm(dst[:, w - P:w], eye_bf[:, :], mask_q[:, :], start=False)
                last.then_inc(sem("s_mm"), 1)

            def max_to_row(hh, p):
                pe.wait_ge(sem("neg_max"), hh + 1)
                pe.wait_ge(sem("v_evac"), 2 * p + 2)
                if not (isinstance(hh, int) and hh == 0):
                    pe.wait_ge(sem("mrow_evac"), 2 * hh)
                for c in range(C):
                    for t in range(4):
                        last = mm(bank[6 + c][HD0:HD0 + 1, t * P:(t + 1) * P], neg_max[:, 4 * c + t:4 * c + t + 1], eye)
                    last.then_inc(sem("mrow_mm"), 1)

            def st_item(p, q, s, n, first):
                c, j, lo = EXP_ITEMS[n]
                dst = bank[2 + s]
                if j == 0:
                    pe.wait_ge(sem("mrow_evac"), 4 * p + 2 * s + c + 1)
                if not (first and n == 0):
                    pe.wait_ge(sem("expd"), 2 * NI * p + 2 * n + s - 1)
                diag = j * P >= c * HALF
                slot = 2 * q + s
                last = mm(dst[:, lo:], kT[slot][:, j * P:(j + 1) * P], qT[slot][:, c * HALF + lo:(c + 1) * HALF], stop=not diag)
                if diag:
                    last = mm(dst[:, lo:lo + P], eye_bf[:, :], mask_k[:, :], start=False)
                last.then_inc(sem("st_mm"), 1)

            def pv_item(p, q, n, first):
                c, j, lo = EXP_ITEMS[n]
                pe.wait_ge(sem("expd"), 2 * NI * p + 2 * n + 2)
                if j == 0 and not first:
                    pe.wait_ge(sem("o_out"), 2 * p - 1 + c)
                for s in range(2):
                    rhs = p_sum[s][c][:, :] if j == 0 else probs[2 * (n % 2) + s][:, 0:HALF - lo]
                    last = mm(bank[4 + c][s * HD0:(s + 1) * HD0, lo:], v0[q][:, j, s * HD0:(s + 1) * HD0], rhs, start=j == 0, stop=j == 4 * c + 3)
                last.then_inc(sem("pv"), 1)

            def sums(p, c):
                pe.wait_ge(sem("added"), 20 * p + (2 * ADDED[3] if c == 0 else 20))
                for s in range(2):
                    last = mm(bank[1 - c][32 * s:32 * s + 1, :], ones[:, 0:1], p_sum[s][c][:, :])
                last.then_inc(sem("den_mm"), 1)

            def inv_to_rows(c, g):
                if g == 0:
                    pe.wait_ge(sem("inv_den"), c + 1)
                    pe.wait_ge(sem("den_evac"), 2 * NP - 1 + c)
                n = c * (H // 2) + g
                if n >= 2:
                    pe.wait_ge(sem("o_norm"), n - 1)
                mm(bank[n % 2][:, :], pair_rows[:, g, :], inv_den[c][:, :]).then_inc(sem("inv_rows"), 1)

            def pair(p, q, nxt, first=False):
                def max_at(n, k):
                    if nxt and n in MAX_AT:
                        s, items = MAX_AT[n]
                        max_item(2 * p + 2 + s, s, items[k], False, p)

                for n in range(NI):
                    if n + 1 < NI:
                        for s in range(2):
                            st_item(p, q, s, n + 1, first)
                            max_at(n, s)
                    if n == DENS_AT[1] and not first:
                        sums(p - 1, 1)
                    if nxt:
                        if n in PROJECT_AT:
                            s = PROJECT_AT[n]
                            project(2 * p + 2 + s, p + 1, s, 1 - q)
                        if n == VALUES_AT:
                            project_v(p + 1, 1 - q)
                        if n == NI - 1:
                            if first:
                                pe.wait_ge(sem("slots_clear"), 3)
                            st_item(p + 1, 1 - q, 0, 0, False)
                        if n in ROWS_AFTER:
                            max_to_row(2 * p + 2 + ROWS_AFTER[n], p + 1)
                    elif n == LAST_DEN_AT:
                        pe.wait_ge(sem("row_max"), NI * H)
                        sums(p, 0)
                    pv_item(p, q, n, first)
                    max_at(n, 2)
                    if nxt and n == DENS_AT[0]:
                        pe.wait_ge(sem("row_max"), NI * (2 * p + 4))
                        sums(p, 0)
                    if nxt and n == NI - 1:
                        st_item(p + 1, 1 - q, 1, 0, False)
                    if not nxt:
                        for g in LAST_ROWS_AT.get(n, ()):
                            inv_to_rows(0, g)
                if not nxt:
                    pe.wait_ge(sem("o_norm"), NP)
                    sums(p, 1)

            with pe.Fori(0, B) as b:
                for l in range(2):
                    pe.wait_ge(sem("cond"), l + 1)
                    for a in range(2):
                        mm(bank[2 * l + a][:, 0:3 * D], cond[:, l, :], wmod[:, l, 3 * a * D:3 * (a + 1) * D]).then_inc(sem("mod_mm"), 1)
                transpose_h("ln_a")
                pe.wait_ge(sem("ln_a_hT"), 2)
                for s in range(2):
                    project(s, 0, s, 0)
                project_v(0, 0)
                pe.wait_ge(sem("mod_evac"), 2)
                for s in range(2):
                    if s:
                        pe.wait_ge(sem("slots_clear"), 1)
                    for n in range(NI):
                        max_item(s, s, n, True)
                    max_to_row(s, 0)
                pe.wait_ge(sem("mod_evac"), 4)
                for s in range(2):
                    st_item(0, 0, s, 0, True)
                pair(0, 0, True, first=True)
                with pe.Fori(0, NP // 2 - 1) as g:
                    for q in (1, 0):
                        pair(2 * g + 2 - q, q, True)
                pair(NP - 1, 1, False)
                pe.wait_ge(sem("expd"), NI * H)
                for c in range(C):
                    for g in range(H // 2):
                        if c == 1:
                            inv_to_rows(1, g)
                    for t in range(4 * c, 4 * c + 4):
                        for g in range(H // 2):
                            pe.wait_ge(sem("o_norm"), 8 * c + g + 1)
                            last = mm(bank[2 + c][:, (t % 4) * P:(t % 4 + 1) * P], oT[:, g, t * P:(t + 1) * P], w_out0[:, g, :], start=g == 0, stop=g == H // 2 - 1)
                    last.then_inc(sem("attn0_mm"), 1)
                transpose_h("ln_b")
                for c in range(C):
                    pe.wait_ge(sem("ln_b_hT"), c + 1)
                    mm(bank[1 + c][:, :], router0_rep[:, :], hT[:, c * HALF:(c + 1) * HALF]).then_inc(sem("w_mm"), 1)
                pe.wait_ge(sem("res_a"), 2)
                for u in range(1, T):
                    pe.wait_ge(sem("larger"), u)
                    for t in range(u):
                        last = mm(bank[3][:, u:u + 1], larger[t][:, (u - t) * P:(u - t + 1) * P], ones_bf[:, 0:1], start=t == 0, stop=t == u - 1)
                last.then_inc(sem("not_before"), 1)
                pe.wait_ge(sem("thr_part"), 1)
                mm(bank[3][:, 0:1], ones[:, :], thr_part[:, :]).then_inc(sem("slot_mm"), 1)
                pe.wait_ge(sem("sel"), 1)
                last = mm(bank[4][:, 0:T], before_bf[:, :], sel_bf[:, :], stop=False)
                for t in range(T - 1):
                    last = mm(bank[4][:, t + 1:T], ones_bf[:, :], sel_bf[:, t:t + 1].to_broadcast([P, T - 1 - t]), start=False, stop=t == T - 2)
                last.then_inc(sem("slot_mm"), 1)
                pe.wait_ge(sem("pick"), T)
                for t in range(T):
                    last = mm(bank[5][:, 0:D + 2], pick[:, t, :], h_room[:, t, :], start=t == 0, stop=t == T - 1)
                last.then_inc(sem("gather_mm"), 1)
                pe.wait_ge(sem("idx"), 1)
                pe.transpose(bank[7][:, 0:SLOTS], ws_idx[:, 1:2].to_broadcast([P, P]), eye).then_inc(sem("idx_tr"), 1)
                for c in range(C):
                    for t in range(4 * c, 4 * c + 4):
                        last = pe.transpose(bank[1 + c][:, (t % 4) * P:(t % 4 + 1) * P], pick[:, t, :], eye)
                    last.then_inc(sem("pickT_tr"), 1)
                pe.wait_ge(sem("mask_pick"), MC)
                pe.wait_ge(sem("mask_in"), 16)
                for c in range(MC):
                    for r in range(MC):
                        last = mm(bank[0][:, c * P:(c + 1) * P], mask_in[:, r, c * P:(c + 1) * P], mask_pick[:, r, :], start=r == 0, stop=r == MC - 1)
                last.then_inc(sem("select_mm"), 1)
                pe.wait_ge(sem("hn"), 1)
                pe.wait_ge(sem("slot_of"), 1)
                pe.transpose(bank[4][:, 0:SLOTS], hn[:, :], eye).then_inc(sem("hn_tr"), 1)
                pe.wait_ge(sem("trig_rep"), 2)
                pe.wait_ge(sem("pickT"), 2)
                for a in range(2):
                    for c in range(MC):
                        last = mm(bank[2][:, a * SLOTS:(a + 1) * SLOTS], trig_rep[:, a, c, :, :].rearrange("p h d -> p (h d)"), mask_pick[:, c, :], start=c == 0, stop=c == MC - 1)
                last.then_inc(sem("select_mm"), 1)
                pe.wait_ge(sem("hnT"), 1)
                for n in range(2):
                    last = mm(bank[5][:, n * SLOTS:(n + 1) * SLOTS], ffn_w[:, n, :], hnT[:, :])
                last.then_inc(sem("qkv_s_mm"), 1)
                mm(bank[6][:, 0:D], hnT[:, :], ffn_w[:, 2, :]).then_inc(sem("qkv_s_mm"), 1)
                pe.wait_ge(sem("qk_s"), 1)
                pe.wait_ge(sem("idx"), 2)
                mm(bank[7][:, 0:2 * SLOTS], const("rot0"), qk_s[:, :, :].rearrange("p a s -> p (a s)")).then_inc(sem("rot0_mm"), 1)
                pe.wait_ge(sem("mask_rows"), 1)
                for c in range(MC):
                    last = mm(bank[1][:, 0:SLOTS], mask_rows[:, c, :], mask_pick[:, c, :], start=c == 0, stop=c == MC - 1)
                last.then_inc(sem("select_mm"), 1)
                pe.wait_ge(sem("mask_sel"), 1)
                pe.wait_ge(sem("trig_sel"), 1)
                for n in range(4):
                    pe.wait_ge(sem("k_diag"), n + 1)
                    mm(bank[n][:, :], qk_s[:, 0, :], k_diag[:, 4 * n:4 * n + 4, :].rearrange("p a s -> p (a s)")).then_inc(sem("sc_mm"), 1)
                pe.wait_ge(sem("v_s"), 1)
                pe.wait_ge(sem("rot_s"), 1)
                for n in range(5):
                    if n < 4:
                        pe.wait_ge(sem("sc_exp"), n + 1)
                        for a in range(4):
                            last = pe.transpose(bank[4 + n][:, a * P:(a + 1) * P], sc[:, 4 * n + a, :], eye)
                        last.then_inc(sem("p_tr"), 1)
                    if n:
                        pe.wait_ge(sem("pT"), n)
                        for hh in range(4 * n - 4, 4 * n):
                            last = mm(bank[0][:, hh * HD:(hh + 1) * HD], pT[:, hh, :], v_s[:, hh * HD:(hh + 1) * HD])
                last.then_inc(sem("o_s_mm"), 1)
                pe.wait_ge(sem("o_s"), 1)
                pe.transpose(bank[1][:, 0:SLOTS], o_s[:, :], eye).then_inc(sem("o_s_tr"), 1)
                pe.wait_ge(sem("o_sT"), 1)
                mm(bank[2][:, 0:D], o_sT[:, :], ffn_w[:, 3, :]).then_inc(sem("wo_mm"), 1)
                pe.wait_ge(sem("hn"), 2)
                pe.transpose(bank[3][:, 0:SLOTS], hn[:, :], eye).then_inc(sem("hn_tr"), 1)
                pe.wait_ge(sem("hnT"), 2)
                for c in range(FC):
                    last = mm(bank[4][:, c * SLOTS:(c + 1) * SLOTS], w1[:, c * P:(c + 1) * P], hnT[:, :])
                last.then_inc(sem("w1_mm"), 1)
                pe.wait_ge(sem("gelu"), 1)
                for c in range(FC):
                    last = mm(bank[5][:, 0:D], gelu[:, c, :], w2[:, c, :], start=c == 0, stop=c == FC - 1)
                last.then_inc(sem("w2_mm"), 1)
                pe.wait_ge(sem("proc"), 1)
                for c in range(C):
                    for t in range(4 * c, 4 * c + 4):
                        last = mm(bank[c][:, (t % 4) * P:(t % 4 + 1) * P], pickT[:, t * P:(t + 1) * P], proc[:, :])
                    last.then_inc(sem("scatter_mm"), 1)
                transpose_h("ln_c")
                pe.wait_ge(sem("ln_c_hT"), 2)
                pe.wait_ge(sem("res_b"), 2)
                def project1(k):
                    n, c = divmod(k, C)
                    mm(bank[k][:, :], attn_w[:, n, :], hT[:, c * HALF:(c + 1) * HALF]).then_inc(sem("qk1_mm"), 1)

                def rotate1(k):
                    n, c = divmod(k, C)
                    pe.wait_ge(sem("qk1"), k + 1)
                    mm(bank[4 + k][:, :], const("rot1"), qk_f[:, n, c * HALF:(c + 1) * HALF]).then_inc(sem("rot1_mm"), 1)

                project1(0)
                project1(1)
                for k in range(4):
                    rotate1(k)
                    if k < 2:
                        project1(k + 2)
                pe.wait_ge(sem("rot1_done"), 3)
                for c in range(C):
                    for t in range(4 * c, 4 * c + 4):
                        last = mm(bank[4 + 2 * c][:, (t % 4) * P:(t % 4 + 1) * P], hT[:, t * P:(t + 1) * P], attn_w[:, 2, :])
                    last.then_inc(sem("v1_mm"), 1)
                pe.wait_ge(sem("stacks"), 16 * 4 * len(TERMS))
                pe.wait_ge(sem("rot1_done"), 4)

                def max1_item(m):
                    u, t, hh, c = max_item1(m)
                    if m >= 3:
                        pe.wait_ge(sem("row_max1"), m - 2)
                    mm(bank[MAX1_BANK[m % 3]][:, :], q_stack[:, hh, t * P:(t + 1) * P], k_stack[:, hh // 2, c * HALF:(c + 1) * HALF]).then_inc(sem("s1_mm"), 1)

                def max1_to_rows(u):
                    pe.wait_ge(sem("nmax_hl"), u + 1)
                    if u >= 2:
                        pe.wait_ge(sem("ctx1"), u - 1)
                    for a in range(GH):
                        r = ROW_AT[a]
                        for t in range(4):
                            last = pe.matmul(bank[6][r:r + 2, t * P:(t + 1) * P], nmax_hl[:, a, 4 * (u % C) + t, :], eye_bf[:, :], start=True, stop=True)
                        last.then_inc(sem("mrow1_mm"), 1)

                def st1_item(n):
                    u, j, hh = exp_item1(n)
                    if n % UI == 0:
                        pe.wait_ge(sem("mrow1"), GH * (u + 1))
                    if n >= 3:
                        pe.wait_ge(sem("expd1"), n - 2)
                    mm(bank[ST1_BANK[n % 3]][:, :], k_stack[:, hh // 2, j * P:(j + 1) * P], q_stack[:, hh, (u % C) * HALF:(u % C + 1) * HALF]).then_inc(sem("st1_mm"), 1)

                def pv1_items(k):
                    for n in range(GH * k, GH * k + GH):
                        u, j, hh = exp_item1(n)
                        a = hh % GH
                        pe.wait_ge(sem("expd1"), n + 1)
                        if n == 0:
                            pe.wait_ge(sem("v1"), 2)
                        if j == 0 and a == 0 and u:
                            pe.wait_ge(sem("o1_raw"), u)
                        last = mm(bank[4][32 * a:32 * a + 32, :], v1[:, j, hh, :], ring1[n % 8][:, :], start=j == 0, stop=j == T - 1)
                    last.then_inc(sem("pv1"), 1)

                def ctx_transposes(u):
                    pe.wait_ge(sem("o1_raw"), u + 1)
                    pe.wait_ge(sem("mrow1"), GH * min(u + 2, UNITS))
                    if u:
                        pe.wait_ge(sem("ctx1"), u)
                    for t in range(4):
                        last = pe.transpose(bank[6][:, t * P:(t + 1) * P], o_raw[u % C][:, t * P:(t + 1) * P], eye)
                    last.then_inc(sem("ctx_raw"), 1)

                for m in range(LEAD):
                    max1_item(m)
                    if m - LEAD + 1 in ROWS_AT:
                        max1_to_rows(ROWS_AT[m - LEAD + 1])
                st1_item(0)
                st1_item(1)
                for n in range(NI1):
                    if n + LEAD < NI1:
                        max1_item(n + LEAD)
                    if n + 2 < NI1:
                        st1_item(n + 2)
                    if n and n % GH == 0:
                        pv1_items(n // GH - 1)
                    if n > 0 and n in ROWS_AT:
                        max1_to_rows(ROWS_AT[n])
                    if n in CTX_AT:
                        ctx_transposes(CTX_AT[n])
                pv1_items(NI1 // GH - 1)
                ctx_transposes(UNITS - 1)
                for c in range(C):
                    pe.wait_ge(sem("ctx1"), UNITS - 1 + c)
                    for t in range(4 * c, 4 * c + 4):
                        last = pe.transpose(bank[c][:, (t % 4) * P:(t % 4 + 1) * P], ctx1[:, t, :], eye)
                    last.then_inc(sem("ctx_tr"), 1)
                for c in range(C):
                    pe.wait_ge(sem("ctxT"), c + 1)
                    for t in range(4 * c, 4 * c + 4):
                        last = mm(bank[2 + c][:, (t % 4) * P:(t % 4 + 1) * P], ctxT[:, t * P:(t + 1) * P], attn_w[:, 3, :])
                    last.then_inc(sem("attn1_mm"), 1)
                transpose_h("ln_d")
                pe.wait_ge(sem("ln_d_hT"), 2)
                for t in range(T):
                    last = mm(bank[0][:, t * E:(t + 1) * E], hT[:, t * P:(t + 1) * P], router1[:, :])
                last.then_inc(sem("lg_mm"), 1)
                pe.wait_ge(sem("res_c"), 2)
                for t in range(T):
                    if t == 2:
                        pe.wait_ge(sem("lg_sub"), 1)
                    for a in range(2):
                        if t >= 4:
                            pe.wait_ge(sem("prod"), E * (t - 4) + 4 * (a + 1))
                        mm(bank[(2 * t + 4) % 8 + a][:, :], hT[:, t * P:(t + 1) * P], experts[:, 4 * a:4 * a + 4, :].rearrange("p e d -> p (e d)")).then_inc(sem("ex_mm"), 1)
                end_of_batch(pe, 3)

        @block.vector
        def _(dve):
            links = {}

            def link(ins, s="dve_chain", base=0):
                links[s] = links.get(s, 0) + 1
                ins.then_inc(sem(s), 1)
                dve.wait_ge(sem(s), links[s])

            def tt(dst, a, b_, op):
                return dve.tensor_tensor(dst, a, b_, op)

            dve.wait_ge(sem("setup_loads"), N_SETUP_LOADS)
            dve.tensor_copy(eye_bf[:, :], eye).then_inc(sem("setup_masks"), 1)
            dve.memset(ones_bf[:, :], 1.0).then_inc(sem("setup_masks"), 1)
            dve.tensor_copy(before_bf[:, :], const("before")).then_inc(sem("setup_masks"), 1)
            dve.tensor_copy(router0_rep[:, :], router0[:, :].to_broadcast([P, P])).then_inc(sem("setup_masks"), 1)
            dve.tensor_copy(mask_q[:, :], const("mask_q")).then_inc(sem("setup_masks"), 1)
            dve.tensor_copy(mask_k[:, :], const("mask_k")).then_inc(sem("setup_masks"), 1)
            dve.wait_ge(sem("setup_c_exp"), 1)
            SC = "setup_chain"
            link(dve.tensor_scalar(c_den[:, :, :], c_den[:, :, :], 1.0, None, ALU.add), SC)
            link(dve.reciprocal(c_den[:, :, :], c_den[:, :, :]), SC)
            link(tt(silu_c[:, :, :], c_raw[:, :, :], c_den[:, :, :], ALU.mult), SC)
            link(dve.tensor_copy(pos_f[:, :], pos_int[:, :]), SC)
            link(tt(angle[:, 1, :, :], pos_f[:, :].unsqueeze(2).to_broadcast([P, B * MC, HD // 2]),
                    const("invf").unsqueeze(1).to_broadcast([P, B * MC, HD // 2]), ALU.mult), SC)
            link(dve.tensor_copy(angle[:, 0, :, :], angle[:, 1, :, :]), SC)
            round_to = 12582912.0
            for a in range(2):
                link(dve.tensor_scalar(turns[:, a, :, :], angle[:, a, :, :], 1.0 / (2.0 * np.pi), 0.25 * (1 - a), ALU.mult, ALU.add), SC)
            link(dve.tensor_scalar(turns[:, :, :, :], turns[:, :, :, :], round_to, None, ALU.add), SC)
            link(dve.tensor_scalar(turns[:, :, :, :], turns[:, :, :, :], -round_to, None, ALU.add), SC)
            two_pi = 2.0 * np.pi
            part1 = 6.28125
            part2 = float(np.float32(round((two_pi - part1) * 2 ** 21) / 2 ** 21))
            part3 = two_pi - part1 - part2
            tn, an = turns[:, :, :, :].rearrange("p a n f -> p (a n f)"), angle[:, :, :, :].rearrange("p a n f -> p (a n f)")
            for part in (part1, part2, part3):
                link(dve.scalar_tensor_tensor(an, tn, -part, an, ALU.mult, ALU.add), SC)
            link(dve.tensor_scalar(angle[:, 0, :, :], angle[:, 0, :, :], float(np.pi / 2), None, ALU.add), SC)
            link(dve.tensor_scalar(an, an, 3.1415925, -3.1415925, ALU.min, ALU.max), SC)
            dve.memset(extra[:, :, 0:1], 0.0).then_inc(sem("setup_dve"), 1)

            def rsqrt(dst, src, bits, t_):
                link(dve.tensor_scalar(bits, src.bitcast(I32), 1, None, ALU.logical_shift_right))
                link(dve.tensor_scalar(bits, bits, -1.0, RSQRT_MAGIC, ALU.mult, ALU.add))
                cur = bits.bitcast(F32)
                for _ in range(3):
                    link(dve.scalar_tensor_tensor(t_, cur, -0.5, cur, ALU.mult, ALU.mult))
                    link(tt(t_, t_, src, ALU.mult))
                    link(dve.scalar_tensor_tensor(dst, t_, 1.5, cur, ALU.add, ALU.mult))
                    cur = dst

            def layernorm(name, c):
                stat = sem(name + "_stats")
                half, tiles = slice(4 * c, 4 * c + 4), range(4 * c, 4 * c + 4)
                for t in tiles:
                    dve.bn_stats(stats[:, t, :], x[:, t, :]).then_inc(stat, 1)
                for t in tiles:
                    dve.wait_ge(stat, 4 * c + t + 1)
                    ins = dve.bn_aggr(mv[:, t, :], stats[:, t, :])
                    ins.then_inc(stat, 1)
                dve.wait_ge(stat, 8 * (c + 1))
                link(dve.tensor_scalar(nvar[:, half], mv[:, half, 1], LN_EPS, None, ALU.add))
                rsqrt(rstd[:, half], nvar[:, half], nbits[:, half], ntmp[:, half])
                for t in tiles:
                    dve.tensor_scalar(h[:, t, :], x[:, t, :], mv[:, t, 0:1], rstd[:, t:t + 1], ALU.subtract, ALU.mult).then_inc(sem(name + "_h"), 1)

            def residual(c, src, l, gate, done, bias=None):
                if c:
                    dve.wait_ge(sem(done), c)
                tv = tmp[:, :].rearrange("p (t d) -> p t d", t=4)
                sv = src[:, :].rearrange("p (t d) -> p t d", t=4)
                g_ = mod[:, l, gate, :].unsqueeze(1).to_broadcast([P, 4, D])
                if bias is not None:
                    link(tt(tv, sv, bias.unsqueeze(1).to_broadcast([P, 4, D]), ALU.add))
                    link(tt(tv, tv, g_, ALU.mult))
                else:
                    link(tt(tv, sv, g_, ALU.mult))
                xv = x[:, 4 * c:4 * c + 4, :]
                ins = tt(xv, xv, tv, ALU.add)
                ins.then_inc(sem(done), 1)

            def keys(hh, s, slot, first):
                for c in range(C):
                    dve.wait_ge(sem("qk_proj"), 2 * hh + c + 1)
                    if first:
                        dve.tensor_copy(k_bf[s][0:HD0, c * HALF:(c + 1) * HALF], bank[6 + c][HD0:P, :]).then_inc(sem("kb_cast"), 1)
                    dve.tensor_copy(kT[slot][0:HD0, c * HALF:(c + 1) * HALF], bank[6 + c][HD0:P, :]).then_inc(sem("k_evac"), 1)

            def row_max(hh, n):
                t, c, w = MAX_ITEMS[n]
                dve.wait_ge(sem("s_mm"), NI * hh + n + 1)
                dve.reduce_max(part_max[:, t, c:c + 1], bank[n % 2][:, 0:w], AX).then_inc(sem("row_max"), 1)

            def final_max(hh, first):
                dve.wait_ge(sem("row_max"), NI * hh + NI)
                if not first:
                    dve.wait_ge(sem("mrow_mm"), 2 * hh)
                dve.tensor_reduce(neg_max[:, :], part_max[:, :, :], AX, ALU.max, negate=True).then_inc(sem("neg_max"), 1)
                dve.wait_ge(sem("neg_max"), hh + 1)

            def add_up(p, n, s):
                c, j, lo = EXP_ITEMS[n]
                if j:
                    dve.wait_ge(sem("expd"), 2 * NI * p + 2 * n + s + 1)
                    if j == 1:
                        dve.wait_ge(sem("pv"), NI * p + n)
                    else:
                        dve.wait_ge(sem("added"), 20 * p + 2 * ADDED[n] - 3 + s)
                    sv = p_sum[s][c][:, lo:]
                    tt(sv, sv, probs[2 * (n % 2) + s][:, 0:HALF - lo], ALU.add).then_inc(sem("added"), 1)

            def contexts(p, c):
                dve.wait_ge(sem("pv"), NI * p + (4 if c == 0 else NI))
                dve.tensor_copy(oT[:, p, c * HALF:(c + 1) * HALF], bank[4 + c][:, :]).then_inc(sem("o_out"), 1)

            def invert_sums(c):
                dve.wait_ge(sem("den_loaded"), 16 * (c + 1))
                rows = inv_den[c][DEN_ROW:DEN_ROW + H, :]
                dve.reciprocal(rows, rows).then_inc(sem("inv_den"), 1)

            def o_norm(c, g):
                n = c * NP + g
                dve.wait_ge(sem("inv_rows"), n + 1)
                dve.wait_ge(sem("o_out"), 2 * NP - 1 + c)
                ov = oT[:, g, c * HALF:(c + 1) * HALF]
                tt(ov, ov, bank[n % 2][:, :], ALU.mult).then_inc(sem("o_norm"), 1)

            def pair(p, q, nxt):
                for n in range(NI):
                    if nxt and n - 1 in PROJECT_AT:
                        s = PROJECT_AT[n - 1]
                        keys(2 * p + 2 + s, s, 2 * (1 - q) + s, False)
                    s_max, items = MAX_AT[n] if nxt and n in MAX_AT else (0, ())
                    for k in range(3):
                        if items:
                            row_max(2 * p + 2 + s_max, items[k])
                            if items[k] == NI - 1:
                                final_max(2 * p + 2 + s_max, False)
                        if k < 2:
                            add_up(p, n, k)
                    if n == 5:
                        contexts(p, 0)
                    if not nxt and n == 7:
                        invert_sums(0)
                    if not nxt:
                        for g in LAST_ROWS_AT.get(n, ()):
                            o_norm(0, g)
                contexts(p, 1)

            dve.wait_ge(sem("setup_mod_mm"), 1)
            link(dve.tensor_copy(mod_col[:, :, :, :].rearrange("p l a b -> p (l a b)"), bank[0][:, 0:12 * B]), SC)
            link(dve.tensor_scalar(mod_col[:, :, 1::3, :], mod_col[:, :, 1::3, :], 1.0, None, ALU.add), SC)
            dve.wait_ge(sem("setup_trig"), 1)
            with dve.Fori(0, B) as b:
                links["dve_chain"] = 0
                for l in range(2):
                    dve.tensor_copy(cond[:, l, :], silu_c[:, l, bass.ds(b, 1)].to_broadcast([P, P])).then_inc(sem("cond"), 1)
                dve.wait_ge(sem("x_in"), 16)
                for c in range(C):
                    layernorm("ln_a", c)
                for s in range(2):
                    keys(s, s, s, True)
                for c in range(C):
                    dve.memset(inv_den[c][:, :], 0.0).then_inc(sem("den_zero"), 1)
                for s in range(2):
                    for n in range(NI):
                        row_max(s, n)
                    final_max(s, s == 0)
                pair(0, 0, True)
                for a in range(2):
                    for hf in range(2):
                        ins = dve.tensor_copy(trig_rep[:, a, :, :, hf * (HD // 2):(hf + 1) * (HD // 2)],
                                              trig[:, a, bass.ds(b, 1), :, :].rearrange("p o c f -> p (o c) f").unsqueeze(2).to_broadcast([P, MC, H, HD // 2]))
                    ins.then_inc(sem("trig_rep"), 1)
                dve.wait_ge(sem("mod_evac"), 4)
                gates = mod[:, :, 2::3, :]
                link(dve.scalar_tensor_tensor(gate_abs.rearrange("p l a d -> p (l a) d"), gates_view(gates), -1.0, gates_view(gates), ALU.mult, ALU.max))
                link(dve.tensor_scalar(gate_abs, gate_abs, 0.25, None, ALU.max))
                link(dve.tensor_scalar(gates, gates, 0.0, 2.0, ALU.is_ge, ALU.mult))
                link(dve.tensor_scalar(gates, gates, -1.0, None, ALU.add))
                link(tt(gates, gates, gate_abs, ALU.mult))
                scales = mod[:, :, 1::3, :]
                link(dve.tensor_scalar(scales, scales, 1.0, None, ALU.add))
                with dve.Fori(0, NP // 2 - 1) as g:
                    for q in (1, 0):
                        pair(2 * g + 2 - q, q, True)
                pair(NP - 1, 1, False)
                invert_sums(1)
                for g in range(H // 2):
                    o_norm(1, g)
                for c in range(C):
                    dve.wait_ge(sem("attn0_mm"), c + 1)
                    residual(c, bank[2 + c], 0, 2, "res_a")
                    dve.wait_ge(sem("res_a"), c + 1)
                    dve.wait_ge(sem("ln_a_tr"), 2)
                    layernorm("ln_b", c)
                dve.wait_ge(sem("ln_b_h"), T)
                dve.wait_ge(sem("ln_b_tr"), 2)
                mod_b = [mod[:, 0, a, :].unsqueeze(1).to_broadcast([P, T, D]) for a in (4, 3)]
                link(tt(h[:, :, :], h[:, :, :], mod_b[0], ALU.mult))
                link(tt(h[:, :, :], h[:, :, :], mod_b[1], ALU.add))
                for t in range(T):
                    dve.wait_ge(sem("w_row"), t // 4 + 1)
                    dve.scalar_tensor_tensor(ties[:, t, :], w_row[:, t * P:(t + 1) * P], 1.0, eye, ALU.mult, ALU.mult, accum_out=w_col[:, t:t + 1]).then_inc(sem("w_col"), 1)
                dve.wait_ge(sem("w_col"), T)
                link(dve.tensor_copy(extra[:, :, 0], w_col[:, :]))
                link(dve.tensor_copy(extra[:, :, 1], const("row")))
                for t in range(T):
                    wt = w_col[:, t:t + 1]
                    dve.tensor_scalar(larger[t], w_row[:, t * P:], wt, None, ALU.is_gt, ALU.add, accum_out=cnt[:, t, 0:1]).then_inc(sem("larger"), 1)
                for t in range(T):
                    wt = w_col[:, t:t + 1]
                    ins = dve.scalar_tensor_tensor(ties[:, t, :], w_row[:, t * P:(t + 1) * P], wt, const("lower"), ALU.is_equal, ALU.mult, accum_out=cnt[:, t, 1:2])
                    ins.then_inc(sem("larger"), 1)
                dve.wait_ge(sem("larger"), 2 * T)
                link(tt(rank[:, :], cnt[:, :, 0], cnt[:, :, 1], ALU.add))
                link(tt(rank[:, :], rank[:, :], const("tile"), ALU.add))
                dve.wait_ge(sem("not_before"), 1)
                link(tt(rank[:, 1:T], rank[:, 1:T], bank[3][:, 1:T], ALU.subtract))
                for dst in (sel_bf, sel):
                    dve.tensor_scalar(dst[:, :], rank[:, :], float(TOPK - 1), None, ALU.is_lt).then_inc(sem("sel"), 1)
                dve.scalar_tensor_tensor(tmp[:, 0:T], rank[:, :], float(TOPK - 1), w_col[:, :], ALU.is_equal, ALU.mult, accum_out=thr_part[:, :]).then_inc(sem("thr_part"), 1)
                dve.wait_ge(sem("slot_mm"), 1)
                link(dve.tensor_copy(thr[:, :], bank[3][:, 0:1]))
                link(dve.tensor_scalar(unpicked[:, :], w_col[:, :], thr[:, 0:1], None, ALU.is_le))
                dve.wait_ge(sem("slot_mm"), 2)
                dve.tensor_copy(slot_of[:, :], bank[4][:, 0:T]).then_inc(sem("slot_of"), 1)
                dve.wait_ge(sem("slot_of"), 1)
                dve.wait_ge(sem("sel"), 2)
                for t in range(T):
                    dve.tensor_scalar(pick[:, t, :], const("slot"), slot_of[:, t:t + 1], sel[:, t:t + 1], ALU.is_equal, ALU.mult).then_inc(sem("pick"), 1)
                dve.wait_ge(sem("gather_mm"), 1)
                dve.tensor_copy(ws_idx[:, :], bank[5][:, D:D + 2]).then_inc(sem("idx"), 1)
                link(dve.tensor_copy(xs[:, :], bank[5][:, 0:D]))
                dve.wait_ge(sem("idx_tr"), 1)
                dve.tensor_scalar(idx_row[:, :], bank[7][:, 0:SLOTS], float(MS - 1), None, ALU.min).then_inc(sem("idx"), 1)
                dve.wait_ge(sem("idx"), 2)
                for c in range(MC):
                    dve.tensor_scalar(mask_pick[:, c, :], idx_row[:, :], const("row")[:, c:c + 1], None, ALU.is_equal).then_inc(sem("mask_pick"), 1)

                def rmsnorm(src, n):
                    link(dve.scalar_tensor_tensor(hn[:, :], src, 1.0 / D, src, ALU.mult, ALU.mult, accum_out=nvar[:, 0:1]))
                    link(dve.tensor_scalar(nvar[:, 0:1], nvar[:, 0:1], RMS_EPS, None, ALU.add))
                    rsqrt(rstd[:, 0:1], nvar[:, 0:1], nbits[:, 0:1], ntmp[:, 0:1])
                    dve.scalar_tensor_tensor(hn[:, :], src, rstd[:, 0:1], ln_rows[:, n, :], ALU.mult, ALU.mult).then_inc(sem("hn"), 1)

                rmsnorm(xs[:, :], 0)
                dve.wait_ge(sem("trig_sel"), 1)
                dve.wait_ge(sem("rot0_mm"), 1)
                dve.wait_ge(sem("qk_s"), 1)
                two = [P, 2, SLOTS]
                link(tt(rot_s[:, :, :], bank[7][:, 0:2 * SLOTS].rearrange("p (a s) -> p a s", a=2), trig_sel[:, 1, :].unsqueeze(1).to_broadcast(two), ALU.mult))
                link(tt(qk_s[:, :, :], qk_s[:, :, :], trig_sel[:, 0, :].unsqueeze(1).to_broadcast(two), ALU.mult))
                tt(qk_s[:, :, :], qk_s[:, :, :], rot_s[:, :, :], ALU.add).then_inc(sem("rot_s"), 1)
                dve.wait_ge(sem("rot_s"), 1)
                four = [P, 4, SLOTS]

                def heads4(n):
                    return slice(4 * n, 4 * n + 4)

                for n in range(4):
                    tt(k_diag[:, heads4(n), :], qk_s[:, 1, :].unsqueeze(1).to_broadcast(four), const("head")[:, heads4(n)].unsqueeze(2).to_broadcast(four), ALU.mult).then_inc(sem("k_diag"), 1)
                dve.wait_ge(sem("select_mm"), 3)
                link(dve.tensor_copy(mask_sel[:, :], bank[1][:, 0:SLOTS]))
                dve.memset(mask_sel[:, SLOTS - 1:SLOTS], BIG).then_inc(sem("mask_sel"), 1)
                dve.wait_ge(sem("mask_sel"), 1)

                for n in range(4):
                    dve.wait_ge(sem("sc_mm"), n + 1)
                    link(dve.scalar_tensor_tensor(sc[:, heads4(n), :], bank[n][:, :].rearrange("p (a s) -> p a s", a=4), SCALE, mask_sel[:, :].unsqueeze(1).to_broadcast(four), ALU.mult, ALU.add))
                    dve.tensor_reduce(sc_max[:, heads4(n)], sc[:, heads4(n), :], AX, ALU.max, negate=True).then_inc(sem("sc_max"), 1)
                dve.wait_ge(sem("sc_exp"), 4)
                link(dve.reciprocal(sc_sum[:, :], sc_sum[:, :]))
                dve.wait_ge(sem("o_s_mm"), 1)
                tt(o_s[:, :].rearrange("p (h d) -> p h d", h=H), bank[0][:, 0:D].rearrange("p (h d) -> p h d", h=H), sc_sum[:, :].unsqueeze(2).to_broadcast([P, H, HD]), ALU.mult).then_inc(sem("o_s"), 1)
                dve.wait_ge(sem("wo_mm"), 1)
                link(tt(x1[:, :], xs[:, :], bank[2][:, 0:D], ALU.add))
                dve.wait_ge(sem("hn_tr"), 1)
                rmsnorm(x1[:, :], 1)
                link(tt(h[:, :, :], h[:, :, :], unpicked[:, :].unsqueeze(2).to_broadcast([P, T, D]), ALU.mult))
                link(tt(h[:, :, :], h[:, :, :], mod[:, 0, 5, :].unsqueeze(1).to_broadcast([P, T, D]), ALU.mult))
                link(tt(x[:, :, :], x[:, :, :], h[:, :, :], ALU.add))
                dve.wait_ge(sem("w2_mm"), 1)
                link(tt(x1[:, :], x1[:, :], bank[5][:, 0:D], ALU.add))
                link(dve.tensor_scalar(x1[:, :], x1[:, :], ws_idx[:, 0:1], None, ALU.mult))
                tt(proc[:, :], x1[:, :], mod[:, 0, 5, :], ALU.mult).then_inc(sem("proc"), 1)
                for c in range(C):
                    xv = x[:, 4 * c:4 * c + 4, :]
                    dve.wait_ge(sem("scatter_mm"), c + 1)
                    tt(xv, xv, bank[c][:, :].rearrange("p (t d) -> p t d", t=4), ALU.add).then_inc(sem("res_b"), 1)
                    dve.wait_ge(sem("res_b"), c + 1)
                    layernorm("ln_c", c)
                parts1 = [(n, c) for n in range(2) for c in range(C)]

                def rope1(k):
                    n, c = parts1[k]
                    cols = slice(c * HALF, (c + 1) * HALF)
                    dve.wait_ge(sem("rot1_mm"), k + 1)
                    tt(rot_f[:, cols], bank[4 + k][:, :], const("sin1")[:, cols], ALU.mult).then_inc(sem("rot1_done"), 1)
                    dve.wait_ge(sem("qk1"), k + 1)
                    link(tt(qk_f[:, n, cols], qk_f[:, n, cols], const("cos1")[:, cols], ALU.mult))
                    dve.wait_ge(sem("rot1_done"), k + 1)
                    tt(qk_f[:, n, cols], qk_f[:, n, cols], rot_f[:, cols], ALU.add).then_inc(sem("rope1"), 1)
                    dve.wait_ge(sem("rope1"), k + 1)

                def rest1(k, part):
                    n, c = parts1[k]
                    cols = slice(c * HALF, (c + 1) * HALF)
                    a = "qk"[n]
                    dve.wait_ge(sem("split_" + part), k + 1)
                    if part == "h":
                        tt(qk_f[:, n, cols], qk_f[:, n, cols], split[a]["h"][:, cols], ALU.subtract).then_inc(sem("rest1"), 1)
                        dve.wait_ge(sem("rest1"), k + 1)
                    else:
                        tt(split[a]["l"][:, cols], qk_f[:, n, cols], split[a]["m"][:, cols], ALU.subtract).then_inc(sem("split_l"), 1)

                for k in range(len(parts1) + 2):
                    if k < 4:
                        rope1(k)
                    if 1 <= k < 5:
                        rest1(k - 1, "h")
                    if k >= 2:
                        rest1(k - 2, "m")
                def values1(c):
                    dve.wait_ge(sem("k_clear"), 5)
                    dve.wait_ge(sem("v1_mm"), c + 1)
                    tt(v1[:, 4 * c:4 * c + 4, :, 0:HD], bank[4 + 2 * c][:, :].rearrange("p (t h d) -> p t h d", t=4, h=H),
                       vo_bias[:, 0, :].rearrange("p (h d) -> p h d", h=H).unsqueeze(1).to_broadcast([P, 4, H, HD]), ALU.add).then_inc(sem("v1"), 1)

                def row_max1(m):
                    u, t, hh, c = max_item1(m)
                    dve.wait_ge(sem("s1_mm"), m + 1)
                    dve.reduce_max(pmax1[:, hh % GH, t, c:c + 1], bank[MAX1_BANK[m % 3]][:, :], AX).then_inc(sem("row_max1"), 1)
                    if m % UI == UI - 1:
                        final_max1(u)

                def final_max1(u):
                    half = slice(4 * (u % C), 4 * (u % C) + 4)
                    dve.wait_ge(sem("row_max1"), UI * (u + 1))
                    link(dve.tensor_reduce(nmax1[:, :, half], pmax1[:, :, half, :], AX, ALU.max, negate=True))
                    if u >= 2:
                        dve.wait_ge(sem("mrow1_mm"), GH * (u - 1))
                    link(dve.tensor_copy(nmax_hl[:, :, half, 0], nmax1[:, :, half]))
                    tt(nmax_hl[:, :, half, 1], nmax1[:, :, half], nmax_hl[:, :, half, 0], ALU.subtract).then_inc(sem("nmax_hl"), 1)

                def o1_raw(u):
                    dve.wait_ge(sem("pv1"), UI // GH * (u + 1))
                    if u >= 2:
                        dve.wait_ge(sem("ctx_raw"), u - 1)
                    dve.tensor_copy(o_raw[u % C][:, :], bank[4][:, :]).then_inc(sem("o1_raw"), 1)

                def ctx_out(u):
                    g, c = divmod(u, C)
                    dve.wait_ge(sem("ctx_raw"), u + 1)
                    bv = bank[6][:, :].rearrange("p (t a e) -> p t a e", t=4, a=GH)
                    link(dve.reciprocal(den1[:, :, :], bv[:, :, :, HD]))
                    tt(ctx1[:, 4 * c:4 * c + 4, GH * HD * g:GH * HD * (g + 1)].rearrange("p t (a d) -> p t a d", a=GH), bv[:, :, :, 0:HD],
                       den1[:, :, :].unsqueeze(3).to_broadcast([P, 4, GH, HD]), ALU.mult).then_inc(sem("ctx1"), 1)

                for m in range(LEAD):
                    row_max1(m)
                    if m in (16, 20):
                        values1((m - 16) // 4)
                for n in range(NI1):
                    if n + LEAD < NI1:
                        row_max1(n + LEAD)
                    if n - 1 in CTX_AT:
                        ctx_out(CTX_AT[n - 1])
                    if n + 3 in CTX_AT:
                        o1_raw(CTX_AT[n + 3])
                o1_raw(UNITS - 1)
                ctx_out(UNITS - 1)
                for c in range(C):
                    dve.wait_ge(sem("attn1_mm"), c + 1)
                    residual(c, bank[2 + c], 1, 2, "res_c", bias=vo_bias[:, 1, :])
                    dve.wait_ge(sem("res_c"), c + 1)
                    layernorm("ln_d", c)
                te = [P, T, E]

                def over_e(a):
                    return a.unsqueeze(2).to_broadcast(te)

                expert = const("expert").unsqueeze(1).to_broadcast(te)
                dve.wait_ge(sem("lg_mm"), 1)
                link(dve.tensor_copy(lg[:, :, :], bank[0][:, 0:T * E].rearrange("p (t e) -> p t e", t=T)))
                link(dve.reduce_max(m1[:, :], lg[:, :, :], AX))
                tt(lg[:, :, :], lg[:, :, :], over_e(m1[:, :]), ALU.subtract).then_inc(sem("lg_sub"), 1)
                dve.wait_ge(sem("lg_exp"), 1)
                link(dve.reduce_sum(m2[:, :], lg[:, :, :], AX))
                link(dve.reciprocal(m2[:, :], m2[:, :]))
                link(tt(lg[:, :, :], lg[:, :, :], over_e(m2[:, :]), ALU.mult))

                def best(p_, top, oh):
                    link(dve.reduce_max(top, p_, AX))
                    link(tt(oh, p_, over_e(top), ALU.is_equal))
                    link(tt(oh, oh, expert, ALU.mult))
                    link(dve.tensor_reduce(e1[:, :], oh, AX, ALU.min))
                    link(tt(oh, expert, over_e(e1[:, :]), ALU.is_equal))

                best(lg[:, :, :], m1[:, :], oh1[:, :, :])
                link(dve.scalar_tensor_tensor(lg2[:, :, :], oh1[:, :, :], -4.0, lg[:, :, :], ALU.mult, ALU.add))
                best(lg2[:, :, :], m2[:, :], oh2[:, :, :])
                link(tt(e1[:, :], m1[:, :], m2[:, :], ALU.add))
                link(dve.tensor_scalar(e1[:, :], e1[:, :], 1e-6, None, ALU.add))
                link(dve.reciprocal(e1[:, :], e1[:, :]))
                link(tt(nvar[:, :], m1[:, :], m1[:, :], ALU.mult))
                link(tt(ntmp[:, :], m2[:, :], m2[:, :], ALU.mult))
                link(tt(nvar[:, :], nvar[:, :], ntmp[:, :], ALU.add))
                tt(bias_tok[:, :], nvar[:, :], e1[:, :], ALU.mult).then_inc(sem("coef"), 1)
                link(tt(m1[:, :], m1[:, :], e1[:, :], ALU.mult))
                link(tt(m2[:, :], m2[:, :], e1[:, :], ALU.mult))
                link(tt(oh1[:, :, :], oh1[:, :, :], over_e(m1[:, :]), ALU.mult))
                link(tt(oh2[:, :, :], oh2[:, :, :], over_e(m2[:, :]), ALU.mult))
                tt(coef[:, :, :], oh1[:, :, :], oh2[:, :, :], ALU.add).then_inc(sem("coef"), 1)
                for r in range(T // 2):
                    pair = slice(2 * r, 2 * r + 2)
                    for t in (2 * r, 2 * r + 1):
                        dve.wait_ge(sem("prod"), E * (t + 1))
                        dve.tensor_reduce(moe[:, t, :], prod[:, t % 4, :, :].rearrange("p e d -> p d e"), AX, ALU.add).then_inc(sem("moe"), 1)
                    dve.wait_ge(sem("moe"), 2 * r + 2)
                    link(tt(moe[:, pair, :], moe[:, pair, :], mod[:, 1, 5, :].unsqueeze(1).to_broadcast([P, 2, D]), ALU.mult))
                    tt(x[:, pair, :], x[:, pair, :], moe[:, pair, :], ALU.add).then_inc(sem("x_final"), 1)
                end_of_batch(dve, 4)


def gates_view(a):
    return a.rearrange("p l a d -> p (l a) d")


_INS = ["L0_attn_x", "L0_attn_w_qkv", "L0_attn_w_out", "L0_ffn_attention_mask", "L0_ffn_position_ids", "L0_ffn_router_w", "L0_ffn_router_b",
        "L0_ffn_wq", "L0_ffn_wk", "L0_ffn_wv", "L0_ffn_wo", "L0_ffn_w1", "L0_ffn_w2", "L0_ffn_ln1", "L0_ffn_ln2", "L0_c", "L0_wmod",
        "L1_attn_Wq", "L1_attn_bq", "L1_attn_Wk", "L1_attn_bk", "L1_attn_Wv", "L1_attn_bv", "L1_attn_Wo", "L1_attn_bo",
        "L1_ffn_router_w", "L1_ffn_expert_weights", "L1_c", "L1_wmod"]


def kernel(**inputs):
    import numpy as _np
    import concourse.bacc as _bacc
    from concourse import mybir as _mybir
    from concourse.bass_utils import run_bass_kernel_spmd as _run

    nc = _bacc.Bacc("TRN2", target_bir_lowering=False, num_devices=1)
    arrays, aps = {}, {}
    for name in _INS:
        a = _np.ascontiguousarray(inputs[name])
        arrays[f"in_{name}"] = a
        aps[name] = nc.dram_tensor(f"in_{name}", a.shape, _mybir.dt.from_np(a.dtype), kind="ExternalInput").ap()
    out = nc.dram_tensor("out_0", (B, S, D), F32, kind="ExternalOutput").ap()
    adaln_kernel(nc, aps, out)
    r = _run(nc, [arrays], core_ids=[0])
    return r.results[0]["out_0"]
```
